# Optimizing a Trainium2 kernel written in Bass

```python
import numpy as np
import jax
import jax.numpy as jnp

def _softmax(x, axis=-1):
    return jax.nn.softmax(x, axis=axis)

def _gelu(x):
    return jax.nn.gelu(x, approximate=True)

def _silu(x):
    return jax.nn.silu(x)

def _sigmoid(x):
    return jax.nn.sigmoid(x)

def _layernorm(x, axis=-1, eps=1e-05):
    m = jnp.mean(x, axis=axis, keepdims=True)
    v = jnp.var(x, axis=axis, keepdims=True)
    return (x - m) / jnp.sqrt(v + eps)

def _scatter_add(tgt, idx, src, axis=0):
    return tgt.at[idx].add(src)

def _segment_sum(src, seg, n):
    return jax.ops.segment_sum(src, seg, n)
kernel_name = 'mk_decoder_postln_d1_seqx_r4_5f9bae'

def setup_inputs(seed: int=0):
    np.random.seed(seed)
    _w = jnp.asarray

    def _rec_inputs():
        import jax
        import jax.numpy as jnp
        _rk = jax.random.key(seed)
        x = -0.0003929 + 0.9999 * jax.random.normal(jax.random.fold_in(_rk, 1), (64, 128, 256), jnp.float32)
        _lenS = 128 - jax.random.randint(jax.random.fold_in(_rk, 7), (64,), 0, max(1, 128 // 4) + 1, jnp.int32)
        _lenS2 = 128 - jax.random.randint(jax.random.fold_in(_rk, 8), (64,), 0, max(1, 128 // 4) + 1, jnp.int32)
        _ctx_512P = jax.random.normal(jax.random.fold_in(_rk, 11), (64, 16, 128), jnp.float32)
        _ctx_512c = jax.random.dirichlet(jax.random.fold_in(_rk, 511), 0.3 * jnp.ones((16,), jnp.float32), (64, 128))
        _ctx_512t = jnp.einsum('bsk,bkd->bsd', _ctx_512c, _ctx_512P)
        _ctx_512t = _ctx_512t * jax.lax.rsqrt(jnp.mean(jnp.square(_ctx_512t)) + 1e-12) * 0.953939
        ctx_512 = -1.39393e-06 + 0.999914 * (_ctx_512t + 0.3 * jax.random.normal(jax.random.fold_in(_rk, 611), (64, 128, 128), jnp.float32))
        return (x, ctx_512)
    x, ctx_512 = _rec_inputs()

    def _L0_attn_setup():
        import jax, jax.numpy as jnp
        import numpy as np
        EMBED_DIM = 256
        NUM_HEADS = 16
        HEAD_DIM = EMBED_DIM // NUM_HEADS
        key = jax.random.key(seed)
        k_x, k_wqkv, k_bqkv, k_wo, k_bo = jax.random.split(key, 5)
        bound_qkv = 1.0 / np.sqrt(EMBED_DIM)
        return {'x': jax.random.normal(k_x, (4, 512, EMBED_DIM), dtype=jnp.float32), 'W_qkv': jax.random.uniform(k_wqkv, (EMBED_DIM, 3 * EMBED_DIM), jnp.float32, -bound_qkv, bound_qkv), 'b_qkv': jax.random.uniform(k_bqkv, (3 * EMBED_DIM,), jnp.float32, -bound_qkv, bound_qkv), 'W_out': jax.random.uniform(k_wo, (EMBED_DIM, EMBED_DIM), jnp.float32, -bound_qkv, bound_qkv), 'b_out': jax.random.uniform(k_bo, (EMBED_DIM,), jnp.float32, -bound_qkv, bound_qkv)}
    _L0_attn_all = _L0_attn_setup()
    _L0_attn_in = {k: v for k, v in _L0_attn_all.items() if k in ('W_qkv', 'b_qkv', 'W_out', 'b_out')}
    del _L0_attn_all

    def _L0_xattn_setup():
        import jax, jax.numpy as jnp
        import numpy as np
        HEADS = 16
        D_MODEL = 256
        IMG_MODEL = 128
        D_K = D_MODEL // HEADS
        key = jax.random.key(seed)
        ks = jax.random.split(key, 12)
        B, LQ, LKV = (8, 512, 256)
        s_dm = 1.0 / np.sqrt(D_MODEL)
        s_im = 1.0 / np.sqrt(IMG_MODEL)
        return {'q': jax.random.normal(ks[0], (B, LQ, D_MODEL), jnp.float32), 'k': jax.random.normal(ks[1], (B, LKV, IMG_MODEL), jnp.float32), 'v': jax.random.normal(ks[2], (B, LKV, IMG_MODEL), jnp.float32), 'Wq': jax.random.normal(ks[3], (D_MODEL, D_MODEL), jnp.float32) * s_dm, 'bq': jnp.zeros((D_MODEL,), jnp.float32), 'Wk': jax.random.normal(ks[4], (IMG_MODEL, D_MODEL), jnp.float32) * s_im, 'bk': jnp.zeros((D_MODEL,), jnp.float32), 'Wv': jax.random.normal(ks[5], (IMG_MODEL, D_MODEL), jnp.float32) * s_im, 'bv': jnp.zeros((D_MODEL,), jnp.float32), 'Wo': jax.random.normal(ks[6], (D_MODEL, D_MODEL), jnp.float32) * s_dm, 'bo': jnp.zeros((D_MODEL,), jnp.float32)}
    _L0_xattn_all = _L0_xattn_setup()
    _L0_xattn_in = {k: v for k, v in _L0_xattn_all.items() if k in ('Wq', 'bq', 'Wk', 'bk', 'Wv', 'bv', 'Wo', 'bo')}
    del _L0_xattn_all

    def _L0_ffn_setup():
        import jax, jax.numpy as jnp
        import numpy as np
        TOP_K = 8
        CAPACITY = 128

        def _silu(x):
            return x * jax.nn.sigmoid(x)
        key = jax.random.key(seed)
        ks = jax.random.split(key, 7)
        B, S, H, E, I, Is = (2, 256, 256, 64, 128, 512)
        s = 0.05
        return {'hidden_states': jax.random.normal(ks[0], (B, S, H), jnp.float32), 'gate_w': jax.random.normal(ks[1], (H, E), jnp.float32) * s, 'shared_gate_w': jax.random.normal(ks[2], (H, 1), jnp.float32) * s, 'shared_gate_up_w': jax.random.normal(ks[3], (H, 2 * Is), jnp.float32) * s, 'shared_down_w': jax.random.normal(ks[4], (Is, H), jnp.float32) * s, 'expert_gate_up_w': jax.random.normal(ks[5], (E, H, 2 * I), jnp.float32) * s, 'expert_down_w': jax.random.normal(ks[6], (E, I, H), jnp.float32) * s}
    _L0_ffn_all = _L0_ffn_setup()
    _L0_ffn_in = {k: v for k, v in _L0_ffn_all.items() if k in ('gate_w', 'shared_gate_w', 'shared_gate_up_w', 'shared_down_w', 'expert_gate_up_w', 'expert_down_w')}
    del _L0_ffn_all
    return {'x': x, 'ctx_512': ctx_512, 'L0_attn_W_qkv': _L0_attn_in['W_qkv'], 'L0_attn_b_qkv': _L0_attn_in['b_qkv'], 'L0_attn_W_out': _L0_attn_in['W_out'], 'L0_attn_b_out': _L0_attn_in['b_out'], 'L0_xattn_Wq': _L0_xattn_in['Wq'], 'L0_xattn_bq': _L0_xattn_in['bq'], 'L0_xattn_Wk': _L0_xattn_in['Wk'], 'L0_xattn_bk': _L0_xattn_in['bk'], 'L0_xattn_Wv': _L0_xattn_in['Wv'], 'L0_xattn_bv': _L0_xattn_in['bv'], 'L0_xattn_Wo': _L0_xattn_in['Wo'], 'L0_xattn_bo': _L0_xattn_in['bo'], 'L0_ffn_gate_w': _L0_ffn_in['gate_w'], 'L0_ffn_shared_gate_w': _L0_ffn_in['shared_gate_w'], 'L0_ffn_shared_gate_up_w': _L0_ffn_in['shared_gate_up_w'], 'L0_ffn_shared_down_w': _L0_ffn_in['shared_down_w'], 'L0_ffn_expert_gate_up_w': _L0_ffn_in['expert_gate_up_w'], 'L0_ffn_expert_down_w': _L0_ffn_in['expert_down_w']}

def reference(x, ctx_512, L0_attn_W_qkv, L0_attn_b_qkv, L0_attn_W_out, L0_attn_b_out, L0_xattn_Wq, L0_xattn_bq, L0_xattn_Wk, L0_xattn_bk, L0_xattn_Wv, L0_xattn_bv, L0_xattn_Wo, L0_xattn_bo, L0_ffn_gate_w, L0_ffn_shared_gate_w, L0_ffn_shared_gate_up_w, L0_ffn_shared_down_w, L0_ffn_expert_gate_up_w, L0_ffn_expert_down_w):
    import jax
    import jax.numpy as jnp

    def _L0_attn_ref(x, W_qkv, b_qkv, W_out, b_out):
        import jax, jax.numpy as jnp
        import numpy as np
        EMBED_DIM = 256
        NUM_HEADS = 16
        HEAD_DIM = EMBED_DIM // NUM_HEADS
        qkv = jnp.einsum('bse,ef->bsf', x, W_qkv) + b_qkv
        q, k, v = jnp.split(qkv, 3, axis=-1)
        scale = 1.0 / jnp.sqrt(jnp.float32(HEAD_DIM))
        scores = jnp.einsum('bqe,bke->bqk', q, k) * scale
        attn = jax.nn.softmax(scores, axis=-1)
        context = jnp.einsum('bqk,bke->bqe', attn, v)
        return jnp.einsum('bse,ef->bsf', context, W_out) + b_out

    def _L0_xattn_ref(q, k, v, Wq, bq, Wk, bk, Wv, bv, Wo, bo):
        import jax, jax.numpy as jnp
        import numpy as np
        HEADS = 16
        D_MODEL = 256
        IMG_MODEL = 128
        D_K = D_MODEL // HEADS
        B, LQ, _ = q.shape
        LKV = k.shape[1]
        qh = (q @ Wq + bq).reshape(B, LQ, HEADS, D_K).transpose(0, 2, 1, 3)
        kh = (k @ Wk + bk).reshape(B, LKV, HEADS, D_K).transpose(0, 2, 1, 3)
        vh = (v @ Wv + bv).reshape(B, LKV, HEADS, D_K).transpose(0, 2, 1, 3)
        scale = 1.0 / np.sqrt(D_K)
        scores = jnp.einsum('bhqd,bhkd->bhqk', qh, kh) * scale
        attn = jax.nn.softmax(scores, axis=-1)
        out = jnp.einsum('bhqk,bhkd->bhqd', attn, vh)
        concat = out.transpose(0, 2, 1, 3).reshape(B, LQ, D_MODEL)
        return concat @ Wo + bo

    def _L0_ffn_ref(hidden_states, gate_w, shared_gate_w, shared_gate_up_w, shared_down_w, expert_gate_up_w, expert_down_w):
        import jax, jax.numpy as jnp
        import numpy as np
        TOP_K = 8
        CAPACITY = 128

        def _silu(x):
            return x * jax.nn.sigmoid(x)
        B, S, H = hidden_states.shape
        x = hidden_states.reshape(-1, H)
        T = x.shape[0]
        E = gate_w.shape[1]
        Is = shared_gate_up_w.shape[1] // 2
        I = expert_gate_up_w.shape[2] // 2
        gu = x @ shared_gate_up_w
        shared = _silu(gu[:, :Is]) * gu[:, Is:] @ shared_down_w
        shared = shared * jax.nn.sigmoid(x @ shared_gate_w)
        logits = x @ gate_w
        probs = jax.nn.softmax(logits.astype(jnp.float32), axis=-1)
        w, idx = jax.lax.top_k(probs, TOP_K)
        w = (w / jnp.sum(w, axis=-1, keepdims=True)).astype(x.dtype)
        e_flat = idx.reshape(-1)
        w_flat = w.reshape(-1)
        A = e_flat.shape[0]
        tok = jnp.arange(A) // TOP_K
        onehot = jax.nn.one_hot(e_flat, E, dtype=jnp.int32)
        pos = jnp.take_along_axis(jnp.cumsum(onehot, axis=0) - 1, e_flat[:, None], axis=1)[:, 0]
        slot = jnp.minimum(pos, CAPACITY)
        buf = jnp.zeros((E, CAPACITY + 1, H), x.dtype).at[e_flat, slot].set(x[tok])
        gu_e = jnp.einsum('ech,ehf->ecf', buf, expert_gate_up_w)
        act = _silu(gu_e[..., :I]) * gu_e[..., I:]
        out_e = jnp.einsum('eci,eih->ech', act, expert_down_w)
        y = out_e[e_flat, slot] * w_flat[:, None]
        y = jnp.where((pos < CAPACITY)[:, None], y, jnp.zeros_like(y))
        y = y.reshape(T, TOP_K, H).sum(axis=1)
        return (y + shared).reshape(B, S, H)
    x = _layernorm(x + _L0_attn_ref(x, L0_attn_W_qkv, L0_attn_b_qkv, L0_attn_W_out, L0_attn_b_out), axis=-1)
    x = _layernorm(x + _L0_xattn_ref(x, ctx_512, ctx_512, L0_xattn_Wq, L0_xattn_bq, L0_xattn_Wk, L0_xattn_bk, L0_xattn_Wv, L0_xattn_bv, L0_xattn_Wo, L0_xattn_bo), axis=-1)
    x = _layernorm(x + _L0_ffn_ref(x, L0_ffn_gate_w, L0_ffn_shared_gate_w, L0_ffn_shared_gate_up_w, L0_ffn_shared_down_w, L0_ffn_expert_gate_up_w, L0_ffn_expert_down_w), axis=-1)
    return x

_drawn_inputs = setup_inputs


def setup_inputs(seed=0):
    import zlib

    import numpy as np

    out = dict(_drawn_inputs(seed))
    spreads = {'L0_xattn_bq': (0.0, 0.35),
     'L0_xattn_bk': (0.0, 0.8),
     'L0_xattn_bv': (0.0, 0.1),
     'L0_xattn_bo': (0.0, 0.1)}
    factors = {}
    for name, (base, spread) in spreads.items():
        noise = np.random.default_rng([zlib.crc32(name.encode()), seed]).standard_normal(out[name].shape)
        drawn = base * np.exp(spread * noise) if base else spread * noise
        out[name] = jnp.asarray(drawn.astype(out[name].dtype))
    for name, factor in factors.items():
        out[name] = (out[name] * factor).astype(out[name].dtype)
    return out
```

```python
from contextlib import ExitStack

import concourse.bass as bass
from concourse import mybir

F32 = mybir.dt.float32
BF16 = mybir.dt.bfloat16
I32 = mybir.dt.int32
U32 = mybir.dt.uint32
ALU = mybir.AluOpType
ACT = mybir.ActivationFunctionType
AX = mybir.AxisListType

P = 128
EPS = 1e-5
TOP_K = 8
CAPACITY = 128
HEADS = 16
A, B, Q, C = 0, 1, 2, 3
PEEL = 6
QUARTERS = 8

SHARED_JOBS = [("xT", A), ("ctxT", B), ("q", A), ("x2T", C), ("x1T", B), ("k", A), ("logits", C),
               ("gu0", C), ("v", A), ("qx", B), ("gu1", C), ("kx", B), ("s", A), ("vx", B),
               ("gu2", C), ("gu3", C), ("pT", A), ("oT", Q), ("dn", C), ("y", A), ("pos", C)]
N_SHARED = 3
assert len(SHARED_JOBS) % N_SHARED == 0


def decoder_layer(nc, x, ctx_in, W_qkv, b_qkv, W_out, b_out, Wq, bq, Wk, bk, Wv, bv, Wo, bo,
                  gate_w, shared_gate_w, shared_gate_up_w, shared_down_w,
                  expert_gate_up_w, expert_down_w, out):
    NSEQ, S, D = x.shape
    DC = ctx_in.shape[2]
    T = NSEQ * S
    PAIRS = NSEQ // 2
    E = gate_w.shape[1]
    FS = shared_down_w.shape[0]
    FB = FS // P
    DH = D // HEADS
    KB = D // P
    SCALE = 1.0 / DH ** 0.5
    XROW = D + E
    assert S == P and D == 2 * P and DC == P and FB == 4 and E == 64 and PAIRS > PEEL
    assert expert_down_w.shape[1] == P

    x_pairs = x.rearrange("(n u) p d -> n p u d", u=2)
    ctx_pairs = ctx_in.rearrange("(n u) p d -> n p u d", u=2)

    token_table = nc.dram_tensor("token_table", [T + CAPACITY, XROW], F32, kind="Internal")
    resid_table = nc.dram_tensor("resid_table", [T + CAPACITY, D], F32, kind="Internal")
    slot_table = nc.dram_tensor("slot_table", [E * CAPACITY, 1], I32, kind="Internal")
    token_pairs = token_table[0:T, :].rearrange("(n u p) f -> n p u f", u=2, p=P)
    resid_pairs = resid_table[0:T, :].rearrange("(n u p) f -> n p u f", u=2, p=P)
    slots_by_expert = slot_table[:, :].rearrange("(e c) o -> e (c o)", c=CAPACITY)

    es = ExitStack()
    with es:
        def sb(name, shape, dt=F32):
            return es.enter_context(nc.sbuf_tensor(name, shape, dt))

        def psum(name):
            return es.enter_context(nc.psum_tensor(name, [P, 512], F32))

        def sem(name):
            return es.enter_context(nc.semaphore(name))

        RING = 4
        ident = sb("ident", [P, P])
        before = sb("before", [P, P], BF16)
        ones_bf = sb("ones_bf", [P, P], BF16)
        par_mask = sb("par_mask", [P, 2])
        eps_col = sb("eps_col", [P, 4])
        pair_step = sb("pair_step", [P, 1], I32)
        neg_half = sb("neg_half", [P, 2])
        slot_base = sb("slot_base", [P, E])
        token_no = [sb(f"token_no{u}", [P, 1], I32) for u in range(2)]
        base_i = sb("base_i", [P, E], I32)
        row_no = sb("row_no", [P, 1], I32)
        row_f = sb("row_f", [P, 1])
        row_ge = sb("row_ge", [P, 1])
        spare_slots = sb("spare_slots", [E, CAPACITY], I32)
        zero_rows = sb("zero_rows", [P, XROW])
        w_qk = sb("w_qk", [P, KB, 2 * D])
        w_v = sb("w_v", [P, KB, D])
        w_vT = sb("w_vT", [P, KB, D])
        w_out = sb("w_out", [P, KB, D])
        w_vo = sb("w_vo", [P, KB, D])
        w_q = sb("w_q", [P, KB, D])
        w_k = sb("w_k", [P, D])
        w_vx = sb("w_vx", [P, D])
        w_o = sb("w_o", [P, KB, D])
        w_gate = sb("w_gate", [P, KB, E + 1])
        w_gu = sb("w_gu", [P, KB, 2 * FS])
        w_dn = sb("w_dn", [P, FB, D])
        b_qk = sb("b_qk", [P, 4])
        b_v = sb("b_v", [P, KB])
        b_q = sb("b_q", [P, KB])
        b_qm = sb("b_qm", [P, 2, KB])
        b_k = sb("b_k", [P, KB])
        b_vx = sb("b_vx", [P, KB])
        bv_rows = sb("bv_rows", [P, 2, KB, P])
        bias_a = sb("bias_a", [P, D])
        bias_x = sb("bias_x", [P, D])
        bout_rows = sb("bout_rows", [P, 2, D])
        x_in = [sb(f"x_in{i}", [P, 2, D]) for i in range(2)]
        ctx_sb = [sb(f"ctx_sb{i}", [P, 2, DC]) for i in range(2)]
        xT = sb("xT", [P, KB, 256])
        q_sb = sb("q_sb", [P, KB, 256])
        k_sb = sb("k_sb", [P, KB, 256])
        v_sb = sb("v_sb", [P, 2, D])
        xb = sb("xb", [P, 2, D])
        s_nmax = sb("s_nmax", [P, 2])
        s_nmax_sc = sb("s_nmax_sc", [P, 2])
        s_sum = sb("s_sum", [P, 2])
        s_rsum = sb("s_rsum", [P, 2])
        p_sb = sb("p_sb", [P, 2, P])
        pT_sb = sb("pT_sb", [P, 2, P])
        r1 = sb("r1", [P, 2, D])
        st1 = sb("st1", [P, 2, 6])
        mv1 = sb("mv1", [P, 2, 2])
        ve1 = sb("ve1", [P, 2])
        rstd1 = sb("rstd1", [P, 2])
        x1 = sb("x1", [P, 2, D])
        x1b = [sb(f"x1b{i}", [P, 2, D]) for i in range(2)]
        x1T = sb("x1T", [P, KB, 256])
        ctxT = sb("ctxT", [P, 256])
        qx = [sb(f"qx{i}", [P, KB, 2, 256]) for i in range(2)]
        kx = [sb(f"kx{i}", [P, KB, 256]) for i in range(2)]
        vx = [sb(f"vx{i}", [P, 2, HEADS, DH + 1]) for i in range(2)]
        h_max = [sb(f"h_max{i}", [P, 4]) for i in range(2)]
        probs = [sb(f"probs{i}", [P, 4, P]) for i in range(4)]
        probsT = [sb(f"probsT{i}", [P, 4, P]) for i in range(4)]
        o_rsum = sb("o_rsum", [P, HEADS])
        o_sb = sb("o_sb", [P, 2, D])
        oT_sb = sb("oT_sb", [P, KB, 256])
        r2 = sb("r2", [P, 2, D])
        st2 = sb("st2", [P, 2, 6])
        mv2 = sb("mv2", [P, 2, 2])
        ve2 = sb("ve2", [P, 2])
        rstd2 = sb("rstd2", [P, 2])
        x2 = [sb(f"x2_{i}", [P, 2, XROW]) for i in range(2)]
        x2T = sb("x2T", [P, KB, 256])
        lg_max = sb("lg_max", [P, 2])
        lg = sb("lg", [P, 2, E + 1])
        ex = sb("ex", [P, 2, E + 1])
        z_sum = sb("z_sum", [P, 2])
        z_rsum = sb("z_rsum", [P, 2])
        sg1 = sb("sg1", [P, 2])
        sg = sb("sg", [P, 2])
        prob = sb("prob", [P, 2, E])
        top = sb("top", [P, 2, TOP_K])
        marked = sb("marked", [P, 2, E])
        chosen = sb("chosen", [P, 2, E])
        chosen_bf = sb("chosen_bf", [P, 2, E], BF16)
        top_sum = sb("top_sum", [P, 2])
        top_rsum = sb("top_rsum", [P, 2])
        count = sb("count", [P, E])
        place = sb("place", [P, 2, E])
        kept = sb("kept", [P, 2, E])
        slot_key = sb("slot_key", [P, 2, E])
        key = sb("key", [P, 2, E])
        key8 = sb("key8", [P, 2, TOP_K])
        slot_no = [sb(f"slot_no{i}", [P, 2, TOP_K], U32) for i in range(2)]
        eg = [sb(f"eg{i}", [P, 256]) for i in range(2)]
        eg_p1 = sb("eg_p1", [P, 256])
        sig = sb("sig", [P, 256])
        silu = sb("silu", [P, 256])
        h_sb = sb("h_sb", [P, FB, 256])
        z_sb = [sb(f"z_sb{i}", [P, 2, D]) for i in range(2)]
        slot_i = sb("slot_i", [E, CAPACITY], I32)
        slot_f = sb("slot_f", [E, CAPACITY])
        slot_ids = sb("slot_ids", [P, E], U32)
        ids = [sb(f"ids{i}", [P, 1], U32) for i in range(2 * RING)]
        xg = [sb(f"xg{i}", [P, XROW]) for i in range(2 * RING)]
        we_gu = [sb(f"we_gu{i}", [P, KB, 2 * P]) for i in range(2 * RING)]
        we_dn = [sb(f"we_dn{i}", [P, D]) for i in range(2 * RING)]
        xgT = [sb(f"xgT{i}", [P, KB, P]) for i in range(2)]
        ee = [sb(f"ee{i}", [P, P]) for i in range(2)]
        ee_p1 = sb("ee_p1", [P, P])
        esig = sb("esig", [P, P])
        esilu = sb("esilu", [P, P])
        eh = [sb(f"eh{i}", [P, P]) for i in range(2)]
        ey = [sb(f"ey{i}", [P, D]) for i in range(2 * RING)]
        FT = 4
        f_in = [sb(f"f_in{i}", [P, FT, D]) for i in range(2)]
        f_out = [sb(f"f_out{i}", [P, FT, D]) for i in range(2)]
        f_st = sb("f_st", [P, FT, 6])
        f_mv = sb("f_mv", [P, FT, 2])
        f_ve = sb("f_ve", [P, FT])
        f_rstd = sb("f_rstd", [P, FT])
        f_nh = sb("f_nh", [P, FT])

        score_ps = [psum(f"score_ps{i}") for i in range(2)]
        probT_ps = [psum(f"probT_ps{i}") for i in range(2)]
        o_ps = psum("o_ps")
        shared_ps = [psum(f"shared_ps{i}") for i in range(N_SHARED)]
        bank_of = {job: shared_ps[i % N_SHARED] for i, (job, _) in enumerate(SHARED_JOBS)}

        done = {job: sem(f"{job}_done") for job, _ in SHARED_JOBS}
        drained = {job: sem(f"{job}_out") for job, _ in SHARED_JOBS}
        score_done = sem("score_done")
        max_done = sem("max_done")
        score_out = sem("score_out")
        exp_done = sem("exp_done")
        probT_done = sem("probT_done")
        probT_out = sem("probT_out")
        o_done = sem("o_done")
        o_recip = [sem(f"o_recip{u}") for u in range(2)]
        o_out = [sem(f"o_out{u}") for u in range(2)]
        yx_done, yx_out = sem("yx_done"), sem("yx_out")
        consts = sem("consts")
        carried = [sem("carried_pool"), sem("carried_vector")]
        pool_step = sem("pool_step")
        loaded_w = sem("loaded_w")
        tables_set = sem("tables_set")
        pre = sem("pre")
        pre_pe = sem("pre_pe")
        x_loaded = [sem(f"x_loaded{i}") for i in range(2)]
        ctx_loaded = [sem(f"ctx_loaded{i}") for i in range(2)]
        xb_done, x1b_done = sem("xb_done"), sem("x1b_done")
        s_max_done, s_max_sc = sem("s_max_done"), sem("s_max_sc")
        ve1_done, rstd1_done, ve2_done, rstd2_done = (sem(n) for n in ("ve1_done", "rstd1_done", "ve2_done", "rstd2_done"))
        s_rsum_done, st1_done, mv1_done, x1_done = (sem(n) for n in ("s_rsum_done", "st1_done", "mv1_done", "x1_done"))
        st2_done, mv2_done, x2_done = (sem(n) for n in ("st2_done", "mv2_done", "x2_done"))
        ex_done = sem("ex_done")
        gate_step = sem("gate_step")
        chosen_done, weight_done, sg_done = (sem(n) for n in ("chosen_done", "weight_done", "sg_done"))
        place_step, slot_done = sem("place_step"), sem("slot_done")
        eg_done = [sem(f"eg_done{j}") for j in range(FB)]
        silu_step = sem("silu_step")
        token_stored = [sem(f"token_stored{i}") for i in range(2)]
        resid_stored = [sem(f"resid_stored{i}") for i in range(2)]
        scattered = [sem(f"scattered{i}") for i in range(2)]
        token_no_done = sem("token_no_done")
        slots_loaded, slots_f, slots_T, slots_u = (sem(n) for n in ("slots_loaded", "slots_f", "slots_T", "slots_u"))
        id_done = sem("id_done")
        we_loaded = [sem(f"we_loaded{i}") for i in range(2 * RING)]
        gathered = [sem(f"gathered{i}") for i in range(2 * RING)]
        xgT_done, xgT_out = sem("xgT_done"), sem("xgT_out")
        egu_done, ee_done, estep, eh_done = sem("egu_done"), sem("ee_done"), sem("estep"), sem("eh_done")
        edn_done, ey_done = sem("edn_done"), sem("ey_done")
        added = sem("added")
        f_loaded = [sem(f"f_loaded{i}") for i in range(2)]
        f_step, f_ve_done, f_rstd_done, f_norm = sem("f_step"), sem("f_ve_done"), sem("f_rstd_done"), sem("f_norm")
        f_stored = [sem(f"f_stored{i}") for i in range(2)]

        def wait(eng, s, n):
            if not isinstance(n, int) or n > 0:
                eng.wait_ge(s, n)

        def carry_wait(eng):
            eng.sem_inc(carried[eng is nc.vector], 1)

        def ticks(eng, tick, lags, peel, unroll, total):
            for t in range(peel):
                tick(t, t)
            with eng.Fori(peel // unroll, total // unroll) as r:
                for u in range(unroll):
                    tick(r * unroll + u, u)
            for t in range(total, total + lags):
                tick(t, t)

        def on(t, lag, total=PAIRS):
            return not isinstance(t, int) or 0 <= t - lag < total

        def bank_free(pe, job, t):
            names = [n for n, _ in SHARED_JOBS]
            i, back = names.index(job), 0
            while True:
                i -= N_SHARED
                if i < 0:
                    i += len(names)
                    back += 1
                if isinstance(t, int) and t - back < 0:
                    return
                name, lag = SHARED_JOBS[i]
                if on(t - back, lag):
                    pe.wait_ge(drained[name], t - back - lag + 1)
                    return

        def half_count(n, i, inc=16):
            return n * (inc // 2) + (inc - i % 2 * (inc // 2))

        def lap(n, k, inc=16):
            return n * (inc // (2 * RING)) + (inc - k % (2 * RING) * (inc // (2 * RING)))

        def nth(n, q):
            return n * QUARTERS + (q + 1)

        def column(n):
            return bass.ds(n, 1)

        W_LOADS = 18

        block = es.enter_context(nc.Block())

        @block.sync
        def _(sp):
            for dst, src in ((x_in[0][:], x_pairs[0]),):
                sp.dma_start(dst, src).then_inc(x_loaded[0], 16)
            with nc.allow_non_contiguous_dma(reason="bias vectors, once"):
                sp.dma_start(w_v[:], W_qkv[:, 2 * D:3 * D].rearrange("(k p) n -> p k n", p=P)).then_inc(loaded_w, 16)
                sp.dma_start(w_out[:], W_out.rearrange("(k p) n -> p k n", p=P)).then_inc(loaded_w, 16)
                sp.dma_start(w_qk[:], W_qkv[:, 0:2 * D].rearrange("(k p) n -> p k n", p=P)).then_inc(loaded_w, 16)
                sp.dma_start(b_qk[:], b_qkv[0:2 * D].rearrange("(m p) -> p m", p=P)).then_inc(loaded_w, 16)
                sp.dma_start(b_v[:], b_qkv[2 * D:3 * D].rearrange("(m p) -> p m", p=P)).then_inc(loaded_w, 16)
                sp.dma_start(bout_rows[:, 0, :], b_out.rearrange("(o n) -> o n", o=1).to_broadcast([P, D])).then_inc(loaded_w, 16)
                sp.dma_start(bout_rows[:, 1, :], bo.rearrange("(o n) -> o n", o=1).to_broadcast([P, D])).then_inc(loaded_w, 16)
                sp.dma_start(w_q[:], Wq.rearrange("(k p) n -> p k n", p=P)).then_inc(loaded_w, 16)
                sp.dma_start(w_k[:], Wk[:, :]).then_inc(loaded_w, 16)
                sp.dma_start(w_vx[:], Wv[:, :]).then_inc(loaded_w, 16)
                sp.dma_start(w_o[:], Wo.rearrange("(k p) n -> p k n", p=P)).then_inc(loaded_w, 16)
                sp.dma_start(b_q[:], bq.rearrange("(m p) -> p m", p=P)).then_inc(loaded_w, 16)
                sp.dma_start(b_k[:], bk.rearrange("(m p) -> p m", p=P)).then_inc(loaded_w, 16)
                sp.dma_start(b_vx[:], bv.rearrange("(m p) -> p m", p=P)).then_inc(loaded_w, 16)
                sp.dma_start(w_gate[:, :, 0:E], gate_w.rearrange("(k p) n -> p k n", p=P)).then_inc(loaded_w, 16)
                sp.dma_start(w_gate[:, :, E:E + 1], shared_gate_w.rearrange("(k p) n -> p k n", p=P)).then_inc(loaded_w, 16)
                sp.dma_start(w_gu[:], shared_gate_up_w.rearrange("(k p) n -> p k n", p=P)).then_inc(loaded_w, 16)
                sp.dma_start(w_dn[:], shared_down_w.rearrange("(k p) n -> p k n", p=P)).then_inc(loaded_w, 16)
            sp.wait_ge(consts, 1)
            sp.dma_start(slots_by_expert, spare_slots[:]).then_inc(tables_set, 16)
            sp.dma_start(token_table[T:T + CAPACITY, :], zero_rows[:]).then_inc(tables_set, 16)
            sp.dma_start(resid_table[T:T + CAPACITY, :], zero_rows[:, 0:D]).then_inc(tables_set, 16)

            def tick(t, i):
                if on(t + 1, A):
                    wait(sp, done["xT"], t)
                    wait(sp, xb_done, t)
                    sp.dma_start(x_in[(i + 1) % 2][:], x_pairs[t + 1]).then_inc(x_loaded[(i + 1) % 2], 16)
                if on(t, A):
                    wait(sp, done["ctxT"], t - 1)
                    sp.dma_start(ctx_sb[i % 2][:], ctx_pairs[t]).then_inc(ctx_loaded[i % 2], 16)
                if on(t, C):
                    c, ci = t - C, (i - C) % 2
                    sp.wait_ge(weight_done, c + 1)
                    sp.dma_start(token_pairs[c], x2[ci][:]).then_inc(token_stored[ci], 16)
                    sp.wait_ge(drained["dn"], c + 1)
                    sp.dma_start(resid_pairs[c], z_sb[ci][:]).then_inc(resid_stored[ci], 16)

            for t in range(PEEL):
                tick(t, t)
            with sp.Fori(PEEL // 2, PAIRS // 2 - 1) as r:
                for u in range(2):
                    tick(r * 2 + u, u)
            for t in range(PAIRS - 2, PAIRS + C):
                tick(t, t)

            def load_expert(n, i):
                wait(sp, edn_done, n - 2 * RING + 1)
                sp.dma_start(we_gu[i][:], expert_gate_up_w[n].rearrange("(k p) f -> p k f", p=P)).then_inc(we_loaded[i], 16)
                sp.dma_start(we_dn[i][:], expert_down_w[n]).then_inc(we_loaded[i], 16)

            for n in range(2 * RING):
                load_expert(n, n)
            with sp.Fori(1, E // (2 * RING)) as r:
                for u in range(2 * RING):
                    load_expert(r * (2 * RING) + u, u)

            sp.wait_ge(added, 16 * E)
            f_tiles = resid_table[0:T, :].rearrange("(n u p) f -> n p u f", u=FT, p=P)

            def load_resid(n, g, i):
                wait(sp, f_norm, n - 1)
                sp.dma_start(f_in[i][:], f_tiles[n]).then_inc(f_loaded[i], 16)
            for n in range(4):
                load_resid(n, n // 2, n % 2)
            with sp.Fori(2, T // (P * FT) // 2) as r:
                for u in range(2):
                    load_resid(r * 2 + u, r, u)

        @block.tensor
        def _(pe):
            def transpose_pair(bank, tile, cols=KB):
                for kb in range(cols):
                    for u in range(2):
                        m = pe.transpose(bank[:, kb * 256 + u * P:kb * 256 + (u + 1) * P],
                                         tile[:, u, kb * P:(kb + 1) * P], ident[:])
                return m

            def project_T(bank, w, col, rhs, blocks=KB):
                for mb in range(2):
                    for kb in range(blocks):
                        lhsT = w[:, kb, col + mb * P:col + (mb + 1) * P] if blocks > 1 else w[:, mb * P:(mb + 1) * P]
                        m = pe.matmul(bank[:, mb * 256:(mb + 1) * 256], lhsT,
                                      rhs[:, kb, :] if blocks > 1 else rhs[:, :],
                                      start=(kb == 0), stop=(kb == blocks - 1))
                return m

            def project(bank, lhs, w, blocks=KB):
                for u in range(2):
                    for kb in range(blocks):
                        lhsT = lhs[:, kb, u * P:(u + 1) * P] if blocks > 1 else lhs[:, u * P:(u + 1) * P]
                        m = pe.matmul(bank[:, u * 256:(u + 1) * 256], lhsT,
                                      w[:, kb, :] if blocks > 1 else w[:, :],
                                      start=(kb == 0), stop=(kb == blocks - 1))
                return m

            pe.wait_ge(consts, 1)
            pe.wait_ge(loaded_w, 16 * W_LOADS)
            for kb in range(KB):
                for mb in range(2):
                    m = pe.transpose(shared_ps[0][:, mb * 256 + kb * P:mb * 256 + (kb + 1) * P],
                                     w_v[:, kb, mb * P:(mb + 1) * P], ident[:])
            m.then_inc(pre_pe, 1)
            pe.wait_ge(pre, 3)
            for mb in range(2):
                for kb in range(KB):
                    m = pe.matmul(shared_ps[1][:, mb * 256:(mb + 1) * 256], w_vT[:, kb, mb * P:(mb + 1) * P],
                                  w_out[:, kb, :], start=(kb == 0), stop=(kb == KB - 1))
            for n, w in ((0, w_out), (1, w_o)):
                for kb in range(KB):
                    m = pe.matmul(shared_ps[2][:, n * 256:(n + 1) * 256], bv_rows[:, n, kb, :], w[:, kb, :],
                                  start=(kb == 0), stop=(kb == KB - 1))
            m.then_inc(pre_pe, 1)
            pe.wait_ge(pre, 6)

            def scores(t, i, q):
                b, bi = t - Q, (i - Q) % 2
                u, g = q // 4, q % 4
                if q == 0:
                    pe.wait_ge(drained["qx"], b + 1)
                    pe.wait_ge(drained["kx"], b + 1)
                if q >= 2:
                    pe.wait_ge(score_out, nth(b, q - 2))
                else:
                    wait(pe, score_out, nth(b - 1, q + QUARTERS - 2))
                rows = slice(32 * g, 32 * g + 32)
                for mb in range(2):
                    for par in range(2):
                        n = 2 * mb + par
                        m = pe.matmul(score_ps[q % 2][:, n * P:(n + 1) * P],
                                      qx[bi][rows, mb, par, u * P:(u + 1) * P],
                                      kx[bi][rows, mb, u * P:(u + 1) * P], start=True, stop=True)
                m.then_inc(score_done, 1)

            def turn_probs(t, i, q):
                b = t - Q
                pe.wait_ge(exp_done, nth(b, q))
                if q >= 2:
                    pe.wait_ge(probT_out, nth(b, q - 2))
                else:
                    wait(pe, probT_out, nth(b - 1, q + QUARTERS - 2))
                for n in range(4):
                    m = pe.transpose(probT_ps[q % 2][:, n * P:(n + 1) * P], probs[q % 4][:, n, :], ident[:])
                m.then_inc(probT_done, 1)

            def weigh_values(t, i, q):
                b, bi = t - Q, (i - Q) % 2
                u, g = q // 4, q % 4
                if q == 0:
                    pe.wait_ge(drained["vx"], b + 1)
                    wait(pe, yx_out, b)
                if q == 4:
                    pe.wait_ge(o_out[0], b + 1)
                pe.wait_ge(probT_out, nth(b, q))
                for mb in range(2):
                    for par in range(2):
                        h = 8 * mb + 2 * g + par
                        m = pe.matmul(o_ps[:, h * (DH + 1):(h + 1) * (DH + 1)],
                                      probsT[q % 4][:, 2 * mb + par, :], vx[bi][:, u, h, :],
                                      start=True, stop=True)
                m.then_inc(o_done, 1)

            def tick(t, i):
                a, b, c = t - A, t - B, t - C

                def job(name):
                    bank_free(pe, name, t)
                    return bank_of[name]

                def mlp(j):
                    bank = job(f"gu{j}")
                    for half in range(2):
                        for kb in range(KB):
                            m = pe.matmul(bank[:, half * 256:(half + 1) * 256],
                                          w_gu[:, kb, half * FS + j * P:half * FS + (j + 1) * P],
                                          x2T[:, kb, :], start=(kb == 0), stop=(kb == KB - 1))
                    m.then_inc(done[f"gu{j}"], 1)

                if on(t, Q):
                    scores(t, i, 0)
                if on(t, A):
                    bank = job("xT")
                    pe.wait_ge(x_loaded[i % 2], half_count(t, i))
                    transpose_pair(bank, x_in[i % 2]).then_inc(done["xT"], 1)
                if on(t, Q):
                    scores(t, i, 1)
                if on(t, B):
                    bank = job("ctxT")
                    pe.wait_ge(ctx_loaded[(i - B) % 2], half_count(b, i - B))
                    for u in range(2):
                        m = pe.transpose(bank[:, u * P:(u + 1) * P], ctx_sb[(i - B) % 2][:, u, :], ident[:])
                    m.then_inc(done["ctxT"], 1)
                if on(t, Q):
                    turn_probs(t, i, 0)
                    scores(t, i, 2)
                if on(t, A):
                    bank = job("q")
                    pe.wait_ge(drained["xT"], a + 1)
                    project_T(bank, w_qk, 0, xT).then_inc(done["q"], 1)
                if on(t, Q):
                    turn_probs(t, i, 1)
                    weigh_values(t, i, 0)
                    scores(t, i, 3)
                if on(t, C):
                    bank = job("x2T")
                    pe.wait_ge(x2_done, c + 1)
                    transpose_pair(bank, x2[(i - C) % 2]).then_inc(done["x2T"], 1)
                if on(t, Q):
                    turn_probs(t, i, 2)
                    weigh_values(t, i, 1)
                    scores(t, i, 4)
                if on(t, B):
                    bank = job("x1T")
                    pe.wait_ge(x1_done, b + 1)
                    transpose_pair(bank, x1).then_inc(done["x1T"], 1)
                if on(t, A):
                    bank = job("k")
                    project_T(bank, w_qk, D, xT).then_inc(done["k"], 1)
                if on(t, Q):
                    turn_probs(t, i, 3)
                    weigh_values(t, i, 2)
                    scores(t, i, 5)
                if on(t, C):
                    bank = job("logits")
                    pe.wait_ge(drained["x2T"], c + 1)
                    for u in range(2):
                        for kb in range(KB):
                            m = pe.matmul(bank[:, u * (E + 1):(u + 1) * (E + 1)], x2T[:, kb, u * P:(u + 1) * P],
                                          w_gate[:, kb, :], start=(kb == 0), stop=(kb == KB - 1))
                    m.then_inc(done["logits"], 1)
                    mlp(0)
                if on(t, A):
                    bank = job("v")
                    project(bank, xT, w_vo).then_inc(done["v"], 1)
                if on(t, Q):
                    turn_probs(t, i, 4)
                    weigh_values(t, i, 3)
                    scores(t, i, 6)
                if on(t, B):
                    bank = job("qx")
                    pe.wait_ge(drained["x1T"], b + 1)
                    project_T(bank, w_q, 0, x1T).then_inc(done["qx"], 1)
                if on(t, C):
                    mlp(1)
                if on(t, Q):
                    turn_probs(t, i, 5)
                    weigh_values(t, i, 4)
                    scores(t, i, 7)
                if on(t, B):
                    bank = job("kx")
                    pe.wait_ge(drained["ctxT"], b + 1)
                    project_T(bank, w_k, 0, ctxT, blocks=1).then_inc(done["kx"], 1)
                if on(t, A):
                    bank = job("s")
                    pe.wait_ge(drained["q"], a + 1)
                    pe.wait_ge(drained["k"], a + 1)
                    for u in range(2):
                        for mb in range(KB):
                            m = pe.matmul(bank[:, u * P:(u + 1) * P], q_sb[:, mb, u * P:(u + 1) * P],
                                          k_sb[:, mb, u * P:(u + 1) * P], start=(mb == 0), stop=(mb == KB - 1))
                    m.then_inc(done["s"], 1)
                if on(t, Q):
                    turn_probs(t, i, 6)
                    weigh_values(t, i, 5)
                if on(t, B):
                    bank = job("vx")
                    project(bank, ctxT, w_vx, blocks=1).then_inc(done["vx"], 1)
                if on(t, C):
                    mlp(2)
                if on(t, Q):
                    turn_probs(t, i, 7)
                    weigh_values(t, i, 6)
                if on(t, C):
                    mlp(3)
                if on(t, A):
                    bank = job("pT")
                    pe.wait_ge(drained["s"], a + 1)
                    for u in range(2):
                        m = pe.transpose(bank[:, u * P:(u + 1) * P], p_sb[:, u, :], ident[:])
                    m.then_inc(done["pT"], 1)
                if on(t, Q):
                    weigh_values(t, i, 7)
                    bank = job("oT")
                    pe.wait_ge(o_out[1], t - Q + 1)
                    transpose_pair(bank, o_sb).then_inc(done["oT"], 1)
                if on(t, C):
                    bank = job("dn")
                    pe.wait_ge(drained["gu3"], c + 1)
                    project(bank, h_sb, w_dn, blocks=FB).then_inc(done["dn"], 1)
                if on(t, A):
                    bank = job("y")
                    pe.wait_ge(drained["pT"], a + 1)
                    pe.wait_ge(drained["v"], a + 1)
                    for u in range(2):
                        m = pe.matmul(bank[:, u * 256:(u + 1) * 256], pT_sb[:, u, :], v_sb[:, u, :], start=True, stop=True)
                    m.then_inc(done["y"], 1)
                if on(t, C):
                    bank = job("pos")
                    pe.wait_ge(chosen_done, c + 1)
                    pe.matmul(bank[:, 0:E], before[:], chosen_bf[:, 0, :], start=True, stop=True)
                    pe.matmul(bank[:, E:2 * E], before[:], chosen_bf[:, 1, :], start=True, stop=False)
                    pe.matmul(bank[:, E:2 * E], ones_bf[:], chosen_bf[:, 0, :], start=False, stop=True)
                    pe.matmul(bank[:, 2 * E:3 * E], ones_bf[:], chosen_bf[:, 0, :], start=True, stop=False)
                    pe.matmul(bank[:, 2 * E:3 * E], ones_bf[:], chosen_bf[:, 1, :], start=False, stop=True)\
                        .then_inc(done["pos"], 1)
                if on(t, Q):
                    pe.wait_ge(drained["oT"], t - Q + 1)
                    project(o_ps, oT_sb, w_o).then_inc(yx_done, 1)

            ticks(pe, tick, C, PEEL, 2, PAIRS)

            pe.wait_ge(slots_f, 1)
            for name, _ in SHARED_JOBS[-N_SHARED:]:
                pe.wait_ge(drained[name], PAIRS)
            pe.wait_ge(yx_out, PAIRS)
            pe.transpose(shared_ps[0][:, 0:E], slot_f[:], ident[0:E, 0:E]).then_inc(slots_T, 1)

            def expert_tick(t, i):
                if on(t, 2, E):
                    n, k = t - 2, (i - 2)
                    wait(pe, xgT_out, n - 1)
                    pe.wait_ge(gathered[k % (2 * RING)], lap(n, k))
                    for kb in range(KB):
                        m = pe.transpose(score_ps[k % 2][:, kb * P:(kb + 1) * P],
                                         xg[k % (2 * RING)][:, kb * P:(kb + 1) * P], ident[:])
                    m.then_inc(xgT_done, 1)
                if on(t, 3, E):
                    n, k = t - 3, (i - 3)
                    pe.wait_ge(xgT_out, n + 1)
                    pe.wait_ge(we_loaded[k % (2 * RING)], lap(n, k, 32))
                    wait(pe, eh_done, n - 1)
                    for half in range(2):
                        for kb in range(KB):
                            m = pe.matmul(probT_ps[k % 2][:, half * P:(half + 1) * P],
                                          we_gu[k % (2 * RING)][:, kb, half * P:(half + 1) * P],
                                          xgT[k % 2][:, kb, :], start=(kb == 0), stop=(kb == KB - 1))
                    m.then_inc(egu_done, 1)
                if on(t, 4, E):
                    n, k = t - 4, (i - 4)
                    pe.wait_ge(eh_done, n + 1)
                    wait(pe, ey_done, n - 1)
                    pe.matmul(shared_ps[1 + k % 2][:, 0:D], eh[k % 2][:], we_dn[k % (2 * RING)][:],
                              start=True, stop=True).then_inc(edn_done, 1)

            ticks(pe, expert_tick, 4, 2 * RING, 2 * RING, E)

        @block.scalar
        def _(act):
            COPY, IDENT = ACT.Copy, ACT.Identity
            act.wait_ge(pre_pe, 1)
            act.activation(w_vT[:].rearrange("p k n -> p (k n)"), shared_ps[0][:, :], COPY).then_inc(pre, 1)

            def drain(name, dst, n, cols=512):
                act.wait_ge(done[name], n)
                act.activation(dst, bank_of[name][:, 0:cols], COPY).then_inc(drained[name], 1)

            def tick(t, i):
                a, b, q2, c = t - A, t - B, t - Q, t - C
                flat = "p k n -> p (k n)"

                def exp_quarter(q):
                    act.wait_ge(score_out, nth(q2, q))
                    act.activation(probs[q % 4][:], probs[q % 4][:], ACT.Exp, scale=SCALE).then_inc(exp_done, 1)

                def drain_quarter(q):
                    act.wait_ge(probT_done, nth(q2, q))
                    if q >= 4:
                        act.wait_ge(o_done, nth(q2, q - 4))
                    else:
                        wait(act, o_done, nth(q2 - 1, q + 4))
                    act.activation(probsT[q % 4][:].rearrange("p n q -> p (n q)"), probT_ps[q % 2][:, :], COPY)\
                        .then_inc(probT_out, 1)

                def exp_gate(j):
                    act.wait_ge(done[f"gu{j}"], c + 1)
                    if j >= 2:
                        act.wait_ge(drained[f"gu{j - 2}"], c + 1)
                    else:
                        wait(act, drained[f"gu{j + 2}"], c)
                    act.activation(eg[j % 2][:], bank_of[f"gu{j}"][:, 0:256], ACT.Exp, scale=-1.0).then_inc(eg_done[j], 1)

                if on(t, A):
                    drain("xT", xT[:].rearrange(flat), a + 1)
                if on(t, Q):
                    exp_quarter(0)
                if on(t, B):
                    drain("ctxT", ctxT[:], b + 1, 256)
                if on(t, Q):
                    exp_quarter(1)
                    drain_quarter(0)
                if on(t, A):
                    act.wait_ge(done["q"], a + 1)
                    act.activation(q_sb[:, 0, :], bank_of["q"][:, 0:256], IDENT, bias=b_qk[:, 0:1])
                    act.activation(q_sb[:, 1, :], bank_of["q"][:, 256:512], IDENT, bias=b_qk[:, 1:2]).then_inc(drained["q"], 1)
                if on(t, Q):
                    exp_quarter(2)
                    drain_quarter(1)
                if on(t, C):
                    drain("x2T", x2T[:].rearrange(flat), c + 1)
                if on(t, Q):
                    exp_quarter(3)
                    drain_quarter(2)
                if on(t, B):
                    drain("x1T", x1T[:].rearrange(flat), b + 1)
                if on(t, A):
                    act.wait_ge(done["k"], a + 1)
                    act.activation(k_sb[:, 0, :], bank_of["k"][:, 0:256], IDENT, bias=b_qk[:, 2:3])
                    act.activation(k_sb[:, 1, :], bank_of["k"][:, 256:512], IDENT, bias=b_qk[:, 3:4]).then_inc(drained["k"], 1)
                if on(t, Q):
                    exp_quarter(4)
                    drain_quarter(3)
                if on(t, C):
                    exp_gate(0)
                    act.wait_ge(drained["logits"], c + 1)
                    act.activation(ex[:], lg[:], ACT.Exp).then_inc(ex_done, 1)
                if on(t, A):
                    drain("v", v_sb[:].rearrange(flat), a + 1)
                if on(t, Q):
                    exp_quarter(5)
                    drain_quarter(4)
                if on(t, B):
                    act.wait_ge(done["qx"], b + 1)
                    for par in range(2):
                        for mb in range(2):
                            m = act.activation(qx[(i - B) % 2][:, mb, par, :], bank_of["qx"][:, mb * 256:(mb + 1) * 256],
                                               IDENT, bias=b_qm[:, par, mb:mb + 1], scale=par_mask[:, par:par + 1])
                    m.then_inc(drained["qx"], 1)
                if on(t, C):
                    exp_gate(1)
                if on(t, Q):
                    exp_quarter(6)
                    drain_quarter(5)
                if on(t, B):
                    act.wait_ge(done["kx"], b + 1)
                    for mb in range(2):
                        m = act.activation(kx[(i - B) % 2][:, mb, :], bank_of["kx"][:, mb * 256:(mb + 1) * 256],
                                           IDENT, bias=b_k[:, mb:mb + 1])
                    m.then_inc(drained["kx"], 1)
                if on(t, A):
                    act.wait_ge(s_max_sc, a + 1)
                    for u in range(2):
                        m = act.activation(p_sb[:, u, :], bank_of["s"][:, u * P:(u + 1) * P], ACT.Exp,
                                           bias=s_nmax_sc[:, u:u + 1], scale=SCALE, accum_out=s_sum[:, u:u + 1])
                    m.then_inc(drained["s"], 1)
                if on(t, Q):
                    exp_quarter(7)
                    drain_quarter(6)
                if on(t, B):
                    act.wait_ge(done["vx"], b + 1)
                    for u in range(2):
                        m = act.activation(vx[(i - B) % 2][:, u, :, 0:DH],
                                           bank_of["vx"][:, u * 256:(u + 1) * 256].rearrange("p (h d) -> p h d", d=DH), COPY)
                    m.then_inc(drained["vx"], 1)
                if on(t, C):
                    exp_gate(2)
                if on(t, Q):
                    drain_quarter(7)
                if on(t, C):
                    exp_gate(3)
                if on(t, A):
                    drain("pT", pT_sb[:].rearrange(flat), a + 1, 256)
                if on(t, Q):
                    drain("oT", oT_sb[:].rearrange(flat), q2 + 1)

            ticks(act, tick, C, PEEL, 2, PAIRS)

            def expert_tick(t, i):
                if on(t, 2, E):
                    n, k = t - 2, i - 2
                    act.wait_ge(xgT_done, n + 1)
                    wait(act, egu_done, n - 1)
                    act.activation(xgT[k % 2][:].rearrange("p k n -> p (k n)"), score_ps[k % 2][:, 0:256], COPY)\
                        .then_inc(xgT_out, 1)
                if on(t, 3, E):
                    n, k = t - 3, i - 3
                    act.wait_ge(egu_done, n + 1)
                    wait(act, eh_done, n - 1)
                    act.activation(ee[k % 2][:], probT_ps[k % 2][:, 0:P], ACT.Exp, scale=-1.0).then_inc(ee_done, 1)

            ticks(act, expert_tick, 4, 2 * RING, 2 * RING, E)

            out_tiles = out.rearrange("(n u) p f -> n p u f", u=FT)

            def store(n, i):
                act.wait_ge(f_norm, n + 1)
                act.dma_start(out_tiles[n], f_out[i][:]).then_inc(f_stored[i], 16)
            with act.Fori(0, T // (P * FT) // 2) as r:
                for u in range(2):
                    store(r * 2 + u, u)
            for i in range(2):
                act.wait_ge(f_stored[i], 16 * (T // (P * FT) // 2))

        @block.vector
        def _(dve):
            dve.wait_ge(loaded_w, 16 * W_LOADS)
            dve.wait_ge(consts, 1)
            for n, b in ((0, b_v), (1, b_vx)):
                for kb in range(KB):
                    m = dve.tensor_scalar(bv_rows[:, n, kb, :], bv_rows[:, n, kb, :], b[:, kb:kb + 1], None, ALU.add)
            m.then_inc(pre, 1)
            for par in range(2):
                m = dve.tensor_scalar(b_qm[:, par, :], b_q[:], par_mask[:, par:par + 1], None, ALU.mult)
            m.then_inc(pre, 1)
            dve.wait_ge(pre_pe, 2)
            dve.tensor_copy(w_vo[:].rearrange("p k n -> p (k n)"), shared_ps[1][:, :]).then_inc(pre, 1)
            dve.tensor_tensor(bias_a[:], shared_ps[2][:, 0:D], bout_rows[:, 0, :], ALU.add).then_inc(pre, 1)
            dve.tensor_tensor(bias_x[:], shared_ps[2][:, D:2 * D], bout_rows[:, 1, :], ALU.add).then_inc(pre, 1)

            def tick(t, i):
                a, q2, c = t - A, t - Q, t - C

                def quarter(q):
                    dve.wait_ge(score_done, nth(q2, q))
                    s = score_ps[q % 2][:, :].rearrange("p (n k) -> p n k", k=P)
                    dve.tensor_reduce(h_max[q % 2][:], s, AX.X, ALU.max).then_inc(max_done, 1)
                    dve.wait_ge(max_done, nth(q2, q))
                    if q >= 4:
                        dve.wait_ge(probT_done, nth(q2, q - 4))
                    else:
                        wait(dve, probT_done, nth(q2 - 1, q + 4))
                    dve.tensor_tensor(probs[q % 4][:], s, h_max[q % 2][:].unsqueeze(2).to_broadcast([P, 4, P]),
                                      ALU.subtract).then_inc(score_out, 1)

                def normalise_heads(u):
                    dve.wait_ge(o_done, nth(q2, 4 * u + 3))
                    o = o_ps[:, 0:HEADS * (DH + 1)].rearrange("p (h d) -> p h d", d=DH + 1)
                    dve.reciprocal(o_rsum[:], o[:, :, DH]).then_inc(o_recip[u], 1)
                    dve.wait_ge(o_recip[u], q2 + 1)
                    wait(dve, done["oT"], q2)
                    dve.tensor_tensor(o_sb[:, u, :].rearrange("p (h d) -> p h d", d=DH), o[:, :, 0:DH],
                                      o_rsum[:].unsqueeze(2).to_broadcast([P, HEADS, DH]), ALU.mult).then_inc(o_out[u], 1)

                STEPS = 3 * FB

                def gated(j):
                    bank = bank_of[f"gu{j}"]
                    n = c * STEPS + 3 * j
                    dve.wait_ge(eg_done[j], c + 1)
                    dve.tensor_scalar(eg_p1[:], eg[j % 2][:], 1.0, None, ALU.add).then_inc(silu_step, 1)
                    dve.wait_ge(silu_step, n + 1)
                    dve.reciprocal(sig[:], eg_p1[:]).then_inc(silu_step, 1)
                    dve.wait_ge(silu_step, n + 2)
                    dve.tensor_tensor(silu[:], bank[:, 0:256], sig[:], ALU.mult).then_inc(silu_step, 1)
                    dve.wait_ge(silu_step, n + 3)
                    if j == 0:
                        wait(dve, done["dn"], c)
                    dve.tensor_tensor(h_sb[:, j, :], bank[:, 256:512], silu[:], ALU.mult).then_inc(drained[f"gu{j}"], 1)

                def layer_norm(r, st, mv, rstd, dst, st_done, mv_done, rstd_done, dst_done, n):
                    for u in range(2):
                        m = dve.bn_stats(st[:, u, :], r[:, u, :])
                    m.then_inc(st_done, 1)
                    dve.wait_ge(st_done, n + 1)
                    carry_wait(dve)
                    for u in range(2):
                        m = dve.bn_aggr(mv[:, u, :], st[:, u, :])
                    m.then_inc(mv_done, 1)
                    dve.wait_ge(rstd_done, n + 1)
                    for u in range(2):
                        m = dve.tensor_scalar(dst[:, u, 0:D], r[:, u, :], mv[:, u, 0:1], rstd[:, u:u + 1],
                                              ALU.subtract, ALU.mult)
                    m.then_inc(dst_done, 1)

                GATE = 10

                def router():
                    n = c * GATE
                    bank = bank_of["logits"][:, 0:2 * (E + 1)].rearrange("p (u e) -> p u e", u=2)

                    def per_seq(col):
                        return col[:].unsqueeze(2).to_broadcast([P, 2, E])
                    dve.wait_ge(done["logits"], c + 1)
                    dve.tensor_reduce(lg_max[:], bank[:, :, 0:E], AX.X, ALU.max).then_inc(gate_step, 1)
                    dve.wait_ge(gate_step, n + 1)
                    dve.tensor_scalar(lg[:, :, E:E + 1], bank[:, :, E:E + 1], -1.0, None, ALU.mult)
                    dve.tensor_tensor(lg[:, :, 0:E], bank[:, :, 0:E], per_seq(lg_max), ALU.subtract).then_inc(drained["logits"], 1)

                def router_weights():
                    n = c * GATE + 1

                    def per_seq(col):
                        return col[:].unsqueeze(2).to_broadcast([P, 2, E])
                    dve.wait_ge(ex_done, c + 1)
                    dve.tensor_reduce(z_sum[:], ex[:, :, 0:E], AX.X, ALU.add).then_inc(gate_step, 1)
                    dve.tensor_scalar(sg1[:], ex[:, :, E], 1.0, None, ALU.add).then_inc(gate_step, 1)
                    dve.wait_ge(gate_step, n + 2)
                    dve.reciprocal(z_rsum[:], z_sum[:]).then_inc(gate_step, 1)
                    dve.wait_ge(gate_step, n + 3)
                    dve.tensor_tensor(prob[:], ex[:, :, 0:E], per_seq(z_rsum), ALU.mult).then_inc(gate_step, 1)
                    dve.wait_ge(gate_step, n + 4)
                    dve.reciprocal(sg[:], sg1[:]).then_inc(sg_done, 1)
                    for u in range(2):
                        m = dve.max(top[:, u, :], prob[:, u, :])
                    m.then_inc(gate_step, 1)
                    dve.wait_ge(gate_step, n + 5)
                    dve.tensor_reduce(top_sum[:], top[:], AX.X, ALU.add).then_inc(gate_step, 1)
                    for u in range(2):
                        m = dve.match_replace(out=marked[:, u, :], in_to_replace=top[:, u, :], in_values=prob[:, u, :], imm_value=-1.0)
                    m.then_inc(gate_step, 1)
                    dve.wait_ge(gate_step, n + 7)
                    dve.tensor_scalar(chosen[:], marked[:], 0.0, None, ALU.is_lt).then_inc(gate_step, 1)
                    wait(dve, done["pos"], c)
                    dve.tensor_scalar(chosen_bf[:], marked[:], 0.0, None, ALU.is_lt).then_inc(chosen_done, 1)
                    dve.wait_ge(gate_step, n + 8)
                    dve.reciprocal(top_rsum[:], top_sum[:]).then_inc(gate_step, 1)
                    dve.wait_ge(gate_step, n + 9)
                    for u in range(2):
                        m = dve.scalar_tensor_tensor(x2[(i - C) % 2][:, u, D:XROW], prob[:, u, :], top_rsum[:, u:u + 1],
                                                     chosen[:, u, :], ALU.mult, ALU.mult)
                    m.then_inc(weight_done, 1)

                PLACE = 5

                def places():
                    n = c * PLACE
                    bank = bank_of["pos"]
                    cnt = count[:].unsqueeze(1).to_broadcast([P, 2, E])
                    dve.wait_ge(done["pos"], c + 1)
                    wait(dve, drained["pos"], c)
                    dve.tensor_tensor(place[:], bank[:, 0:2 * E].rearrange("p (u e) -> p u e", u=2), cnt, ALU.add)\
                        .then_inc(place_step, 1)
                    dve.wait_ge(place_step, n + 1)
                    dve.scalar_tensor_tensor(kept[:], place[:], float(CAPACITY), chosen[:], ALU.is_lt, ALU.mult)\
                        .then_inc(place_step, 1)
                    dve.tensor_tensor(slot_key[:], slot_base[:].unsqueeze(1).to_broadcast([P, 2, E]), place[:],
                                      ALU.subtract).then_inc(place_step, 1)
                    dve.wait_ge(place_step, n + 3)
                    dve.tensor_tensor(key[:], slot_key[:], kept[:], ALU.mult).then_inc(place_step, 1)
                    dve.wait_ge(place_step, n + 4)
                    dve.tensor_tensor(count[:], bank[:, 2 * E:3 * E], count[:], ALU.add).then_inc(drained["pos"], 1)
                    for u in range(2):
                        m = dve.max(key8[:, u, :], key[:, u, :])
                    m.then_inc(place_step, 1)
                    dve.wait_ge(place_step, n + 5)
                    wait(dve, scattered[(i - C) % 2], half_count(c, i - C, 2 * TOP_K * 16) - 2 * TOP_K * 16)
                    dve.tensor_scalar(slot_no[(i - C) % 2][:], key8[:], -1.0, float(T), ALU.mult, ALU.add).then_inc(slot_done, 1)

                if on(t, Q):
                    for q in range(5):
                        quarter(q)
                if on(t, C):
                    router()
                if on(t, Q):
                    quarter(5)
                if on(t, C):
                    gated(0)
                    router_weights()
                if on(t, Q):
                    normalise_heads(0)
                    quarter(6)
                if on(t, C):
                    gated(1)
                if on(t, Q):
                    quarter(7)
                if on(t, A):
                    dve.wait_ge(done["s"], a + 1)
                    dve.tensor_reduce(s_nmax[:], bank_of["s"][:, 0:256].rearrange("p (u k) -> p u k", u=2), AX.X,
                                      ALU.max, negate=True).then_inc(s_max_done, 1)
                    dve.wait_ge(s_max_done, a + 1)
                    dve.tensor_scalar(s_nmax_sc[:], s_nmax[:], SCALE, None, ALU.mult).then_inc(s_max_sc, 1)
                if on(t, C):
                    gated(2)
                    gated(3)
                if on(t, Q):
                    normalise_heads(1)
                if on(t, C):
                    dve.wait_ge(done["dn"], c + 1)
                    wait(dve, resid_stored[(i - C) % 2], half_count(c, i - C) - 16)
                    dve.wait_ge(sg_done, c + 1)
                    for u in range(2):
                        m = dve.scalar_tensor_tensor(z_sb[(i - C) % 2][:, u, :], bank_of["dn"][:, u * D:(u + 1) * D],
                                                     sg[:, u:u + 1], x2[(i - C) % 2][:, u, 0:D], ALU.mult, ALU.add)
                    m.then_inc(drained["dn"], 1)
                if on(t, A):
                    dve.wait_ge(drained["s"], a + 1)
                    dve.reciprocal(s_rsum[:], s_sum[:]).then_inc(s_rsum_done, 1)
                    dve.wait_ge(done["y"], a + 1)
                    dve.wait_ge(s_rsum_done, a + 1)
                    dve.wait_ge(xb_done, a + 1)
                    for u in range(2):
                        m = dve.scalar_tensor_tensor(r1[:, u, :], bank_of["y"][:, u * D:(u + 1) * D], s_rsum[:, u:u + 1],
                                                     xb[:, u, :], ALU.mult, ALU.add)
                    m.then_inc(drained["y"], 1)
                    dve.wait_ge(drained["y"], a + 1)
                    wait(dve, done["x1T"], a)
                    wait(dve, x1b_done, a)
                    layer_norm(r1, st1, mv1, rstd1, x1, st1_done, mv1_done, rstd1_done, x1_done, a)
                if on(t, C):
                    places()
                if on(t, Q):
                    xi = (i - Q) % 2
                    dve.wait_ge(yx_done, q2 + 1)
                    dve.tensor_tensor(r2[:].rearrange("p u d -> p (u d)"), o_ps[:, :],
                                      x1b[xi][:].rearrange("p u d -> p (u d)"), ALU.add).then_inc(yx_out, 1)
                    dve.wait_ge(yx_out, q2 + 1)
                    wait(dve, token_stored[xi], half_count(q2, i - Q) - 16)
                    wait(dve, done["x2T"], q2 - 1)
                    layer_norm(r2, st2, mv2, rstd2, x2[xi], st2_done, mv2_done, rstd2_done, x2_done, q2)

            ticks(dve, tick, C, PEEL, 2, PAIRS)

            dve.wait_ge(slots_loaded, 16)
            dve.tensor_copy(slot_f[:], slot_i[:]).then_inc(slots_f, 1)
            dve.wait_ge(slots_T, 1)
            dve.tensor_copy(slot_ids[:], shared_ps[0][:, 0:E]).then_inc(slots_u, 1)
            dve.wait_ge(slots_u, 1)

            def expert_tick(t, i):
                if on(t, 0, E):
                    k = i % (2 * RING)
                    wait(dve, added, (t - 2 * RING + 1) * 16)
                    dve.tensor_copy(ids[k][:], slot_ids[:, column(t)]).then_inc(id_done, 1)
                if on(t, 3, E):
                    n, k = t - 3, i - 3
                    bank = probT_ps[k % 2]
                    dve.wait_ge(ee_done, n + 1)
                    dve.tensor_scalar(ee_p1[:], ee[k % 2][:], 1.0, None, ALU.add).then_inc(estep, 1)
                    dve.wait_ge(estep, n * 3 + 1)
                    dve.reciprocal(esig[:], ee_p1[:]).then_inc(estep, 1)
                    dve.wait_ge(estep, n * 3 + 2)
                    dve.tensor_tensor(esilu[:], bank[:, 0:P], esig[:], ALU.mult).then_inc(estep, 1)
                    dve.wait_ge(estep, n * 3 + 3)
                    wait(dve, edn_done, n - 1)
                    dve.tensor_tensor(eh[k % 2][:], bank[:, P:2 * P], esilu[:], ALU.mult).then_inc(eh_done, 1)
                if on(t, 4, E):
                    n, k = t - 4, (i - 4) % (2 * RING)
                    dve.wait_ge(edn_done, n + 1)
                    dve.tensor_scalar(ey[k][:], shared_ps[1 + k % 2][:, 0:D], xg[k][:, column(n + D)], None,
                                      ALU.mult).then_inc(ey_done, 1)

            ticks(dve, expert_tick, 4, 2 * RING, 2 * RING, E)

            def final(n, i, first):
                s = n * 2
                dve.wait_ge(f_loaded[i], half_count(n, i))
                for u in range(FT):
                    m = dve.bn_stats(f_st[:, u, :], f_in[i][:, u, :])
                m.then_inc(f_step, 1)
                dve.wait_ge(f_step, s + 1)
                carry_wait(dve)
                for u in range(FT):
                    m = dve.bn_aggr(f_mv[:, u, :], f_st[:, u, :])
                m.then_inc(f_step, 1)
                dve.wait_ge(f_rstd_done, n + 1)
                wait(dve, f_stored[i], half_count(n, i) - 16)
                for u in range(FT):
                    m = dve.tensor_scalar(f_out[i][:, u, :], f_in[i][:, u, :], f_mv[:, u, 0:1], f_rstd[:, u:u + 1],
                                          ALU.subtract, ALU.mult)
                m.then_inc(f_norm, 1)
            for n in range(2):
                final(n, n, True)
            with dve.Fori(1, T // (P * FT) // 2) as r:
                for u in range(2):
                    final(r * 2 + u, u, False)

        @block.gpsimd
        def _(pool):
            steps = 0

            def step(instruction):
                nonlocal steps
                steps += 1
                instruction.then_inc(pool_step, 1)
                pool.wait_ge(pool_step, steps)

            step(pool.memset(ident[:], 0.0))
            step(pool.affine_select(out=ident[:], in_=ident[:], compare_op=ALU.not_equal, fill=1.0, base=0,
                                    pattern=[[-1, P]], channel_multiplier=1))
            step(pool.memset(before[:], 1.0))
            step(pool.affine_select(out=before[:], in_=before[:], compare_op=ALU.is_gt, fill=0.0, base=0,
                                    pattern=[[1, P]], channel_multiplier=-1))
            step(pool.iota(row_no[:], pattern=[[0, 1]], base=0, channel_multiplier=1))
            step(pool.tensor_copy(row_f[:], row_no[:]))
            step(pool.memset(par_mask[:], 0.0))
            for g in range(1, P // DH):
                step(pool.tensor_scalar(row_ge[:], row_f[:], float(DH * g), 1.0 if g % 2 else -1.0, ALU.is_ge, ALU.mult))
                step(pool.tensor_tensor(par_mask[:, 1:2], par_mask[:, 1:2], row_ge[:], ALU.add))
            step(pool.tensor_scalar(par_mask[:, 0:1], par_mask[:, 1:2], -1.0, 1.0, ALU.mult, ALU.add))
            step(pool.memset(bv_rows[:], 0.0))
            step(pool.memset(zero_rows[:], 0.0))
            step(pool.iota(spare_slots[:], pattern=[[1, CAPACITY]], base=T, channel_multiplier=0))
            step(pool.memset(ones_bf[:], 1.0))
            step(pool.memset(neg_half[:], -0.5))
            step(pool.memset(f_nh[:], -0.5))
            step(pool.memset(eps_col[:], EPS))
            step(pool.iota(pair_step[:], pattern=[[0, 1]], base=2 * P, channel_multiplier=0))
            step(pool.memset(count[:], 0.0))
            for v in vx:
                step(pool.memset(v[:, :, :, DH:DH + 1], 1.0))
            for u in range(2):
                step(pool.iota(token_no[u][:], pattern=[[0, 1]], base=u * P - 2 * P, channel_multiplier=1))
            step(pool.iota(base_i[:], pattern=[[-CAPACITY, E]], base=T, channel_multiplier=0))
            pool.tensor_copy(slot_base[:], base_i[:]).then_inc(consts, 1)
            slot_bound = pool.to_reg(E * CAPACITY - 1)
            row_bound = pool.to_reg(T + CAPACITY - 1)
            pool.wait_ge(pre, 6)
            pool.wait_ge(tables_set, 48)

            def tick(t, i):
                a, b, q2, c = t - A, t - B, t - Q, t - C
                if on(t, A):
                    pool.wait_ge(x_loaded[i % 2], half_count(t, i))
                    wait(pool, drained["y"], a)
                    pool.tensor_tensor(xb[:], x_in[i % 2][:], bias_a[:].unsqueeze(1).to_broadcast([P, 2, D]), ALU.add)\
                        .then_inc(xb_done, 1)
                if on(t, B):
                    pool.wait_ge(x1_done, b + 1)
                    wait(pool, yx_out, b - 1)
                    pool.tensor_tensor(x1b[(i - B) % 2][:], x1[:], bias_x[:].unsqueeze(1).to_broadcast([P, 2, D]), ALU.add)\
                        .then_inc(x1b_done, 1)

                def scatter(c, ci, k):
                    if k == 0:
                        wait(pool, scattered[(ci + 1) % 2], half_count(c - 1, ci - 1, 2 * TOP_K * 16))
                        for u in range(2):
                            m = pool.tensor_tensor(token_no[u][:], token_no[u][:], pair_step[:], ALU.add)
                        m.then_inc(token_no_done, 1)
                        wait(pool, token_no_done, c + 1)
                        carry_wait(pool)
                    for u in range(2):
                        pool.indirect_dma_start(slot_table[:, :], bass.IndirectOffsetOnAxis(ap=slot_no[ci % 2][:, u, k:k + 1], axis=0),
                                                token_no[u][:], None, bounds_check=slot_bound,
                                                oob_is_err=False).then_inc(scattered[ci % 2], 16)
                if on(t, C + 1):
                    wait(pool, slot_done, c)
                    for k in range(TOP_K):
                        scatter(c - 1, i - C - 1, k)

                def rstd(mv, ve, r, mv_done, ve_done, rstd_done, n):
                    pool.wait_ge(mv_done, n + 1)
                    pool.tensor_tensor(ve[:], mv[:, :, 1], eps_col[:, 0:2], ALU.add).then_inc(ve_done, 1)
                    pool.wait_ge(ve_done, n + 1)
                    pool.tensor_tensor(r[:], ve[:], neg_half[:], ALU.pow).then_inc(rstd_done, 1)
                if on(t, A):
                    rstd(mv1, ve1, rstd1, mv1_done, ve1_done, rstd1_done, a)
                if on(t, Q):
                    rstd(mv2, ve2, rstd2, mv2_done, ve2_done, rstd2_done, q2)

            ticks(pool, tick, C + 1, PEEL, 2, PAIRS)

            for i in range(2):
                pool.wait_ge(scattered[i], PAIRS // 2 * 2 * TOP_K * 16)
                pool.wait_ge(token_stored[i], PAIRS // 2 * 16)
                pool.wait_ge(resid_stored[i], PAIRS // 2 * 16)
            pool.dma_start(slot_i[:], slots_by_expert).then_inc(slots_loaded, 16)

            def expert_tick(t, i):
                if on(t, 0, E):
                    k = i % (2 * RING)
                    wait(pool, id_done, t + 1)
                    carry_wait(pool)
                    pool.indirect_dma_start(xg[k][:], None, token_table[:, :],
                                            bass.IndirectOffsetOnAxis(ap=ids[k][:], axis=0),
                                            bounds_check=row_bound).then_inc(gathered[k], 16)
                if on(t, 4, E):
                    n, k = t - 4, (i - 4) % (2 * RING)
                    pool.wait_ge(ey_done, n + 1)
                    wait(pool, added, n * 16)
                    carry_wait(pool)
                    pool.indirect_dma_start(resid_table[:, :], bass.IndirectOffsetOnAxis(ap=ids[k][:], axis=0),
                                            ey[k][:], None, bounds_check=row_bound,
                                            compute_op=ALU.add).then_inc(added, 16)

            ticks(pool, expert_tick, 4, 2 * RING, 2 * RING, E)

            def final(n):
                pool.wait_ge(f_step, n * 2 + 2)
                pool.tensor_tensor(f_ve[:], f_mv[:, :, 1], eps_col[:], ALU.add).then_inc(f_ve_done, 1)
                pool.wait_ge(f_ve_done, n + 1)
                pool.tensor_tensor(f_rstd[:], f_ve[:], f_nh[:], ALU.pow).then_inc(f_rstd_done, 1)
            with pool.Fori(0, T // (P * FT)) as n:
                final(n)


_INS = ['x', 'ctx_512', 'L0_attn_W_qkv', 'L0_attn_b_qkv', 'L0_attn_W_out', 'L0_attn_b_out', 'L0_xattn_Wq', 'L0_xattn_bq',
        'L0_xattn_Wk', 'L0_xattn_bk', 'L0_xattn_Wv', 'L0_xattn_bv', 'L0_xattn_Wo', 'L0_xattn_bo', 'L0_ffn_gate_w',
        'L0_ffn_shared_gate_w', 'L0_ffn_shared_gate_up_w', 'L0_ffn_shared_down_w', 'L0_ffn_expert_gate_up_w',
        'L0_ffn_expert_down_w']
_OUTS = [((64, 128, 256), 'float32')]


def kernel(**inputs):
    import numpy as _np
    import concourse.bacc as _bacc
    from concourse import mybir as _mybir
    from concourse.bass_utils import run_bass_kernel_spmd as _run

    nc = _bacc.Bacc("TRN2", target_bir_lowering=False, num_devices=1)
    arrays, args = {}, []
    for name in _INS:
        a = _np.ascontiguousarray(inputs[name])
        arrays[f"in_{name}_dram"] = a
        args.append(nc.dram_tensor(f"in_{name}_dram", a.shape, _mybir.dt.from_np(a.dtype), kind="ExternalInput").ap())
    for i, (shape, dtype) in enumerate(_OUTS):
        dt = _mybir.dt.from_np(_np.dtype(dtype))
        args.append(nc.dram_tensor(f"out_{i}_dram", shape, dt, kind="ExternalOutput").ap())
    decoder_layer(nc, *args)
    r = _run(nc, [arrays], core_ids=[0])
    return r.results[0]["out_0_dram"]
```

```python
from contextlib import ExitStack

import concourse.bass as bass
from concourse import mybir

F32 = mybir.dt.float32
BF16 = mybir.dt.bfloat16
I32 = mybir.dt.int32
U32 = mybir.dt.uint32
ALU = mybir.AluOpType
ACT = mybir.ActivationFunctionType
AX = mybir.AxisListType

P = 128
EPS = 1e-5
TOP_K = 8
CAPACITY = 128
HEADS = 16
A, B, Q, C = 0, 1, 2, 3
PEEL = 6
QUARTERS = 8

SHARED_JOBS = [("xT", A), ("ctxT", B), ("q", A), ("kx", B), ("k", A), ("vx", B), ("v", A),
               ("x1T", B), ("s", A), ("x2T", C), ("logits", C), ("gu0", C), ("qx", B), ("gu1", C),
               ("pT", A), ("gu2", C), ("gu3", C), ("pos", C), ("dn", C), ("y", A), ("yx", Q)]
N_SHARED = 3
assert len(SHARED_JOBS) % N_SHARED == 0


def decoder_layer(nc, x, ctx_in, W_qkv, b_qkv, W_out, b_out, Wq, bq, Wk, bk, Wv, bv, Wo, bo,
                  gate_w, shared_gate_w, shared_gate_up_w, shared_down_w,
                  expert_gate_up_w, expert_down_w, out):
    NSEQ, S, D = x.shape
    DC = ctx_in.shape[2]
    T = NSEQ * S
    PAIRS = NSEQ // 2
    E = gate_w.shape[1]
    FS = shared_down_w.shape[0]
    FB = FS // P
    DH = D // HEADS
    KB = D // P
    SCALE = 1.0 / DH ** 0.5
    ROW = D + E + 1
    assert S == P and D == 2 * P and DC == P and FB == 4 and E == 64 and PAIRS > PEEL
    assert expert_down_w.shape[1] == P

    x_pairs = x.rearrange("(n u) p d -> n p u d", u=2)
    ctx_pairs = ctx_in.rearrange("(n u) p d -> n p u d", u=2)

    slot_table = nc.dram_tensor("slot_table", [E * CAPACITY, ROW], F32, kind="Internal")
    slots_by_expert = slot_table[:, :].rearrange("(e c) f -> e c f", c=CAPACITY)
    slots_by_place = slot_table[:, :].rearrange("(e c) f -> c e f", c=CAPACITY)
    resid_table = nc.dram_tensor("resid_table", [T + CAPACITY, D], F32, kind="Internal")
    resid_table2 = nc.dram_tensor("resid_table2", [T + CAPACITY, D], F32, kind="Internal")
    resid_pairs = resid_table[0:T, :].rearrange("(n u p) f -> n p u f", u=2, p=P)
    resid_pairs2 = resid_table2[0:T, :].rearrange("(n u p) f -> n p u f", u=2, p=P)

    es = ExitStack()
    with es:
        def sb(name, shape, dt=F32):
            return es.enter_context(nc.sbuf_tensor(name, shape, dt))

        def psum(name):
            return es.enter_context(nc.psum_tensor(name, [P, 512], F32))

        def sem(name):
            return es.enter_context(nc.semaphore(name))

        RING = 4
        ident = sb("ident", [P, P])
        before = sb("before", [P, P], BF16)
        ones_bf = sb("ones_bf", [P, P], BF16)
        par_mask = sb("par_mask", [P, 2])
        eps_col = sb("eps_col", [P, 4])
        neg_half = sb("neg_half", [P, 2])
        slot_base = sb("slot_base", [P, E])
        base_i = sb("base_i", [P, E], I32)
        row_no = sb("row_no", [P, 1], I32)
        row_f = sb("row_f", [P, 1])
        row_ge = sb("row_ge", [P, 1])
        spare_rows = sb("spare_rows", [P, ROW])
        zero_pair = sb("zero_pair", [P, 2, D])
        w_qk = sb("w_qk", [P, KB, 2 * D])
        w_v = sb("w_v", [P, KB, D])
        w_vT = sb("w_vT", [P, KB, D])
        w_out = sb("w_out", [P, KB, D])
        w_vo = sb("w_vo", [P, KB, D])
        w_q = sb("w_q", [P, KB, D])
        w_k = sb("w_k", [P, D])
        w_vx = sb("w_vx", [P, D])
        w_o = sb("w_o", [P, KB, D])
        w_gate = sb("w_gate", [P, KB, E + 1])
        w_gu = sb("w_gu", [P, KB, 2 * FS])
        w_dn = sb("w_dn", [P, FB, D])
        b_qk = sb("b_qk", [P, 4])
        b_v = sb("b_v", [P, KB])
        b_q = sb("b_q", [P, KB])
        b_q1 = sb("b_q1", [P, KB])
        b_qm = sb("b_qm", [P, 2, KB])
        b_k = sb("b_k", [P, KB])
        b_vx = sb("b_vx", [P, KB])
        bv_rows = sb("bv_rows", [P, 2, KB, P])
        bias_a = sb("bias_a", [P, D])
        bias_x = sb("bias_x", [P, D])
        bout_rows = sb("bout_rows", [P, 2, D])
        x_in = [sb(f"x_in{i}", [P, 2, D]) for i in range(2)]
        ctx_sb = [sb(f"ctx_sb{i}", [P, 2, DC]) for i in range(2)]
        xT = sb("xT", [P, KB, 256])
        q_sb = sb("q_sb", [P, KB, 256])
        k_sb = sb("k_sb", [P, KB, 256])
        v_sb = sb("v_sb", [P, 2, D])
        xb = sb("xb", [P, 2, D])
        s_nmax = sb("s_nmax", [P, 2])
        s_sum = sb("s_sum", [P, 2])
        s_rsum = sb("s_rsum", [P, 2])
        p_sb = sb("p_sb", [P, 2, P])
        pT_sb = sb("pT_sb", [P, 2, P])
        r1 = sb("r1", [P, 2, D])
        st1 = sb("st1", [P, 2, 6])
        mv1 = sb("mv1", [P, 2, 2])
        ve1 = sb("ve1", [P, 2])
        rstd1 = sb("rstd1", [P, 2])
        x1 = sb("x1", [P, 2, D])
        x1b = [sb(f"x1b{i}", [P, 2, D]) for i in range(2)]
        x1T = sb("x1T", [P, KB, 256])
        ctxT = sb("ctxT", [P, 256])
        qx = [sb(f"qx{i}", [P, KB, 2, 256]) for i in range(2)]
        kx = [sb(f"kx{i}", [P, KB, 256]) for i in range(2)]
        vx = [sb(f"vx{i}", [P, 2, HEADS // 2, 2, 2 * DH]) for i in range(2)]
        h_nmax = [sb(f"h_nmax{i}", [P, 4]) for i in range(4)]
        h_sum = [sb(f"h_sum{i}", [P, 4]) for i in range(4)]
        h_rsum = [sb(f"h_rsum{i}", [P, 4]) for i in range(4)]
        probs = [sb(f"probs{i}", [P, 4, P]) for i in range(4)]
        probsT_all = sb("probsT_all", [P, QUARTERS, 4, P])
        probsT = [probsT_all[:, i] for i in range(QUARTERS)]
        oT_sb = sb("oT_sb", [P, KB, 256])
        r2 = sb("r2", [P, 2, D])
        st2 = sb("st2", [P, 2, 6])
        mv2 = sb("mv2", [P, 2, 2])
        ve2 = sb("ve2", [P, 2])
        rstd2 = sb("rstd2", [P, 2])
        x2 = [sb(f"x2_{i}", [P, 2, D]) for i in range(2)]
        x2T = sb("x2T", [P, KB, 256])
        lg_max = sb("lg_max", [P, 2])
        lg = sb("lg", [P, 2, E + 1])
        ex = sb("ex", [P, 2, E + 1])
        z_sum = sb("z_sum", [P, 2])
        z_rsum = sb("z_rsum", [P, 2])
        sg1 = sb("sg1", [P, 2])
        sg = sb("sg", [P, 2])
        prob = sb("prob", [P, 2, E])
        top = sb("top", [P, 2, TOP_K])
        marked = sb("marked", [P, 2, E])
        chosen = sb("chosen", [P, 2, E])
        chosen_bf = sb("chosen_bf", [P, 2, E], BF16)
        top_sum = sb("top_sum", [P, 2])
        top_rsum = sb("top_rsum", [P, 2])
        count = sb("count", [P, E])
        place = sb("place", [P, 2, E])
        kept = sb("kept", [P, 2, E])
        slot_key = sb("slot_key", [P, 2, E])
        key = sb("key", [P, 2, E])
        key8 = sb("key8", [P, 2, TOP_K])
        slot_no = [sb(f"slot_no{i}", [P, 2, TOP_K], U32) for i in range(2)]
        send = [sb(f"send{i}", [P, 2, ROW]) for i in range(2)]
        th = [sb(f"th{i}", [P, 256]) for i in range(2)]
        silu = [sb(f"silu{i}", [P, 256]) for i in range(2)]
        h_sb = sb("h_sb", [P, FB, 256])
        z_sb = [sb(f"z_sb{i}", [P, 2, D]) for i in range(2)]
        ids = [sb(f"ids{i}", [P, 1], U32) for i in range(2 * RING)]
        xg = [sb(f"xg{i}", [P, ROW]) for i in range(2 * RING)]
        we_gu = [sb(f"we_gu{i}", [P, KB, 2 * P]) for i in range(2 * RING)]
        we_dn = [sb(f"we_dn{i}", [P, D]) for i in range(2 * RING)]
        xgT = [sb(f"xgT{i}", [P, KB, P]) for i in range(2)]
        eth = [sb(f"eth{i}", [P, P]) for i in range(2)]
        esilu = [sb(f"esilu{i}", [P, P]) for i in range(2)]
        eh = [sb(f"eh{i}", [P, P]) for i in range(2)]
        ey = [sb(f"ey{i}", [P, D]) for i in range(2 * RING)]
        FT = 4
        f_in = [sb(f"f_in{i}", [P, FT, D]) for i in range(2)]
        f_in = [buffer[:] for buffer in f_in]
        f_in += [w_gu[:, i].rearrange("p (t d) -> p t d", t=FT) for i in range(KB)]
        f_in2 = [probsT_all[:, 2 * i:2 * i + 2].rearrange("p a n q -> p (a n q)")
                 .rearrange("p (t d) -> p t d", t=FT) for i in range(4)]
        f_nb = [sb(f"f_nb{i}", [P, FT]) for i in range(2)]
        f_st = [sb(f"f_st{i}", [P, FT, 6]) for i in range(2)]
        f_mv = [sb(f"f_mv{i}", [P, FT, 2]) for i in range(2)]
        f_ve = [sb(f"f_ve{i}", [P, FT]) for i in range(2)]
        f_rstd = [sb(f"f_rstd{i}", [P, FT]) for i in range(2)]
        f_nh = sb("f_nh", [P, FT])

        score_ps = [psum(f"score_ps{i}") for i in range(2)]
        probT_ps = [psum(f"probT_ps{i}") for i in range(2)]
        o_ps = psum("o_ps")
        shared_ps = [psum(f"shared_ps{i}") for i in range(N_SHARED)]
        bank_of = {job: shared_ps[i % N_SHARED] for i, (job, _) in enumerate(SHARED_JOBS)}

        done = {job: sem(f"{job}_done") for job, _ in SHARED_JOBS}
        drained = {job: sem(f"{job}_out") for job, _ in SHARED_JOBS}
        score_done = sem("score_done")
        max_done = sem("max_done")
        exp_done = sem("exp_done")
        probT_done = sem("probT_done")
        probT_out = sem("probT_out")
        recip_done, norm_done = sem("recip_done"), sem("norm_done")
        o_done = [sem(f"o_done{u}") for u in range(2)]
        o_out = [sem(f"o_out{u}") for u in range(2)]
        consts = sem("consts")
        carried = [sem("carried_pool"), sem("carried_vector")]
        pool_step = sem("pool_step")
        loaded_w = sem("loaded_w")
        tables_set, slots_filled = sem("tables_set"), sem("slots_filled")
        pre = sem("pre")
        pre_pe = sem("pre_pe")
        x_loaded = [sem(f"x_loaded{i}") for i in range(2)]
        ctx_loaded = [sem(f"ctx_loaded{i}") for i in range(2)]
        xb_done, x1b_done = sem("xb_done"), sem("x1b_done")
        s_max_done = sem("s_max_done")
        ve1_done, rstd1_done, ve2_done, rstd2_done = (sem(n) for n in ("ve1_done", "rstd1_done", "ve2_done", "rstd2_done"))
        s_rsum_done, st1_done, mv1_done, x1_done = (sem(n) for n in ("s_rsum_done", "st1_done", "mv1_done", "x1_done"))
        st2_done, mv2_done, x2_done = (sem(n) for n in ("st2_done", "mv2_done", "x2_done"))
        ex_done = sem("ex_done")
        gate_step = sem("gate_step")
        chosen_done, sg_done = (sem(n) for n in ("chosen_done", "sg_done"))
        place_step, slot_done = sem("place_step"), sem("slot_done")
        th_done = [sem(f"th_done{j}") for j in range(FB)]
        silu_step = sem("silu_step")
        resid_stored = [sem(f"resid_stored{i}") for i in range(2)]
        scattered = [sem(f"scattered{i}") for i in range(2)]
        expert_loaded = [sem(f"expert_loaded{i}") for i in range(2 * RING)]
        xgT_done, xgT_out = sem("xgT_done"), sem("xgT_out")
        egu_done, eth_done, estep, eh_done = sem("egu_done"), sem("eth_done"), sem("estep"), sem("eh_done")
        edn_done, ey_done = sem("edn_done"), sem("ey_done")
        added = [sem(f"added{i}") for i in range(2)]
        f_loaded = [sem(f"f_loaded{i}") for i in range(4)]
        f_sum, f_st_done, f_mv_done, f_ve_done, f_rstd_done, f_nb_done, f_norm = (
            sem(n) for n in ("f_sum", "f_st_done", "f_mv_done", "f_ve_done", "f_rstd_done", "f_nb_done", "f_norm"))
        f_stored = [sem(f"f_stored{i}") for i in range(4)]

        def wait(eng, s, n):
            if not isinstance(n, int) or n > 0:
                eng.wait_ge(s, n)

        def carry_wait(eng):
            eng.sem_inc(carried[eng is nc.vector], 1)

        def ticks(eng, tick, lags, peel, unroll, total):
            for t in range(peel):
                tick(t, t)
            with eng.Fori(peel // unroll, total // unroll) as r:
                for u in range(unroll):
                    tick(r * unroll + u, u)
            for t in range(total, total + lags):
                tick(t, t)

        def on(t, lag, total=PAIRS):
            return not isinstance(t, int) or 0 <= t - lag < total

        def bank_free(pe, job, t):
            names = [n for n, _ in SHARED_JOBS]
            i, back = names.index(job), 0
            while True:
                i -= N_SHARED
                if i < 0:
                    i += len(names)
                    back += 1
                if isinstance(t, int) and t - back < 0:
                    return
                name, lag = SHARED_JOBS[i]
                if on(t - back, lag):
                    pe.wait_ge(drained[name], t - back - lag + 1)
                    return

        def half_count(n, i, inc=16):
            return n * (inc // 2) + (inc - i % 2 * (inc // 2))

        def lap(n, k, inc=16, ring=2 * RING):
            return n * (inc // ring) + (inc - k % ring * (inc // ring))

        def nth(n, q):
            return n * QUARTERS + (q + 1)

        def column(n):
            return bass.ds(n, 1)

        W_LOADS = 18
        FILLS = C
        F_STEPS = T // (P * FT)
        RESID_STORES = 2

        block = es.enter_context(nc.Block())

        @block.sync
        def _(sp):
            for dst, src in ((x_in[0][:], x_pairs[0]),):
                sp.dma_start(dst, src).then_inc(x_loaded[0], 16)
            with nc.allow_non_contiguous_dma(reason="bias vectors, once"):
                sp.dma_start(w_v[:], W_qkv[:, 2 * D:3 * D].rearrange("(k p) n -> p k n", p=P)).then_inc(loaded_w, 16)
                sp.dma_start(w_out[:], W_out.rearrange("(k p) n -> p k n", p=P)).then_inc(loaded_w, 16)
                sp.dma_start(w_qk[:], W_qkv[:, 0:2 * D].rearrange("(k p) n -> p k n", p=P)).then_inc(loaded_w, 16)
                sp.dma_start(b_qk[:], b_qkv[0:2 * D].rearrange("(m p) -> p m", p=P)).then_inc(loaded_w, 16)
                sp.dma_start(b_v[:], b_qkv[2 * D:3 * D].rearrange("(m p) -> p m", p=P)).then_inc(loaded_w, 16)
                sp.dma_start(bout_rows[:, 0, :], b_out.rearrange("(o n) -> o n", o=1).to_broadcast([P, D])).then_inc(loaded_w, 16)
                sp.dma_start(bout_rows[:, 1, :], bo.rearrange("(o n) -> o n", o=1).to_broadcast([P, D])).then_inc(loaded_w, 16)
                sp.dma_start(w_q[:], Wq.rearrange("(k p) n -> p k n", p=P)).then_inc(loaded_w, 16)
                sp.dma_start(w_k[:], Wk[:, :]).then_inc(loaded_w, 16)
                sp.dma_start(w_vx[:], Wv[:, :]).then_inc(loaded_w, 16)
                sp.dma_start(w_o[:], Wo.rearrange("(k p) n -> p k n", p=P)).then_inc(loaded_w, 16)
                sp.dma_start(b_q[:], bq.rearrange("(m p) -> p m", p=P)).then_inc(loaded_w, 16)
                sp.dma_start(b_k[:], bk.rearrange("(m p) -> p m", p=P)).then_inc(loaded_w, 16)
                sp.dma_start(b_vx[:], bv.rearrange("(m p) -> p m", p=P)).then_inc(loaded_w, 16)
                sp.dma_start(w_gate[:, :, 0:E], gate_w.rearrange("(k p) n -> p k n", p=P)).then_inc(loaded_w, 16)
                sp.dma_start(w_gate[:, :, E:E + 1], shared_gate_w.rearrange("(k p) n -> p k n", p=P)).then_inc(loaded_w, 16)
                sp.dma_start(w_gu[:], shared_gate_up_w.rearrange("(k p) n -> p k n", p=P)).then_inc(loaded_w, 16)
                sp.dma_start(w_dn[:], shared_down_w.rearrange("(k p) n -> p k n", p=P)).then_inc(loaded_w, 16)
            sp.wait_ge(consts, 1)
            sp.dma_start(resid_table[T:T + CAPACITY, :], spare_rows[:, 0:D]).then_inc(tables_set, 16)
            sp.dma_start(resid_table2[T:T + CAPACITY, :], spare_rows[:, 0:D]).then_inc(tables_set, 16)

            def tick(t, i):
                if on(t + 1, A):
                    wait(sp, done["xT"], t)
                    wait(sp, xb_done, t)
                    sp.dma_start(x_in[(i + 1) % 2][:], x_pairs[t + 1]).then_inc(x_loaded[(i + 1) % 2], 16)
                if isinstance(t, int) and t < FILLS:
                    part = slice(t * (E // FILLS), (t + 1) * (E // FILLS))
                    sp.dma_start(slots_by_place[:, part, :],
                                 spare_rows[:].unsqueeze(1).to_broadcast([P, E // FILLS, ROW])).then_inc(slots_filled, 16)
                if on(t, A):
                    wait(sp, done["ctxT"], t - 1)
                    sp.dma_start(ctx_sb[i % 2][:], ctx_pairs[t]).then_inc(ctx_loaded[i % 2], 16)
                if on(t, C):
                    c, ci = t - C, (i - C) % 2
                    sp.wait_ge(drained["dn"], c + 1)
                    sp.dma_start(resid_pairs2[c], zero_pair[:]).then_inc(resid_stored[ci], 16)
                    sp.dma_start(resid_pairs[c], z_sb[ci][:]).then_inc(resid_stored[ci], 16)

            for t in range(PEEL):
                tick(t, t)
            with sp.Fori(PEEL // 2, PAIRS // 2 - 1) as r:
                for u in range(2):
                    tick(r * 2 + u, u)
            for t in range(PAIRS - 2, PAIRS + C):
                tick(t, t)

            def load_weights(n, i):
                sp.dma_start(we_gu[i][:], expert_gate_up_w[n].rearrange("(k p) f -> p k f", p=P)).then_inc(expert_loaded[i], 16)
                sp.dma_start(we_dn[i][:], expert_down_w[n]).then_inc(expert_loaded[i], 16)

            def load_slots(n, i):
                sp.dma_start(xg[i][:], slots_by_expert[n]).then_inc(expert_loaded[i], 16)

            for n in range(2 * RING):
                load_weights(n, n)
            for i in range(2):
                sp.wait_ge(scattered[i], PAIRS // 2 * 2 * TOP_K * 16)
            for n in range(2 * RING):
                load_slots(n, n)
            with sp.Fori(1, E // (2 * RING)) as r:
                for u in range(2 * RING):
                    n = r * (2 * RING) + u
                    sp.wait_ge(ey_done, n - 2 * RING + 1)
                    load_slots(n, u)
                    load_weights(n, u)

            for i in range(2):
                sp.wait_ge(added[i], 16 * E // 2)
            f_tiles = resid_table[0:T, :].rearrange("(n u p) f -> n p u f", u=FT, p=P)
            f_tiles2 = resid_table2[0:T, :].rearrange("(n u p) f -> n p u f", u=FT, p=P)

            def load_resid(n, i):
                sp.dma_start(f_in[i], f_tiles[n]).then_inc(f_loaded[i], 16)
                sp.dma_start(f_in2[i], f_tiles2[n]).then_inc(f_loaded[i], 16)
            for n in range(4):
                load_resid(n, n)
            with sp.Fori(1, F_STEPS // 4) as r:
                for u in range(4):
                    sp.wait_ge(f_stored[u], r * 16)
                    load_resid(r * 4 + u, u)

        @block.tensor
        def _(pe):
            def transpose_pair(bank, tile, cols=KB):
                for kb in range(cols):
                    for u in range(2):
                        m = pe.transpose(bank[:, kb * 256 + u * P:kb * 256 + (u + 1) * P],
                                         tile[:, u, kb * P:(kb + 1) * P], ident[:])
                return m

            def project_T(bank, w, col, rhs, blocks=KB):
                for mb in range(2):
                    for kb in range(blocks):
                        lhsT = w[:, kb, col + mb * P:col + (mb + 1) * P] if blocks > 1 else w[:, mb * P:(mb + 1) * P]
                        m = pe.matmul(bank[:, mb * 256:(mb + 1) * 256], lhsT,
                                      rhs[:, kb, :] if blocks > 1 else rhs[:, :],
                                      start=(kb == 0), stop=(kb == blocks - 1))
                return m

            def project(bank, lhs, w, blocks=KB):
                for u in range(2):
                    for kb in range(blocks):
                        lhsT = lhs[:, kb, u * P:(u + 1) * P] if blocks > 1 else lhs[:, u * P:(u + 1) * P]
                        m = pe.matmul(bank[:, u * 256:(u + 1) * 256], lhsT,
                                      w[:, kb, :] if blocks > 1 else w[:, :],
                                      start=(kb == 0), stop=(kb == blocks - 1))
                return m

            pe.wait_ge(consts, 1)
            pe.wait_ge(loaded_w, 16 * W_LOADS)
            for kb in range(KB):
                for mb in range(2):
                    m = pe.transpose(shared_ps[0][:, mb * 256 + kb * P:mb * 256 + (kb + 1) * P],
                                     w_v[:, kb, mb * P:(mb + 1) * P], ident[:])
            m.then_inc(pre_pe, 1)
            pe.wait_ge(pre, 3)
            for mb in range(2):
                for kb in range(KB):
                    m = pe.matmul(shared_ps[1][:, mb * 256:(mb + 1) * 256], w_vT[:, kb, mb * P:(mb + 1) * P],
                                  w_out[:, kb, :], start=(kb == 0), stop=(kb == KB - 1))
            for n, w in ((0, w_out), (1, w_o)):
                for kb in range(KB):
                    m = pe.matmul(shared_ps[2][:, n * 256:(n + 1) * 256], bv_rows[:, n, kb, :], w[:, kb, :],
                                  start=(kb == 0), stop=(kb == KB - 1))
            m.then_inc(pre_pe, 1)
            pe.wait_ge(pre, 6)

            def scores(t, i, q):
                b, bi = t - Q, (i - Q) % 2
                u, g = q // 4, q % 4
                if q == 0:
                    pe.wait_ge(drained["qx"], b + 1)
                    pe.wait_ge(drained["kx"], b + 1)
                wait(pe, exp_done, nth(b, q - 2))
                rows = slice(32 * g, 32 * g + 32)
                for mb in range(2):
                    for par in range(2):
                        n = 2 * mb + par
                        m = pe.matmul(score_ps[q % 2][:, n * P:(n + 1) * P],
                                      qx[bi][rows, mb, par, u * P:(u + 1) * P],
                                      kx[bi][rows, mb, u * P:(u + 1) * P], start=True, stop=True)
                m.then_inc(score_done, 1)

            def turn_probs(t, i, q):
                b = t - Q
                pe.wait_ge(norm_done, nth(b, q))
                wait(pe, probT_out, nth(b, q - 2))
                for n in range(4):
                    m = pe.transpose(probT_ps[q % 2][:, n * P:(n + 1) * P], probs[q % 4][:, n, :], ident[:])
                m.then_inc(probT_done, 1)

            def weigh_values(t, i, u):
                b, bi = t - Q, (i - Q) % 2
                if u == 0:
                    pe.wait_ge(drained["vx"], b + 1)
                    wait(pe, o_out[1], b)
                else:
                    pe.wait_ge(o_out[0], b + 1)
                pe.wait_ge(probT_out, nth(b, 4 * u + 3))
                for mb in range(2):
                    for par in range(2):
                        for g in range(4):
                            m = pe.matmul(o_ps[32 * g:32 * g + 32, (2 * u + mb) * P:(2 * u + mb + 1) * P],
                                          vx[bi][:, u, 4 * mb + g, par, :], probsT[4 * u + g][:, 2 * mb + par, :],
                                          start=(par == 0), stop=(par == 1))
                m.then_inc(o_done[u], 1)

            def tick(t, i):
                a, b, c = t - A, t - B, t - C

                def job(name):
                    bank_free(pe, name, t)
                    return bank_of[name]

                def mlp(j):
                    bank = job(f"gu{j}")
                    for half in range(2):
                        for kb in range(KB):
                            m = pe.matmul(bank[:, half * 256:(half + 1) * 256],
                                          w_gu[:, kb, half * FS + j * P:half * FS + (j + 1) * P],
                                          x2T[:, kb, :], start=(kb == 0), stop=(kb == KB - 1))
                    m.then_inc(done[f"gu{j}"], 1)

                def quarter(turn, score):
                    if on(t, Q):
                        if turn is not None:
                            turn_probs(t, i, turn)
                        if score is not None:
                            scores(t, i, score)

                quarter(None, 0)
                if on(t, A):
                    bank = job("xT")
                    pe.wait_ge(x_loaded[i % 2], half_count(t, i))
                    transpose_pair(bank, x_in[i % 2]).then_inc(done["xT"], 1)
                if on(t, B):
                    bank = job("ctxT")
                    pe.wait_ge(ctx_loaded[(i - B) % 2], half_count(b, i - B))
                    for u in range(2):
                        m = pe.transpose(bank[:, u * P:(u + 1) * P], ctx_sb[(i - B) % 2][:, u, :], ident[:])
                    m.then_inc(done["ctxT"], 1)
                quarter(None, 1)
                if on(t, A):
                    bank = job("q")
                    pe.wait_ge(drained["xT"], a + 1)
                    project_T(bank, w_qk, 0, xT).then_inc(done["q"], 1)
                if on(t, B):
                    bank = job("kx")
                    pe.wait_ge(drained["ctxT"], b + 1)
                    project_T(bank, w_k, 0, ctxT, blocks=1).then_inc(done["kx"], 1)
                quarter(None, 2)
                if on(t, A):
                    bank = job("k")
                    project_T(bank, w_qk, D, xT).then_inc(done["k"], 1)
                quarter(0, 3)
                if on(t, B):
                    bank = job("vx")
                    project(bank, ctxT, w_vx, blocks=1).then_inc(done["vx"], 1)
                if on(t, A):
                    bank = job("v")
                    project(bank, xT, w_vo).then_inc(done["v"], 1)
                quarter(1, 4)
                if on(t, B):
                    bank = job("x1T")
                    pe.wait_ge(x1_done, b + 1)
                    transpose_pair(bank, x1).then_inc(done["x1T"], 1)
                if on(t, A):
                    bank = job("s")
                    pe.wait_ge(drained["q"], a + 1)
                    pe.wait_ge(drained["k"], a + 1)
                    for u in range(2):
                        for mb in range(KB):
                            m = pe.matmul(bank[:, u * P:(u + 1) * P], q_sb[:, mb, u * P:(u + 1) * P],
                                          k_sb[:, mb, u * P:(u + 1) * P], start=(mb == 0), stop=(mb == KB - 1))
                    m.then_inc(done["s"], 1)
                quarter(2, 5)
                if on(t, C):
                    bank = job("x2T")
                    pe.wait_ge(x2_done, c + 1)
                    transpose_pair(bank, x2[(i - C) % 2]).then_inc(done["x2T"], 1)
                quarter(3, 6)
                if on(t, C):
                    bank = job("logits")
                    pe.wait_ge(drained["x2T"], c + 1)
                    for u in range(2):
                        for kb in range(KB):
                            m = pe.matmul(bank[:, u * (E + 1):(u + 1) * (E + 1)], x2T[:, kb, u * P:(u + 1) * P],
                                          w_gate[:, kb, :], start=(kb == 0), stop=(kb == KB - 1))
                    m.then_inc(done["logits"], 1)
                    mlp(0)
                if on(t, B):
                    bank = job("qx")
                    pe.wait_ge(drained["x1T"], b + 1)
                    project_T(bank, w_q, 0, x1T).then_inc(done["qx"], 1)
                quarter(4, 7)
                if on(t, Q):
                    weigh_values(t, i, 0)
                if on(t, C):
                    mlp(1)
                quarter(5, None)
                if on(t, A):
                    bank = job("pT")
                    pe.wait_ge(drained["s"], a + 1)
                    for u in range(2):
                        m = pe.transpose(bank[:, u * P:(u + 1) * P], p_sb[:, u, :], ident[:])
                    m.then_inc(done["pT"], 1)
                if on(t, C):
                    mlp(2)
                quarter(6, None)
                if on(t, C):
                    mlp(3)
                quarter(7, None)
                if on(t, C):
                    bank = job("pos")
                    pe.wait_ge(chosen_done, c + 1)
                    pe.matmul(bank[:, 0:E], before[:], chosen_bf[:, 0, :], start=True, stop=True)
                    pe.matmul(bank[:, E:2 * E], before[:], chosen_bf[:, 1, :], start=True, stop=False)
                    pe.matmul(bank[:, E:2 * E], ones_bf[:], chosen_bf[:, 0, :], start=False, stop=True)
                    pe.matmul(bank[:, 2 * E:3 * E], ones_bf[:], chosen_bf[:, 0, :], start=True, stop=False)
                    pe.matmul(bank[:, 2 * E:3 * E], ones_bf[:], chosen_bf[:, 1, :], start=False, stop=True)\
                        .then_inc(done["pos"], 1)
                if on(t, C):
                    bank = job("dn")
                    pe.wait_ge(drained["gu3"], c + 1)
                    project(bank, h_sb, w_dn, blocks=FB).then_inc(done["dn"], 1)
                if on(t, Q):
                    weigh_values(t, i, 1)
                if on(t, A):
                    bank = job("y")
                    pe.wait_ge(drained["pT"], a + 1)
                    pe.wait_ge(drained["v"], a + 1)
                    for u in range(2):
                        m = pe.matmul(bank[:, u * 256:(u + 1) * 256], pT_sb[:, u, :], v_sb[:, u, :], start=True, stop=True)
                    m.then_inc(done["y"], 1)
                if on(t, Q):
                    bank = job("yx")
                    pe.wait_ge(o_out[1], t - Q + 1)
                    project(bank, oT_sb, w_o).then_inc(done["yx"], 1)

            ticks(pe, tick, C, PEEL, 2, PAIRS)

            for name, _ in SHARED_JOBS[-N_SHARED:]:
                pe.wait_ge(drained[name], PAIRS)

            def expert_tick(t, i):
                if on(t, 0, E):
                    wait(pe, xgT_out, t - 1)
                    pe.wait_ge(expert_loaded[i % (2 * RING)], lap(t, i, 48))
                    for kb in range(KB):
                        m = pe.transpose(score_ps[i % 2][:, kb * P:(kb + 1) * P],
                                         xg[i % (2 * RING)][:, kb * P:(kb + 1) * P], ident[:])
                    m.then_inc(xgT_done, 1)
                if on(t, 1, E):
                    n, k = t - 1, (i - 1)
                    pe.wait_ge(xgT_out, n + 1)
                    wait(pe, eh_done, n - 1)
                    for half in range(2):
                        for kb in range(KB):
                            m = pe.matmul(probT_ps[k % 2][:, half * P:(half + 1) * P],
                                          we_gu[k % (2 * RING)][:, kb, half * P:(half + 1) * P],
                                          xgT[k % 2][:, kb, :], start=(kb == 0), stop=(kb == KB - 1))
                    m.then_inc(egu_done, 1)
                if on(t, 2, E):
                    n, k = t - 2, (i - 2)
                    pe.wait_ge(eh_done, n + 1)
                    wait(pe, ey_done, n - 1)
                    pe.matmul(shared_ps[1 + k % 2][:, 0:D], eh[k % 2][:], we_dn[k % (2 * RING)][:],
                              start=True, stop=True).then_inc(edn_done, 1)

            ticks(pe, expert_tick, 2, 2 * RING, 2 * RING, E)

        @block.scalar
        def _(act):
            COPY, IDENT = ACT.Copy, ACT.Identity
            act.wait_ge(pre_pe, 1)
            act.activation(w_vT[:].rearrange("p k n -> p (k n)"), shared_ps[0][:, :], COPY).then_inc(pre, 1)

            def drain(name, dst, n, cols=512):
                act.wait_ge(done[name], n)
                act.activation(dst, bank_of[name][:, 0:cols], COPY).then_inc(drained[name], 1)

            def tick(t, i):
                a, b, q2, c = t - A, t - B, t - Q, t - C
                flat = "p k n -> p (k n)"

                def exp_quarter(q):
                    act.wait_ge(max_done, nth(q2, q))
                    wait(act, probT_done, nth(q2, q - 4))
                    for n in range(4):
                        m = act.activation(probs[q % 4][:, n, :], score_ps[q % 2][:, n * P:(n + 1) * P], ACT.Exp,
                                           bias=h_nmax[q % 4][:, n:n + 1], accum_out=h_sum[q % 4][:, n:n + 1])
                    m.then_inc(exp_done, 1)

                def drain_quarter(q):
                    act.wait_ge(probT_done, nth(q2, q))
                    wait(act, o_done[q // 4], q2)
                    act.activation(probsT[q].rearrange("p n q -> p (n q)"), probT_ps[q % 2][:, :], COPY)\
                        .then_inc(probT_out, 1)

                def drain_heads(u):
                    act.wait_ge(o_done[u], q2 + 1)
                    wait(act, done["yx"], q2)
                    act.activation(oT_sb[:, :, u * P:(u + 1) * P],
                                   o_ps[:, 2 * u * P:2 * (u + 1) * P].rearrange("p (k n) -> p k n", k=KB), COPY)\
                        .then_inc(o_out[u], 1)

                def tanh_gate(j):
                    act.wait_ge(done[f"gu{j}"], c + 1)
                    if j >= 2:
                        act.wait_ge(drained[f"gu{j - 2}"], c + 1)
                    else:
                        wait(act, drained[f"gu{j + 2}"], c)
                    act.activation(th[j % 2][:], bank_of[f"gu{j}"][:, 0:256], ACT.Tanh, scale=0.5).then_inc(th_done[j], 1)

                def quarter(exp, turned):
                    if on(t, Q):
                        if exp is not None:
                            exp_quarter(exp)
                        if turned is not None:
                            drain_quarter(turned)

                if on(t, A):
                    drain("xT", xT[:].rearrange(flat), a + 1)
                if on(t, B):
                    drain("ctxT", ctxT[:], b + 1, 256)
                quarter(0, None)
                if on(t, A):
                    act.wait_ge(done["q"], a + 1)
                    for mb in range(2):
                        m = act.activation(q_sb[:, mb, :], bank_of["q"][:, mb * 256:(mb + 1) * 256], IDENT,
                                           bias=b_q1[:, mb:mb + 1], scale=SCALE)
                    m.then_inc(drained["q"], 1)
                if on(t, B):
                    act.wait_ge(done["kx"], b + 1)
                    for mb in range(2):
                        m = act.activation(kx[(i - B) % 2][:, mb, :], bank_of["kx"][:, mb * 256:(mb + 1) * 256],
                                           IDENT, bias=b_k[:, mb:mb + 1])
                    m.then_inc(drained["kx"], 1)
                quarter(1, None)
                if on(t, A):
                    act.wait_ge(done["k"], a + 1)
                    for mb in range(2):
                        m = act.activation(k_sb[:, mb, :], bank_of["k"][:, mb * 256:(mb + 1) * 256], IDENT,
                                           bias=b_qk[:, KB + mb:KB + mb + 1])
                    m.then_inc(drained["k"], 1)
                quarter(2, 0)
                if on(t, B):
                    act.wait_ge(done["vx"], b + 1)
                    v = bank_of["vx"][:, :].rearrange("p (u g r d) -> p u g r d", u=2, r=2, d=DH)
                    for par in range(2):
                        for u in range(2):
                            m = act.activation(vx[(i - B) % 2][:, u, :, par, par * DH:(par + 1) * DH], v[:, u, :, par, :], COPY)
                    m.then_inc(drained["vx"], 1)
                if on(t, A):
                    drain("v", v_sb[:].rearrange(flat), a + 1)
                quarter(3, 1)
                if on(t, B):
                    drain("x1T", x1T[:].rearrange(flat), b + 1)
                if on(t, A):
                    act.wait_ge(s_max_done, a + 1)
                    for u in range(2):
                        m = act.activation(p_sb[:, u, :], bank_of["s"][:, u * P:(u + 1) * P], ACT.Exp,
                                           bias=s_nmax[:, u:u + 1], accum_out=s_sum[:, u:u + 1])
                    m.then_inc(drained["s"], 1)
                quarter(4, 2)
                if on(t, C):
                    drain("x2T", x2T[:].rearrange(flat), c + 1)
                quarter(5, 3)
                if on(t, C):
                    tanh_gate(0)
                    act.wait_ge(drained["logits"], c + 1)
                    act.activation(ex[:], lg[:], ACT.Exp).then_inc(ex_done, 1)
                if on(t, B):
                    act.wait_ge(done["qx"], b + 1)
                    for par in range(2):
                        for mb in range(2):
                            m = act.activation(qx[(i - B) % 2][:, mb, par, :], bank_of["qx"][:, mb * 256:(mb + 1) * 256],
                                               IDENT, bias=b_qm[:, par, mb:mb + 1], scale=par_mask[:, par:par + 1])
                    m.then_inc(drained["qx"], 1)
                quarter(6, 4)
                if on(t, Q):
                    drain_heads(0)
                if on(t, C):
                    tanh_gate(1)
                quarter(7, 5)
                if on(t, A):
                    drain("pT", pT_sb[:].rearrange(flat), a + 1, 256)
                if on(t, C):
                    tanh_gate(2)
                quarter(None, 6)
                if on(t, C):
                    tanh_gate(3)
                quarter(None, 7)
                if on(t, Q):
                    drain_heads(1)

            ticks(act, tick, C, PEEL, 2, PAIRS)

            def expert_tick(t, i):
                if on(t, 0, E):
                    act.wait_ge(xgT_done, t + 1)
                    wait(act, egu_done, t - 1)
                    act.activation(xgT[i % 2][:].rearrange("p k n -> p (k n)"), score_ps[i % 2][:, 0:256], COPY)\
                        .then_inc(xgT_out, 1)
                if on(t, 1, E):
                    n, k = t - 1, i - 1
                    act.wait_ge(egu_done, n + 1)
                    wait(act, eh_done, n - 1)
                    act.activation(eth[k % 2][:], probT_ps[k % 2][:, 0:P], ACT.Tanh, scale=0.5).then_inc(eth_done, 1)

            ticks(act, expert_tick, 2, 2 * RING, 2 * RING, E)

            out_tiles = out.rearrange("(n u) p f -> n p u f", u=FT)

            def finish(n, i):
                act.wait_ge(f_nb_done, n + 1)
                for u in range(FT):
                    m = act.activation(f_in[i][:, u, :], f_in[i][:, u, :], ACT.Identity, bias=f_nb[i % 2][:, u:u + 1],
                                       scale=f_rstd[i % 2][:, u:u + 1])
                m.then_inc(f_norm, 1)
                act.wait_ge(f_norm, n + 1)
                act.dma_start(out_tiles[n], f_in[i]).then_inc(f_stored[i], 16)
            with act.Fori(0, F_STEPS // 4) as r:
                for u in range(4):
                    finish(r * 4 + u, u)
            for i in range(4):
                act.wait_ge(f_stored[i], 16 * (F_STEPS // 4))

        @block.vector
        def _(dve):
            dve.wait_ge(loaded_w, 16 * W_LOADS)
            dve.wait_ge(consts, 1)
            for n, b in ((0, b_v), (1, b_vx)):
                for kb in range(KB):
                    m = dve.tensor_scalar(bv_rows[:, n, kb, :], bv_rows[:, n, kb, :], b[:, kb:kb + 1], None, ALU.add)
            m.then_inc(pre, 1)
            for par in range(2):
                dve.tensor_scalar(b_qm[:, par, :], b_q[:], par_mask[:, par:par + 1], None, ALU.mult)
            dve.tensor_scalar(b_q1[:], b_qk[:, 0:KB], SCALE, None, ALU.mult).then_inc(pre, 1)
            dve.wait_ge(pre_pe, 2)
            dve.tensor_copy(w_vo[:].rearrange("p k n -> p (k n)"), shared_ps[1][:, :]).then_inc(pre, 1)
            dve.tensor_tensor(bias_a[:], shared_ps[2][:, 0:D], bout_rows[:, 0, :], ALU.add).then_inc(pre, 1)
            dve.tensor_tensor(bias_x[:], shared_ps[2][:, D:2 * D], bout_rows[:, 1, :], ALU.add).then_inc(pre, 1)

            def tick(t, i):
                a, b, q2, c = t - A, t - B, t - Q, t - C

                def head_max(q):
                    dve.wait_ge(score_done, nth(q2, q))
                    wait(dve, exp_done, nth(q2, q - 4))
                    dve.tensor_reduce(h_nmax[q % 4][:], score_ps[q % 2][:, :].rearrange("p (n k) -> p n k", k=P), AX.X,
                                      ALU.max, negate=True).then_inc(max_done, 1)

                def head_recip(q):
                    dve.wait_ge(exp_done, nth(q2, q))
                    wait(dve, norm_done, nth(q2, q - 4))
                    dve.reciprocal(h_rsum[q % 4][:], h_sum[q % 4][:]).then_inc(recip_done, 1)

                def gated(j):
                    bank = bank_of[f"gu{j}"]
                    dve.wait_ge(th_done[j], c + 1)
                    dve.scalar_tensor_tensor(silu[j % 2][:], th[j % 2][:], 1.0, bank[:, 0:256], ALU.add, ALU.mult)\
                        .then_inc(silu_step, 1)
                    dve.wait_ge(silu_step, c * FB + (j + 1))
                    if j == 0:
                        wait(dve, done["dn"], c)
                    dve.scalar_tensor_tensor(h_sb[:, j, :], silu[j % 2][:], 0.5, bank[:, 256:512], ALU.mult, ALU.mult)\
                        .then_inc(drained[f"gu{j}"], 1)

                def statistics(r, st, mv, st_done, mv_done, n):
                    for u in range(2):
                        m = dve.bn_stats(st[:, u, :], r[:, u, :])
                    m.then_inc(st_done, 1)
                    dve.wait_ge(st_done, n + 1)
                    carry_wait(dve)
                    for u in range(2):
                        m = dve.bn_aggr(mv[:, u, :], st[:, u, :])
                    m.then_inc(mv_done, 1)

                def normalise(r, mv, rstd, dst, rstd_done, dst_done, n):
                    dve.wait_ge(rstd_done, n + 1)
                    for u in range(2):
                        m = dve.tensor_scalar(dst[:, u, 0:D], r[:, u, :], mv[:, u, 0:1], rstd[:, u:u + 1],
                                              ALU.subtract, ALU.mult)
                    m.then_inc(dst_done, 1)

                GATE = 10

                def router():
                    n = c * GATE
                    bank = bank_of["logits"][:, 0:2 * (E + 1)].rearrange("p (u e) -> p u e", u=2)

                    def per_seq(col):
                        return col[:].unsqueeze(2).to_broadcast([P, 2, E])
                    dve.wait_ge(done["logits"], c + 1)
                    dve.tensor_reduce(lg_max[:], bank[:, :, 0:E], AX.X, ALU.max).then_inc(gate_step, 1)
                    dve.wait_ge(gate_step, n + 1)
                    dve.tensor_scalar(lg[:, :, E:E + 1], bank[:, :, E:E + 1], -1.0, None, ALU.mult)
                    dve.tensor_tensor(lg[:, :, 0:E], bank[:, :, 0:E], per_seq(lg_max), ALU.subtract).then_inc(drained["logits"], 1)

                def router_weights():
                    n = c * GATE + 1

                    def per_seq(col):
                        return col[:].unsqueeze(2).to_broadcast([P, 2, E])
                    dve.wait_ge(ex_done, c + 1)
                    dve.tensor_reduce(z_sum[:], ex[:, :, 0:E], AX.X, ALU.add).then_inc(gate_step, 1)
                    dve.tensor_scalar(sg1[:], ex[:, :, E], 1.0, None, ALU.add).then_inc(gate_step, 1)
                    dve.wait_ge(gate_step, n + 2)
                    dve.reciprocal(z_rsum[:], z_sum[:]).then_inc(gate_step, 1)
                    dve.wait_ge(gate_step, n + 3)
                    dve.tensor_tensor(prob[:], ex[:, :, 0:E], per_seq(z_rsum), ALU.mult).then_inc(gate_step, 1)
                    dve.wait_ge(gate_step, n + 4)
                    dve.reciprocal(sg[:], sg1[:]).then_inc(sg_done, 1)
                    for u in range(2):
                        m = dve.max(top[:, u, :], prob[:, u, :])
                    m.then_inc(gate_step, 1)
                    dve.wait_ge(gate_step, n + 5)
                    dve.tensor_reduce(top_sum[:], top[:], AX.X, ALU.add).then_inc(gate_step, 1)
                    for u in range(2):
                        m = dve.match_replace(out=marked[:, u, :], in_to_replace=top[:, u, :], in_values=prob[:, u, :], imm_value=-1.0)
                    m.then_inc(gate_step, 1)
                    dve.wait_ge(gate_step, n + 7)
                    wait(dve, scattered[(i - C) % 2], half_count(c, i - C, 2 * TOP_K * 16) - 2 * TOP_K * 16)
                    row = send[(i - C) % 2]
                    dve.tensor_copy(row[:, :, 0:D], x2[(i - C) % 2][:])
                    dve.tensor_scalar(row[:, :, ROW - 1:ROW], row[:, :, ROW - 1:ROW], float(4 * P), None, ALU.add)
                    dve.tensor_scalar(chosen[:], marked[:], 0.0, None, ALU.is_lt).then_inc(gate_step, 1)
                    wait(dve, done["pos"], c)
                    dve.tensor_scalar(chosen_bf[:], marked[:], 0.0, None, ALU.is_lt).then_inc(chosen_done, 1)
                    dve.wait_ge(gate_step, n + 8)
                    dve.reciprocal(top_rsum[:], top_sum[:]).then_inc(gate_step, 1)
                    dve.wait_ge(gate_step, n + 9)
                    for u in range(2):
                        m = dve.scalar_tensor_tensor(row[:, u, D:D + E], prob[:, u, :], top_rsum[:, u:u + 1],
                                                     chosen[:, u, :], ALU.mult, ALU.mult)

                PLACE = 5

                def places():
                    n = c * PLACE
                    bank = bank_of["pos"]
                    cnt = count[:].unsqueeze(1).to_broadcast([P, 2, E])
                    dve.wait_ge(done["pos"], c + 1)
                    wait(dve, drained["pos"], c)
                    dve.tensor_tensor(place[:], bank[:, 0:2 * E].rearrange("p (u e) -> p u e", u=2), cnt, ALU.add)\
                        .then_inc(place_step, 1)
                    dve.wait_ge(place_step, n + 1)
                    dve.scalar_tensor_tensor(kept[:], place[:], float(CAPACITY), chosen[:], ALU.is_lt, ALU.mult)\
                        .then_inc(place_step, 1)
                    dve.tensor_tensor(slot_key[:], slot_base[:].unsqueeze(1).to_broadcast([P, 2, E]), place[:],
                                      ALU.subtract).then_inc(place_step, 1)
                    dve.wait_ge(place_step, n + 3)
                    dve.tensor_tensor(key[:], slot_key[:], kept[:], ALU.mult).then_inc(place_step, 1)
                    dve.wait_ge(place_step, n + 4)
                    dve.tensor_tensor(count[:], bank[:, 2 * E:3 * E], count[:], ALU.add).then_inc(drained["pos"], 1)
                    for u in range(2):
                        m = dve.max(key8[:, u, :], key[:, u, :])
                    m.then_inc(place_step, 1)
                    dve.wait_ge(place_step, n + 5)
                    dve.tensor_scalar(slot_no[(i - C) % 2][:], key8[:], -1.0, float(T), ALU.mult, ALU.add).then_inc(slot_done, 1)

                def quarter(recip, top):
                    if on(t, Q):
                        if recip is not None:
                            head_recip(recip)
                        if top is not None:
                            head_max(top)

                quarter(None, 0)
                if on(t, B):
                    wait(dve, done["x1T"], b)
                    wait(dve, x1b_done, b)
                    normalise(r1, mv1, rstd1, x1, rstd1_done, x1_done, b)
                quarter(None, 1)
                if on(t, C):
                    wait(dve, done["x2T"], c - 1)
                    normalise(r2, mv2, rstd2, x2[(i - C) % 2], rstd2_done, x2_done, c)
                quarter(0, 2)
                quarter(1, 3)
                quarter(2, 4)
                if on(t, A):
                    dve.wait_ge(done["s"], a + 1)
                    dve.tensor_reduce(s_nmax[:], bank_of["s"][:, 0:256].rearrange("p (u k) -> p u k", u=2), AX.X,
                                      ALU.max, negate=True).then_inc(s_max_done, 1)
                quarter(3, 5)
                quarter(4, 6)
                if on(t, C):
                    router()
                    gated(0)
                quarter(5, 7)
                if on(t, C):
                    router_weights()
                    gated(1)
                quarter(6, None)
                if on(t, C):
                    gated(2)
                quarter(7, None)
                if on(t, C):
                    gated(3)
                    places()
                if on(t, C):
                    dve.wait_ge(done["dn"], c + 1)
                    wait(dve, resid_stored[(i - C) % 2], half_count(c, i - C, RESID_STORES * 16) - RESID_STORES * 16)
                    dve.wait_ge(sg_done, c + 1)
                    for u in range(2):
                        m = dve.scalar_tensor_tensor(z_sb[(i - C) % 2][:, u, :], bank_of["dn"][:, u * D:(u + 1) * D],
                                                     sg[:, u:u + 1], x2[(i - C) % 2][:, u, 0:D], ALU.mult, ALU.add)
                    m.then_inc(drained["dn"], 1)
                if on(t, A):
                    dve.wait_ge(drained["s"], a + 1)
                    dve.reciprocal(s_rsum[:], s_sum[:]).then_inc(s_rsum_done, 1)
                    dve.wait_ge(done["y"], a + 1)
                    dve.wait_ge(s_rsum_done, a + 1)
                    dve.wait_ge(xb_done, a + 1)
                    for u in range(2):
                        m = dve.scalar_tensor_tensor(r1[:, u, :], bank_of["y"][:, u * D:(u + 1) * D], s_rsum[:, u:u + 1],
                                                     xb[:, u, :], ALU.mult, ALU.add)
                    m.then_inc(drained["y"], 1)
                    dve.wait_ge(drained["y"], a + 1)
                    statistics(r1, st1, mv1, st1_done, mv1_done, a)
                if on(t, Q):
                    dve.wait_ge(done["yx"], q2 + 1)
                    dve.tensor_tensor(r2[:].rearrange("p u d -> p (u d)"), bank_of["yx"][:, :],
                                      x1b[(i - Q) % 2][:].rearrange("p u d -> p (u d)"), ALU.add).then_inc(drained["yx"], 1)
                    dve.wait_ge(drained["yx"], q2 + 1)
                    statistics(r2, st2, mv2, st2_done, mv2_done, q2)

            ticks(dve, tick, C, PEEL, 2, PAIRS)

            def expert_tick(t, i):
                if on(t, 1, E):
                    n, k = t - 1, i - 1
                    bank = probT_ps[k % 2]
                    dve.wait_ge(eth_done, n + 1)
                    dve.scalar_tensor_tensor(esilu[k % 2][:], eth[k % 2][:], 1.0, bank[:, 0:P], ALU.add, ALU.mult).then_inc(estep, 1)
                    dve.wait_ge(estep, n + 1)
                    wait(dve, edn_done, n - 1)
                    dve.scalar_tensor_tensor(eh[k % 2][:], esilu[k % 2][:], 0.5, bank[:, P:2 * P], ALU.mult, ALU.mult)\
                        .then_inc(eh_done, 1)
                if on(t, 2, E):
                    n, k = t - 2, (i - 2) % (2 * RING)
                    wait(dve, added[k % 2], half_count(n, k) - RING * 16)
                    dve.wait_ge(edn_done, n + 1)
                    dve.tensor_copy(ids[k][:], xg[k][:, ROW - 1:ROW])
                    dve.tensor_scalar(ey[k][:], shared_ps[1 + k % 2][:, 0:D], xg[k][:, column(n + D)], None,
                                      ALU.mult).then_inc(ey_done, 1)

            ticks(dve, expert_tick, 2, 2 * RING, 2 * RING, E)

            def final(t, i):
                if on(t, 0, F_STEPS):
                    dve.wait_ge(f_sum, t + 1)
                    for u in range(FT):
                        m = dve.bn_stats(f_st[i % 2][:, u, :], f_in[i % 4][:, u, :])
                    m.then_inc(f_st_done, 1)
                    dve.wait_ge(f_st_done, t + 1)
                    carry_wait(dve)
                    for u in range(FT):
                        m = dve.bn_aggr(f_mv[i % 2][:, u, :], f_st[i % 2][:, u, :])
                    m.then_inc(f_mv_done, 1)
                    k = i % 2
                    dve.wait_ge(f_rstd_done, t + 1)
                    wait(dve, f_norm, t - 1)
                    dve.scalar_tensor_tensor(f_nb[k][:], f_mv[k][:, :, 0], -1.0, f_rstd[k][:], ALU.mult, ALU.mult)\
                        .then_inc(f_nb_done, 1)
            ticks(dve, final, 0, 4, 4, F_STEPS)

        @block.gpsimd
        def _(pool):
            steps = 0

            def step(instruction):
                nonlocal steps
                steps += 1
                instruction.then_inc(pool_step, 1)
                pool.wait_ge(pool_step, steps)

            step(pool.memset(ident[:], 0.0))
            step(pool.affine_select(out=ident[:], in_=ident[:], compare_op=ALU.not_equal, fill=1.0, base=0,
                                    pattern=[[-1, P]], channel_multiplier=1))
            step(pool.memset(before[:], 1.0))
            step(pool.affine_select(out=before[:], in_=before[:], compare_op=ALU.is_gt, fill=0.0, base=0,
                                    pattern=[[1, P]], channel_multiplier=-1))
            step(pool.iota(row_no[:], pattern=[[0, 1]], base=0, channel_multiplier=1))
            step(pool.tensor_copy(row_f[:], row_no[:]))
            step(pool.memset(par_mask[:], 0.0))
            for g in range(1, P // DH):
                step(pool.tensor_scalar(row_ge[:], row_f[:], float(DH * g), 1.0 if g % 2 else -1.0, ALU.is_ge, ALU.mult))
                step(pool.tensor_tensor(par_mask[:, 1:2], par_mask[:, 1:2], row_ge[:], ALU.add))
            step(pool.tensor_scalar(par_mask[:, 0:1], par_mask[:, 1:2], -SCALE, SCALE, ALU.mult, ALU.add))
            step(pool.tensor_scalar(par_mask[:, 1:2], par_mask[:, 1:2], SCALE, None, ALU.mult))
            step(pool.memset(bv_rows[:], 0.0))
            step(pool.memset(spare_rows[:], 0.0))
            step(pool.tensor_scalar(spare_rows[:, ROW - 1:ROW], row_f[:], float(T), None, ALU.add))
            for i in range(2):
                for u in range(2):
                    step(pool.tensor_scalar(send[i][:, u, ROW - 1:ROW], row_f[:], float((2 * i + u) * P - 4 * P), None, ALU.add))
            step(pool.memset(zero_pair[:], 0.0))
            step(pool.memset(ones_bf[:], 1.0))
            step(pool.memset(neg_half[:], -0.5))
            step(pool.memset(f_nh[:], -0.5))
            step(pool.memset(eps_col[:], EPS))
            step(pool.memset(count[:], 0.0))
            for v in vx:
                step(pool.memset(v[:], 0.0))
            step(pool.iota(base_i[:], pattern=[[-CAPACITY, E]], base=T, channel_multiplier=0))
            pool.tensor_copy(slot_base[:], base_i[:]).then_inc(consts, 1)
            slot_bound = pool.to_reg(E * CAPACITY - 1)
            row_bound = pool.to_reg(T + CAPACITY - 1)
            pool.wait_ge(pre, 6)

            def tick(t, i):
                a, b, q2, c = t - A, t - B, t - Q, t - C
                if on(t, A):
                    pool.wait_ge(x_loaded[i % 2], half_count(t, i))
                    wait(pool, drained["y"], a)
                    pool.tensor_tensor(xb[:], x_in[i % 2][:], bias_a[:].unsqueeze(1).to_broadcast([P, 2, D]), ALU.add)\
                        .then_inc(xb_done, 1)
                if on(t, B):
                    pool.wait_ge(x1_done, b + 1)
                    wait(pool, drained["yx"], b - 1)
                    pool.tensor_tensor(x1b[(i - B) % 2][:], x1[:], bias_x[:].unsqueeze(1).to_broadcast([P, 2, D]), ALU.add)\
                        .then_inc(x1b_done, 1)

                def scatter(ci, k):
                    for u in range(2):
                        pool.indirect_dma_start(slot_table[:, :], bass.IndirectOffsetOnAxis(ap=slot_no[ci % 2][:, u, k:k + 1], axis=0),
                                                send[ci % 2][:, u, :], None, bounds_check=slot_bound,
                                                oob_is_err=False).then_inc(scattered[ci % 2], 16)

                def normalise_quarter(q):
                    pool.wait_ge(recip_done, nth(q2, q))
                    pool.tensor_tensor(probs[q % 4][:], probs[q % 4][:],
                                       h_rsum[q % 4][:].unsqueeze(2).to_broadcast([P, 4, P]), ALU.mult).then_inc(norm_done, 1)

                if on(t, C + 1):
                    if isinstance(t, int) and t == C + 1:
                        pool.wait_ge(slots_filled, 16 * FILLS)
                    pool.wait_ge(slot_done, c)
                    carry_wait(pool)
                for k in range(TOP_K):
                    if on(t, Q):
                        normalise_quarter(k)
                    if on(t, C + 1):
                        scatter(i - C - 1, k)

                def rstd(mv, ve, r, mv_done, ve_done, rstd_done, n):
                    pool.wait_ge(mv_done, n + 1)
                    pool.tensor_tensor(ve[:], mv[:, :, 1], eps_col[:, 0:2], ALU.add).then_inc(ve_done, 1)
                    pool.wait_ge(ve_done, n + 1)
                    pool.tensor_tensor(r[:], ve[:], neg_half[:], ALU.pow).then_inc(rstd_done, 1)
                if on(t, A):
                    rstd(mv1, ve1, rstd1, mv1_done, ve1_done, rstd1_done, a)
                if on(t, Q):
                    rstd(mv2, ve2, rstd2, mv2_done, ve2_done, rstd2_done, q2)

            ticks(pool, tick, C + 1, PEEL, 2, PAIRS)

            for i in range(2):
                pool.wait_ge(resid_stored[i], PAIRS // 2 * RESID_STORES * 16)
            pool.wait_ge(tables_set, 32)

            def expert_tick(t, i):
                if on(t, 2, E):
                    n, k = t - 2, (i - 2) % (2 * RING)
                    pool.wait_ge(ey_done, n + 1)
                    wait(pool, added[k % 2], half_count(n, k) - 16)
                    carry_wait(pool)
                    pool.indirect_dma_start((resid_table, resid_table2)[k % 2][:, :],
                                            bass.IndirectOffsetOnAxis(ap=ids[k][:], axis=0),
                                            ey[k][:], None, bounds_check=row_bound,
                                            compute_op=ALU.add).then_inc(added[k % 2], 16)

            ticks(pool, expert_tick, 2, 2 * RING, 2 * RING, E)

            def final(t, i):
                if on(t, 0, F_STEPS):
                    k = i % 4
                    pool.wait_ge(f_loaded[k], lap(t, i, 32, 4))
                    pool.tensor_tensor(f_in[k], f_in[k], f_in2[k], ALU.add).then_inc(f_sum, 1)
                if on(t, 1, F_STEPS):
                    k = (i - 1) % 2
                    pool.wait_ge(f_mv_done, t)
                    pool.tensor_tensor(f_ve[k][:], f_mv[k][:, :, 1], eps_col[:], ALU.add).then_inc(f_ve_done, 1)
                    pool.wait_ge(f_ve_done, t)
                    wait(pool, f_norm, t - 2)
                    pool.tensor_tensor(f_rstd[k][:], f_ve[k][:], f_nh[:], ALU.pow).then_inc(f_rstd_done, 1)
            ticks(pool, final, 1, 4, 4, F_STEPS)


_INS = ['x', 'ctx_512', 'L0_attn_W_qkv', 'L0_attn_b_qkv', 'L0_attn_W_out', 'L0_attn_b_out', 'L0_xattn_Wq', 'L0_xattn_bq',
        'L0_xattn_Wk', 'L0_xattn_bk', 'L0_xattn_Wv', 'L0_xattn_bv', 'L0_xattn_Wo', 'L0_xattn_bo', 'L0_ffn_gate_w',
        'L0_ffn_shared_gate_w', 'L0_ffn_shared_gate_up_w', 'L0_ffn_shared_down_w', 'L0_ffn_expert_gate_up_w',
        'L0_ffn_expert_down_w']
_OUTS = [((64, 128, 256), 'float32')]


def kernel(**inputs):
    import numpy as _np
    import concourse.bacc as _bacc
    from concourse import mybir as _mybir
    from concourse.bass_utils import run_bass_kernel_spmd as _run

    nc = _bacc.Bacc("TRN2", target_bir_lowering=False, num_devices=1)
    arrays, args = {}, []
    for name in _INS:
        a = _np.ascontiguousarray(inputs[name])
        arrays[f"in_{name}_dram"] = a
        args.append(nc.dram_tensor(f"in_{name}_dram", a.shape, _mybir.dt.from_np(a.dtype), kind="ExternalInput").ap())
    for i, (shape, dtype) in enumerate(_OUTS):
        dt = _mybir.dt.from_np(_np.dtype(dtype))
        args.append(nc.dram_tensor(f"out_{i}_dram", shape, dt, kind="ExternalOutput").ap())
    decoder_layer(nc, *args)
    r = _run(nc, [arrays], core_ids=[0])
    return r.results[0]["out_0_dram"]
```

```python
from contextlib import ExitStack

import concourse.bass as bass
from concourse import mybir

F32 = mybir.dt.float32
BF16 = mybir.dt.bfloat16
I32 = mybir.dt.int32
U32 = mybir.dt.uint32
ALU = mybir.AluOpType
ACT = mybir.ActivationFunctionType
AX = mybir.AxisListType

P = 128
EPS = 1e-5
TOP_K = 8
CAPACITY = 128
HEADS = 16
A, B, Q, C = 0, 1, 2, 3
PEEL = 6
QUARTERS = 8

SHARED_JOBS = [("xT", A), ("ctxT", B), ("q", A), ("kx", B), ("k", A), ("vx", B),
               ("x1T", B), ("s", A), ("x2T", C), ("v", A), ("logits", C), ("gu0", C), ("qx", B), ("gu1", C),
               ("pT", A), ("gu2", C), ("gu3", C), ("pos", C), ("y", A), ("dn", C), ("yx", Q)]
N_SHARED = 3
assert len(SHARED_JOBS) % N_SHARED == 0


def decoder_layer(nc, x, ctx_in, W_qkv, b_qkv, W_out, b_out, Wq, bq, Wk, bk, Wv, bv, Wo, bo,
                  gate_w, shared_gate_w, shared_gate_up_w, shared_down_w,
                  expert_gate_up_w, expert_down_w, out):
    NSEQ, S, D = x.shape
    DC = ctx_in.shape[2]
    T = NSEQ * S
    PAIRS = NSEQ // 2
    E = gate_w.shape[1]
    FS = shared_down_w.shape[0]
    FB = FS // P
    DH = D // HEADS
    KB = D // P
    SCALE = 1.0 / DH ** 0.5
    ROW = D + E + 1
    assert S == P and D == 2 * P and DC == P and FB == 4 and E == 64 and PAIRS > PEEL
    assert expert_down_w.shape[1] == P

    x_pairs = x.rearrange("(n u) p d -> n p u d", u=2)
    ctx_pairs = ctx_in.rearrange("(n u) p d -> n p u d", u=2)

    slot_table = nc.dram_tensor("slot_table", [E * CAPACITY, ROW], F32, kind="Internal")
    slots_by_expert = slot_table[:, :].rearrange("(e c) f -> e c f", c=CAPACITY)
    slots_by_place = slot_table[:, :].rearrange("(e c) f -> c e f", c=CAPACITY)
    resid_table = nc.dram_tensor("resid_table", [T + CAPACITY, D], F32, kind="Internal")
    resid_table2 = nc.dram_tensor("resid_table2", [T + CAPACITY, D], F32, kind="Internal")
    resid_pairs = resid_table[0:T, :].rearrange("(n u p) f -> n p u f", u=2, p=P)
    resid_pairs2 = resid_table2[0:T, :].rearrange("(n u p) f -> n p u f", u=2, p=P)

    es = ExitStack()
    with es:
        def sb(name, shape, dt=F32):
            return es.enter_context(nc.sbuf_tensor(name, shape, dt))

        def psum(name):
            return es.enter_context(nc.psum_tensor(name, [P, 512], F32))

        def sem(name):
            return es.enter_context(nc.semaphore(name))

        RING = 4
        FIRST = 2 * RING
        ident = sb("ident", [P, P])
        before = sb("before", [P, P], BF16)
        ones_bf = sb("ones_bf", [P, P], BF16)
        par_mask = sb("par_mask", [P, 2])
        eps_col = sb("eps_col", [P, 4])
        neg_half = sb("neg_half", [P, 2])
        slot_base = sb("slot_base", [P, E])
        base_i = sb("base_i", [P, E], I32)
        row_no = sb("row_no", [P, 1], I32)
        row_f = sb("row_f", [P, 1])
        row_ge = sb("row_ge", [P, 1])
        spare_rows = sb("spare_rows", [P, ROW])
        zero_pair = sb("zero_pair", [P, 2, D])
        w_qk = sb("w_qk", [P, KB, 2 * D])
        w_v = sb("w_v", [P, KB, D])
        w_vT = sb("w_vT", [P, KB, D])
        w_out = sb("w_out", [P, KB, D])
        w_vo = sb("w_vo", [P, KB, D])
        w_q = sb("w_q", [P, KB, D])
        w_k = sb("w_k", [P, D])
        w_vx = sb("w_vx", [P, D])
        w_o = sb("w_o", [P, KB, D])
        w_gate = sb("w_gate", [P, KB, E + 1])
        w_gu = sb("w_gu", [P, KB, 2 * FS])
        w_dn = sb("w_dn", [P, FB, D])
        b_qk = sb("b_qk", [P, 4])
        b_v = sb("b_v", [P, KB])
        b_q = sb("b_q", [P, KB])
        b_q1 = sb("b_q1", [P, KB])
        b_qm = sb("b_qm", [P, 2, KB])
        b_k = sb("b_k", [P, KB])
        b_vx = sb("b_vx", [P, KB])
        bv_rows = sb("bv_rows", [P, 2, KB, P])
        bias_a = sb("bias_a", [P, D])
        bias_x = sb("bias_x", [P, D])
        bout_rows = sb("bout_rows", [P, 2, D])
        x_in = [sb(f"x_in{i}", [P, 2, D]) for i in range(2)]
        ctx_sb = [sb(f"ctx_sb{i}", [P, 2, DC]) for i in range(2)]
        xT = sb("xT", [P, KB, 256])
        q_sb = sb("q_sb", [P, KB, 256])
        k_sb = sb("k_sb", [P, KB, 256])
        v_sb = sb("v_sb", [P, 2, D])
        xb = sb("xb", [P, 2, D])
        s_nmax = sb("s_nmax", [P, 2])
        s_sum = sb("s_sum", [P, 2])
        s_rsum = sb("s_rsum", [P, 2])
        p_sb = sb("p_sb", [P, 2, P])
        pT_sb = sb("pT_sb", [P, 2, P])
        r1 = sb("r1", [P, 2, D])
        st1 = sb("st1", [P, 2, 6])
        mv1 = sb("mv1", [P, 2, 2])
        ve1 = sb("ve1", [P, 2])
        rstd1 = sb("rstd1", [P, 2])
        x1 = sb("x1", [P, 2, D])
        x1b = [sb(f"x1b{i}", [P, 2, D]) for i in range(2)]
        x1T = sb("x1T", [P, KB, 256])
        ctxT = sb("ctxT", [P, 256])
        qx = [sb(f"qx{i}", [P, KB, 2, 256]) for i in range(2)]
        kx = [sb(f"kx{i}", [P, KB, 256]) for i in range(2)]
        vx = [sb(f"vx{i}", [P, 2, HEADS // 2, 2, 2 * DH]) for i in range(2)]
        h_nmax = [sb(f"h_nmax{i}", [P, 4]) for i in range(4)]
        h_sum = [sb(f"h_sum{i}", [P, 4]) for i in range(4)]
        h_rsum = [sb(f"h_rsum{i}", [P, 4]) for i in range(4)]
        probs = [sb(f"probs{i}", [P, 4, P]) for i in range(4)]
        probsT_all = sb("probsT_all", [P, QUARTERS, 4, P])
        probsT = [probsT_all[:, i] for i in range(QUARTERS)]
        oT_sb = sb("oT_sb", [P, KB, 256])
        r2 = sb("r2", [P, 2, D])
        st2 = sb("st2", [P, 2, 6])
        mv2 = sb("mv2", [P, 2, 2])
        ve2 = sb("ve2", [P, 2])
        rstd2 = sb("rstd2", [P, 2])
        x2 = [sb(f"x2_{i}", [P, 2, D]) for i in range(2)]
        x2T = sb("x2T", [P, KB, 256])
        lg_max = sb("lg_max", [P, 2])
        lg = sb("lg", [P, 2, E + 1])
        ex = sb("ex", [P, 2, E + 1])
        z_sum = sb("z_sum", [P, 2])
        z_rsum = sb("z_rsum", [P, 2])
        sg1 = sb("sg1", [P, 2])
        sg = sb("sg", [P, 2])
        prob = sb("prob", [P, 2, E])
        top = sb("top", [P, 2, TOP_K])
        marked = sb("marked", [P, 2, E])
        chosen = sb("chosen", [P, 2, E])
        chosen_bf = sb("chosen_bf", [P, 2, E], BF16)
        top_sum = sb("top_sum", [P, 2])
        top_rsum = sb("top_rsum", [P, 2])
        count = sb("count", [P, E])
        place = sb("place", [P, 2, E])
        kept = sb("kept", [P, 2, E])
        slot_key = sb("slot_key", [P, 2, E])
        key = sb("key", [P, 2, E])
        key8 = sb("key8", [P, 2, TOP_K])
        slot_no = [sb(f"slot_no{i}", [P, 2, TOP_K], U32) for i in range(2)]
        send = [sb(f"send{i}", [P, 2, ROW]) for i in range(2)]
        th = [sb(f"th{i}", [P, 256]) for i in range(2)]
        silu = [sb(f"silu{i}", [P, 256]) for i in range(2)]
        h_sb = sb("h_sb", [P, FB, 256])
        z_sb = [sb(f"z_sb{i}", [P, 2, D]) for i in range(2)]
        ids = [sb(f"ids{i}", [P, 1], U32) for i in range(2 * RING)]
        xg = [sb(f"xg{i}", [P, ROW]) for i in range(2 * RING)]
        we_gu_first = [w[:] for w in (w_v, w_vT, w_out, bout_rows)]
        we_gu_first += [bv_rows[:].rearrange("p n k m -> p (n k m)").rearrange("p (k f) -> p k f", k=KB)]
        we_gu_first += [sb(f"we_gu_first{i}", [P, KB, 2 * P])[:] for i in range(5, FIRST)]
        we_dn_first = [sb(f"we_dn_first{i}", [P, D])[:] for i in range(FIRST)]
        we_gu = [sb(f"we_gu{i}", [P, KB, 2 * P])[:] for i in range(2 * RING)]
        we_dn = [sb(f"we_dn{i}", [P, D])[:] for i in range(2 * RING)]
        we_gu += [probsT_all[:, i].rearrange("p n q -> p (n q)").rearrange("p (k f) -> p k f", k=KB) for i in range(2 * RING)]
        we_dn += [w_qk[:, kb, half * D:(half + 1) * D] for kb in range(KB) for half in range(2)]
        we_dn += [buffer[:, kb, :] for buffer in (q_sb, k_sb) for kb in range(KB)]
        xgT = [sb(f"xgT{i}", [P, KB, P]) for i in range(2)]
        eth = [sb(f"eth{i}", [P, P]) for i in range(2)]
        esilu = [sb(f"esilu{i}", [P, P]) for i in range(2)]
        eh = [sb(f"eh{i}", [P, P]) for i in range(2)]
        ey = [v[:].rearrange("p u g r d -> p (u g r d)")[:, j * D:(j + 1) * D] for v in vx for j in range(RING)]
        FT = 4
        f_in = [buffer[:] for buffer in (sb("f_in0", [P, FT, D]), h_sb, w_dn)]
        f_in += [w_gu[:, i].rearrange("p (t d) -> p t d", t=FT) for i in range(KB)]
        f_in += [w_qk[:].rearrange("p k (t d) -> p (k t) d", t=2)]
        f_in += [buffer[:].rearrange("p k r n -> p (k r) n") for buffer in qx]
        F_RING = len(f_in)
        f_in2 = [probsT_all[:, 2 * i:2 * i + 2].rearrange("p a n q -> p (a n q)")
                 .rearrange("p (t d) -> p t d", t=FT) for i in range(4)]
        f_nb = [sb(f"f_nb{i}", [P, FT]) for i in range(2)]
        f_st = [sb(f"f_st{i}", [P, FT, 6]) for i in range(2)]
        f_mv = [sb(f"f_mv{i}", [P, FT, 2]) for i in range(2)]
        f_ve = [sb(f"f_ve{i}", [P, FT]) for i in range(2)]
        f_rstd = [sb(f"f_rstd{i}", [P, FT]) for i in range(2)]
        f_nh = sb("f_nh", [P, FT])

        score_ps = [psum(f"score_ps{i}") for i in range(2)]
        probT_ps = [psum(f"probT_ps{i}") for i in range(2)]
        o_ps = psum("o_ps")
        shared_ps = [psum(f"shared_ps{i}") for i in range(N_SHARED)]
        bank_of = {job: shared_ps[i % N_SHARED] for i, (job, _) in enumerate(SHARED_JOBS)}

        done = {job: sem(f"{job}_done") for job, _ in SHARED_JOBS}
        drained = {job: sem(f"{job}_out") for job, _ in SHARED_JOBS}
        score_done = sem("score_done")
        max_done = sem("max_done")
        exp_done = sem("exp_done")
        probT_done = sem("probT_done")
        probT_out = sem("probT_out")
        recip_done, norm_done = sem("recip_done"), sem("norm_done")
        o_done = [sem(f"o_done{u}") for u in range(2)]
        o_out = [sem(f"o_out{u}") for u in range(2)]
        first_consts, consts = sem("first_consts"), sem("consts")
        carried = [sem("carried_pool"), sem("carried_vector")]
        pool_step = sem("pool_step")
        loaded_w = [sem(f"loaded_w{group}") for group in range(3)]
        tables_set = sem("tables_set")
        pre = sem("pre")
        bv_rows_done, w_vT_done = sem("bv_rows_done"), sem("w_vT_done")
        pre_pe = sem("pre_pe")
        x_loaded = [sem(f"x_loaded{i}") for i in range(2)]
        ctx_loaded = [sem(f"ctx_loaded{i}") for i in range(2)]
        xb_done, x1b_done = sem("xb_done"), sem("x1b_done")
        s_max_done = sem("s_max_done")
        ve1_done, rstd1_done, ve2_done, rstd2_done = (sem(n) for n in ("ve1_done", "rstd1_done", "ve2_done", "rstd2_done"))
        s_rsum_done, st1_done, mv1_done, x1_done = (sem(n) for n in ("s_rsum_done", "st1_done", "mv1_done", "x1_done"))
        st2_done, mv2_done, x2_done = (sem(n) for n in ("st2_done", "mv2_done", "x2_done"))
        ex_done = sem("ex_done")
        gate_step = sem("gate_step")
        chosen_done, sg_done = (sem(n) for n in ("chosen_done", "sg_done"))
        place_step, slot_done = sem("place_step"), sem("slot_done")
        th_done = [sem(f"th_done{j}") for j in range(FB)]
        silu_step = sem("silu_step")
        resid_stored = [sem(f"resid_stored{i}") for i in range(2)]
        scattered = [sem(f"scattered{i}") for i in range(2)]
        slots_loaded = [sem(f"slots_loaded{i}") for i in range(2 * RING)]
        we_first_loaded = sem("we_first_loaded")
        we_loaded = [sem(f"we_loaded{i}") for i in range(4 * RING)]
        xgT_done, xgT_out = sem("xgT_done"), sem("xgT_out")
        egu_done, eth_done, estep, eh_done = sem("egu_done"), sem("eth_done"), sem("estep"), sem("eh_done")
        edn_done, ey_done = sem("edn_done"), sem("ey_done")
        added = [sem(f"added{i}") for i in range(2)]
        f_loaded = [sem(f"f_loaded{i}") for i in range(F_RING)]
        f_sum, f_st_done, f_mv_done, f_ve_done, f_rstd_done, f_nb_done, f_norm = (
            sem(n) for n in ("f_sum", "f_st_done", "f_mv_done", "f_ve_done", "f_rstd_done", "f_nb_done", "f_norm"))
        f_stored = [sem(f"f_stored{i}") for i in range(F_RING)]

        def wait(eng, s, n):
            if not isinstance(n, int) or n > 0:
                eng.wait_ge(s, n)

        def carry_wait(eng):
            eng.sem_inc(carried[eng is nc.vector], 1)

        def ticks(eng, tick, lags, peel, unroll, total):
            for t in range(peel):
                tick(t, t)
            with eng.Fori(peel // unroll, total // unroll) as r:
                for u in range(unroll):
                    tick(r * unroll + u, u)
            for t in range(total, total + lags):
                tick(t, t)

        def on(t, lag, total=PAIRS):
            return not isinstance(t, int) or 0 <= t - lag < total

        def bank_free(pe, job, t):
            names = [n for n, _ in SHARED_JOBS]
            i, back = names.index(job), 0
            while True:
                i -= N_SHARED
                if i < 0:
                    i += len(names)
                    back += 1
                if isinstance(t, int) and t - back < 0:
                    return
                name, lag = SHARED_JOBS[i]
                if on(t - back, lag):
                    pe.wait_ge(drained[name], t - back - lag + 1)
                    return

        def half_count(n, i, inc=16):
            return n * (inc // 2) + (inc - i % 2 * (inc // 2))

        def lap(n, k, inc=16, ring=2 * RING):
            return n * (inc // ring) + (inc - k % ring * (inc // ring))

        def nth(n, q):
            return n * QUARTERS + (q + 1)

        def column(n):
            return bass.ds(n, 1)

        W_LOADS = (5, 5, 8)
        FILLS = C
        F_STEPS = T // (P * FT)
        RESID_STORES = 2

        block = es.enter_context(nc.Block())

        @block.sync
        def _(sp):
            sp.dma_start(x_in[0][:], x_pairs[0]).then_inc(x_loaded[0], 16)

            def load(group, dst, src):
                sp.dma_start(dst, src).then_inc(loaded_w[group], 16)

            def rows(w):
                return w.rearrange("(k p) n -> p k n", p=P)

            def columns(bias):
                return bias.rearrange("(m p) -> p m", p=P)

            def repeated(bias):
                return bias.rearrange("(o n) -> o n", o=1).to_broadcast([P, D])
            with nc.allow_non_contiguous_dma(reason="bias vectors, once"):
                load(0, w_v[:], rows(W_qkv[:, 2 * D:3 * D]))
                load(0, b_v[:], columns(b_qkv[2 * D:3 * D]))
                load(0, b_vx[:], columns(bv))
                load(0, w_out[:], rows(W_out))
                load(0, w_o[:], rows(Wo))
                load(1, w_qk[:], rows(W_qkv[:, 0:2 * D]))
                load(1, b_qk[:], columns(b_qkv[0:2 * D]))
                load(1, b_q[:], columns(bq))
                load(1, bout_rows[:, 0, :], repeated(b_out))
                load(1, bout_rows[:, 1, :], repeated(bo))
                load(2, w_k[:], Wk[:, :])
                load(2, w_vx[:], Wv[:, :])
                load(2, b_k[:], columns(bk))
                load(2, w_q[:], rows(Wq))
                load(2, w_gate[:, :, 0:E], rows(gate_w))
                load(2, w_gate[:, :, E:E + 1], rows(shared_gate_w))
                load(2, w_gu[:], rows(shared_gate_up_w))
                load(2, w_dn[:], rows(shared_down_w))
            sp.wait_ge(consts, 1)
            sp.dma_start(resid_table[T:T + CAPACITY, :], spare_rows[:, 0:D]).then_inc(tables_set, 16)
            sp.dma_start(resid_table2[T:T + CAPACITY, :], spare_rows[:, 0:D]).then_inc(tables_set, 16)

            def load_weights(n, i):
                sp.dma_start(we_gu[i], expert_gate_up_w[n].rearrange("(k p) f -> p k f", p=P)).then_inc(we_loaded[i], 16)
                sp.dma_start(we_dn[i], expert_down_w[n]).then_inc(we_loaded[i], 16)

            def tick(t, i):
                if isinstance(t, int) and t == PEEL - 1:
                    sp.wait_ge(pre, 4)
                    for n in range(FIRST):
                        sp.dma_start(we_gu_first[n], expert_gate_up_w[n].rearrange("(k p) f -> p k f", p=P)).then_inc(we_first_loaded, 16)
                        sp.dma_start(we_dn_first[n], expert_down_w[n]).then_inc(we_first_loaded, 16)
                if isinstance(t, int) and t == PAIRS:
                    for n in range(4 * RING, 4 * RING + FIRST):
                        load_weights(n, n - 4 * RING)
                if isinstance(t, int) and t == PAIRS + Q:
                    sp.wait_ge(done["k"], PAIRS)
                    sp.wait_ge(done["s"], PAIRS)
                    sp.wait_ge(o_done[1], PAIRS)
                    for n in range(2 * RING, 4 * RING):
                        load_weights(n, n)
                if on(t + 1, A):
                    wait(sp, done["xT"], t)
                    wait(sp, xb_done, t)
                    sp.dma_start(x_in[(i + 1) % 2][:], x_pairs[t + 1]).then_inc(x_loaded[(i + 1) % 2], 16)
                if isinstance(t, int) and t < FILLS:
                    part = slice(t * (E // FILLS), (t + 1) * (E // FILLS))
                    sp.dma_start(slots_by_place[:, part, :],
                                 spare_rows[:].unsqueeze(1).to_broadcast([P, E // FILLS, ROW])).then_inc(tables_set, 16)
                if on(t, A):
                    wait(sp, done["ctxT"], t - 1)
                    sp.dma_start(ctx_sb[i % 2][:], ctx_pairs[t]).then_inc(ctx_loaded[i % 2], 16)
                if on(t, C):
                    c, ci = t - C, (i - C) % 2
                    sp.wait_ge(drained["dn"], c + 1)
                    sp.dma_start(resid_pairs2[c], zero_pair[:]).then_inc(resid_stored[ci], 16)
                    sp.dma_start(resid_pairs[c], z_sb[ci][:]).then_inc(resid_stored[ci], 16)

            for t in range(PEEL):
                tick(t, t)
            with sp.Fori(PEEL // 2, PAIRS // 2 - 1) as r:
                for u in range(2):
                    tick(r * 2 + u, u)
            for t in range(PAIRS - 2, PAIRS + C):
                tick(t, t)

            def load_slots(n, i):
                sp.dma_start(xg[i][:], slots_by_expert[n]).then_inc(slots_loaded[i], 16)

            for i in range(2):
                sp.wait_ge(scattered[i], PAIRS // 2 * 2 * TOP_K * 16)
            for n in range(2 * RING):
                load_slots(n, n)
            for n in range(2 * RING, 4 * RING):
                sp.wait_ge(ey_done, n - (2 * RING - 1))
                load_slots(n, n - 2 * RING)

            def refill(n, u):
                sp.wait_ge(ey_done, n - (2 * RING - 1))
                load_slots(n, u % (2 * RING))
                load_weights(n + 2 * RING, (u + 2 * RING) % (4 * RING))

            with sp.Fori(1, E // (4 * RING) - 1) as r:
                for u in range(4 * RING):
                    refill(r * (4 * RING) + u, u)
            for n in range(E - 4 * RING, E - 2 * RING):
                refill(n, n % (4 * RING))
            for n in range(E - 2 * RING, E):
                sp.wait_ge(ey_done, n - (2 * RING - 1))
                load_slots(n, n % (2 * RING))

            for i in range(2):
                sp.wait_ge(added[i], 16 * E // 2)
            f_tiles = resid_table[0:T, :].rearrange("(n p u) f -> n p u f", u=FT, p=P)
            f_tiles2 = resid_table2[0:T, :].rearrange("(n p u) f -> n p u f", u=FT, p=P)

            def load_resid(n, i):
                sp.dma_start(f_in[i], f_tiles[n]).then_inc(f_loaded[i], 16)
                if not isinstance(n, int) or n >= 4:
                    sp.wait_ge(f_sum, n - 3)
                sp.dma_start(f_in2[i % 4], f_tiles2[n]).then_inc(f_loaded[i], 16)
            for n in range(F_RING):
                load_resid(n, n)
            with sp.Fori(1, F_STEPS // F_RING) as r:
                for u in range(F_RING):
                    sp.wait_ge(f_stored[u], r * 16)
                    load_resid(r * F_RING + u, u)

        @block.tensor
        def _(pe):
            def transpose_pair(bank, tile, cols=KB):
                for kb in range(cols):
                    for u in range(2):
                        m = pe.transpose(bank[:, kb * 256 + u * P:kb * 256 + (u + 1) * P],
                                         tile[:, u, kb * P:(kb + 1) * P], ident[:])
                return m

            def project_T(bank, w, col, rhs, blocks=KB):
                for mb in range(2):
                    for kb in range(blocks):
                        lhsT = w[:, kb, col + mb * P:col + (mb + 1) * P] if blocks > 1 else w[:, mb * P:(mb + 1) * P]
                        m = pe.matmul(bank[:, mb * 256:(mb + 1) * 256], lhsT,
                                      rhs[:, kb, :] if blocks > 1 else rhs[:, :],
                                      start=(kb == 0), stop=(kb == blocks - 1))
                return m

            def project(bank, lhs, w, blocks=KB):
                for u in range(2):
                    for kb in range(blocks):
                        lhsT = lhs[:, kb, u * P:(u + 1) * P] if blocks > 1 else lhs[:, u * P:(u + 1) * P]
                        m = pe.matmul(bank[:, u * 256:(u + 1) * 256], lhsT,
                                      w[:, kb, :] if blocks > 1 else w[:, :],
                                      start=(kb == 0), stop=(kb == blocks - 1))
                return m

            pe.wait_ge(first_consts, 1)
            pe.wait_ge(loaded_w[0], 16 * W_LOADS[0])
            for kb in range(KB):
                for mb in range(2):
                    m = pe.transpose(shared_ps[0][:, mb * 256 + kb * P:mb * 256 + (kb + 1) * P],
                                     w_v[:, kb, mb * P:(mb + 1) * P], ident[:])
            m.then_inc(pre_pe, 1)
            pe.wait_ge(bv_rows_done, 1)
            pe.wait_ge(w_vT_done, 1)
            for mb in range(2):
                for kb in range(KB):
                    m = pe.matmul(shared_ps[1][:, mb * 256:(mb + 1) * 256], w_vT[:, kb, mb * P:(mb + 1) * P],
                                  w_out[:, kb, :], start=(kb == 0), stop=(kb == KB - 1))
            for n, w in ((0, w_out), (1, w_o)):
                for kb in range(KB):
                    m = pe.matmul(shared_ps[2][:, n * 256:(n + 1) * 256], bv_rows[:, n, kb, :], w[:, kb, :],
                                  start=(kb == 0), stop=(kb == KB - 1))
            m.then_inc(pre_pe, 1)
            pe.wait_ge(pre, 4)
            pe.wait_ge(loaded_w[1], 16 * W_LOADS[1])

            def scores(t, i, q):
                b, bi = t - Q, (i - Q) % 2
                u, g = q // 4, q % 4
                if q == 0:
                    pe.wait_ge(drained["qx"], b + 1)
                    pe.wait_ge(drained["kx"], b + 1)
                wait(pe, exp_done, nth(b, q - 2))
                rows = slice(32 * g, 32 * g + 32)
                for mb in range(2):
                    for par in range(2):
                        n = 2 * mb + par
                        m = pe.matmul(score_ps[q % 2][:, n * P:(n + 1) * P],
                                      qx[bi][rows, mb, par, u * P:(u + 1) * P],
                                      kx[bi][rows, mb, u * P:(u + 1) * P], start=True, stop=True)
                m.then_inc(score_done, 1)

            def turn_probs(t, i, q):
                b = t - Q
                pe.wait_ge(norm_done, nth(b, q))
                wait(pe, probT_out, nth(b, q - 2))
                for n in range(4):
                    m = pe.transpose(probT_ps[q % 2][:, n * P:(n + 1) * P], probs[q % 4][:, n, :], ident[:])
                m.then_inc(probT_done, 1)

            def weigh_values(t, i, u):
                b, bi = t - Q, (i - Q) % 2
                if u == 0:
                    pe.wait_ge(drained["vx"], b + 1)
                    wait(pe, o_out[1], b)
                else:
                    pe.wait_ge(o_out[0], b + 1)
                pe.wait_ge(probT_out, nth(b, 4 * u + 3))
                for mb in range(2):
                    for par in range(2):
                        for g in range(4):
                            m = pe.matmul(o_ps[32 * g:32 * g + 32, (2 * u + mb) * P:(2 * u + mb + 1) * P],
                                          vx[bi][:, u, 4 * mb + g, par, :], probsT[4 * u + g][:, 2 * mb + par, :],
                                          start=(par == 0), stop=(par == 1))
                m.then_inc(o_done[u], 1)

            def tick(t, i):
                a, b, c = t - A, t - B, t - C

                def job(name):
                    bank_free(pe, name, t)
                    return bank_of[name]

                def mlp(j):
                    bank = job(f"gu{j}")
                    for half in range(2):
                        for kb in range(KB):
                            m = pe.matmul(bank[:, half * 256:(half + 1) * 256],
                                          w_gu[:, kb, half * FS + j * P:half * FS + (j + 1) * P],
                                          x2T[:, kb, :], start=(kb == 0), stop=(kb == KB - 1))
                    m.then_inc(done[f"gu{j}"], 1)

                def quarter(turn, score):
                    if on(t, Q):
                        if turn is not None:
                            turn_probs(t, i, turn)
                        if score is not None:
                            scores(t, i, score)

                quarter(None, 0)
                if on(t, A):
                    bank = job("xT")
                    pe.wait_ge(x_loaded[i % 2], half_count(t, i))
                    transpose_pair(bank, x_in[i % 2]).then_inc(done["xT"], 1)
                if on(t, B):
                    if isinstance(t, int) and t == B:
                        pe.wait_ge(loaded_w[2], 16 * W_LOADS[2])
                        pe.wait_ge(consts, 1)
                    bank = job("ctxT")
                    pe.wait_ge(ctx_loaded[(i - B) % 2], half_count(b, i - B))
                    for u in range(2):
                        m = pe.transpose(bank[:, u * P:(u + 1) * P], ctx_sb[(i - B) % 2][:, u, :], ident[:])
                    m.then_inc(done["ctxT"], 1)
                quarter(None, 1)
                if on(t, A):
                    bank = job("q")
                    pe.wait_ge(drained["xT"], a + 1)
                    project_T(bank, w_qk, 0, xT).then_inc(done["q"], 1)
                if on(t, B):
                    bank = job("kx")
                    pe.wait_ge(drained["ctxT"], b + 1)
                    project_T(bank, w_k, 0, ctxT, blocks=1).then_inc(done["kx"], 1)
                if on(t, A):
                    bank = job("k")
                    project_T(bank, w_qk, D, xT).then_inc(done["k"], 1)
                quarter(None, 2)
                if on(t, B):
                    bank = job("vx")
                    project(bank, ctxT, w_vx, blocks=1).then_inc(done["vx"], 1)
                quarter(0, 3)
                quarter(1, 4)
                if on(t, B):
                    bank = job("x1T")
                    pe.wait_ge(x1_done, b + 1)
                    transpose_pair(bank, x1).then_inc(done["x1T"], 1)
                if on(t, A):
                    bank = job("s")
                    pe.wait_ge(drained["q"], a + 1)
                    pe.wait_ge(drained["k"], a + 1)
                    for u in range(2):
                        for mb in range(KB):
                            m = pe.matmul(bank[:, u * P:(u + 1) * P], q_sb[:, mb, u * P:(u + 1) * P],
                                          k_sb[:, mb, u * P:(u + 1) * P], start=(mb == 0), stop=(mb == KB - 1))
                    m.then_inc(done["s"], 1)
                quarter(2, 5)
                if on(t, C):
                    bank = job("x2T")
                    pe.wait_ge(x2_done, c + 1)
                    transpose_pair(bank, x2[(i - C) % 2]).then_inc(done["x2T"], 1)
                if on(t, A):
                    bank = job("v")
                    project(bank, xT, w_vo).then_inc(done["v"], 1)
                quarter(3, 6)
                if on(t, C):
                    bank = job("logits")
                    pe.wait_ge(drained["x2T"], c + 1)
                    for u in range(2):
                        for kb in range(KB):
                            m = pe.matmul(bank[:, u * (E + 1):(u + 1) * (E + 1)], x2T[:, kb, u * P:(u + 1) * P],
                                          w_gate[:, kb, :], start=(kb == 0), stop=(kb == KB - 1))
                    m.then_inc(done["logits"], 1)
                    mlp(0)
                if on(t, B):
                    bank = job("qx")
                    pe.wait_ge(drained["x1T"], b + 1)
                    project_T(bank, w_q, 0, x1T).then_inc(done["qx"], 1)
                quarter(4, 7)
                if on(t, Q):
                    weigh_values(t, i, 0)
                if on(t, C):
                    mlp(1)
                quarter(5, None)
                if on(t, A):
                    bank = job("pT")
                    pe.wait_ge(drained["s"], a + 1)
                    for u in range(2):
                        m = pe.transpose(bank[:, u * P:(u + 1) * P], p_sb[:, u, :], ident[:])
                    m.then_inc(done["pT"], 1)
                if on(t, C):
                    mlp(2)
                quarter(6, None)
                if on(t, C):
                    mlp(3)
                quarter(7, None)
                if on(t, C):
                    bank = job("pos")
                    pe.wait_ge(chosen_done, c + 1)
                    pe.matmul(bank[:, 0:E], before[:], chosen_bf[:, 0, :], start=True, stop=True)
                    pe.matmul(bank[:, E:2 * E], before[:], chosen_bf[:, 1, :], start=True, stop=False)
                    pe.matmul(bank[:, E:2 * E], ones_bf[:], chosen_bf[:, 0, :], start=False, stop=True)
                    pe.matmul(bank[:, 2 * E:3 * E], ones_bf[:], chosen_bf[:, 0, :], start=True, stop=False)
                    pe.matmul(bank[:, 2 * E:3 * E], ones_bf[:], chosen_bf[:, 1, :], start=False, stop=True)\
                        .then_inc(done["pos"], 1)
                if on(t, A):
                    bank = job("y")
                    pe.wait_ge(drained["pT"], a + 1)
                    pe.wait_ge(drained["v"], a + 1)
                    for u in range(2):
                        m = pe.matmul(bank[:, u * 256:(u + 1) * 256], pT_sb[:, u, :], v_sb[:, u, :], start=True, stop=True)
                    m.then_inc(done["y"], 1)
                if on(t, Q):
                    weigh_values(t, i, 1)
                if on(t, C):
                    bank = job("dn")
                    pe.wait_ge(drained["gu3"], c + 1)
                    project(bank, h_sb, w_dn, blocks=FB).then_inc(done["dn"], 1)
                if on(t, Q):
                    bank = job("yx")
                    pe.wait_ge(o_out[1], t - Q + 1)
                    project(bank, oT_sb, w_o).then_inc(done["yx"], 1)

            ticks(pe, tick, C, PEEL, 2, PAIRS)

            for name, _ in SHARED_JOBS[-N_SHARED:]:
                pe.wait_ge(drained[name], PAIRS)

            def expert_tick(t, i):
                if on(t, 0, E):
                    wait(pe, xgT_out, t - 1)
                    pe.wait_ge(slots_loaded[i % (2 * RING)], lap(t, i))
                    for kb in range(KB):
                        m = pe.transpose(score_ps[i % 2][:, kb * P:(kb + 1) * P],
                                         xg[i % (2 * RING)][:, kb * P:(kb + 1) * P], ident[:])
                    m.then_inc(xgT_done, 1)
                if on(t, 1, E):
                    n, k = t - 1, (i - 1)
                    pe.wait_ge(xgT_out, n + 1)
                    if isinstance(n, int) and n < FIRST:
                        pe.wait_ge(we_first_loaded, 32 * FIRST)
                        gate_up = we_gu_first[n]
                    else:
                        place, gate_up = k % (4 * RING), we_gu[k % (4 * RING)]
                        pe.wait_ge(we_loaded[place], lap(n, k, 32, 4 * RING) - (32 if place < FIRST else 0))
                    wait(pe, eh_done, n - 1)
                    for half in range(2):
                        for kb in range(KB):
                            m = pe.matmul(probT_ps[k % 2][:, half * P:(half + 1) * P],
                                          gate_up[:, kb, half * P:(half + 1) * P],
                                          xgT[k % 2][:, kb, :], start=(kb == 0), stop=(kb == KB - 1))
                    m.then_inc(egu_done, 1)
                if on(t, 2, E):
                    n, k = t - 2, (i - 2)
                    pe.wait_ge(eh_done, n + 1)
                    wait(pe, ey_done, n - 1)
                    down = we_dn_first[n] if isinstance(n, int) and n < FIRST else we_dn[k % (4 * RING)]
                    pe.matmul(shared_ps[1 + k % 2][:, 0:D], eh[k % 2][:], down,
                              start=True, stop=True).then_inc(edn_done, 1)

            ticks(pe, expert_tick, 2, 4 * RING, 4 * RING, E)

        @block.scalar
        def _(act):
            COPY, IDENT = ACT.Copy, ACT.Identity
            act.wait_ge(pre_pe, 1)
            act.activation(w_vT[:].rearrange("p k n -> p (k n)"), shared_ps[0][:, :], COPY).then_inc(w_vT_done, 1)

            def drain(name, dst, n, cols=512):
                act.wait_ge(done[name], n)
                act.activation(dst, bank_of[name][:, 0:cols], COPY).then_inc(drained[name], 1)

            def tick(t, i):
                a, b, q2, c = t - A, t - B, t - Q, t - C
                flat = "p k n -> p (k n)"

                def exp_quarter(q):
                    act.wait_ge(max_done, nth(q2, q))
                    wait(act, probT_done, nth(q2, q - 4))
                    for n in range(4):
                        m = act.activation(probs[q % 4][:, n, :], score_ps[q % 2][:, n * P:(n + 1) * P], ACT.Exp,
                                           bias=h_nmax[q % 4][:, n:n + 1], accum_out=h_sum[q % 4][:, n:n + 1])
                    m.then_inc(exp_done, 1)

                def drain_quarter(q):
                    act.wait_ge(probT_done, nth(q2, q))
                    wait(act, o_done[q // 4], q2)
                    act.activation(probsT[q].rearrange("p n q -> p (n q)"), probT_ps[q % 2][:, :], COPY)\
                        .then_inc(probT_out, 1)

                def drain_heads(u):
                    act.wait_ge(o_done[u], q2 + 1)
                    wait(act, done["yx"], q2)
                    act.activation(oT_sb[:, :, u * P:(u + 1) * P],
                                   o_ps[:, 2 * u * P:2 * (u + 1) * P].rearrange("p (k n) -> p k n", k=KB), COPY)\
                        .then_inc(o_out[u], 1)

                def tanh_gate(j):
                    act.wait_ge(done[f"gu{j}"], c + 1)
                    if j >= 2:
                        act.wait_ge(drained[f"gu{j - 2}"], c + 1)
                    else:
                        wait(act, drained[f"gu{j + 2}"], c)
                    act.activation(th[j % 2][:], bank_of[f"gu{j}"][:, 0:256], ACT.Tanh, scale=0.5).then_inc(th_done[j], 1)

                def quarter(exp, turned):
                    if on(t, Q):
                        if exp is not None:
                            exp_quarter(exp)
                        if turned is not None:
                            drain_quarter(turned)

                if on(t, A):
                    drain("xT", xT[:].rearrange(flat), a + 1)
                if on(t, B):
                    drain("ctxT", ctxT[:], b + 1, 256)
                quarter(0, None)
                if on(t, A):
                    act.wait_ge(done["q"], a + 1)
                    for mb in range(2):
                        m = act.activation(q_sb[:, mb, :], bank_of["q"][:, mb * 256:(mb + 1) * 256], IDENT,
                                           bias=b_q1[:, mb:mb + 1], scale=SCALE)
                    m.then_inc(drained["q"], 1)
                if on(t, B):
                    act.wait_ge(done["kx"], b + 1)
                    for mb in range(2):
                        m = act.activation(kx[(i - B) % 2][:, mb, :], bank_of["kx"][:, mb * 256:(mb + 1) * 256],
                                           IDENT, bias=b_k[:, mb:mb + 1])
                    m.then_inc(drained["kx"], 1)
                quarter(1, None)
                if on(t, A):
                    act.wait_ge(done["k"], a + 1)
                    for mb in range(2):
                        m = act.activation(k_sb[:, mb, :], bank_of["k"][:, mb * 256:(mb + 1) * 256], IDENT,
                                           bias=b_qk[:, KB + mb:KB + mb + 1])
                    m.then_inc(drained["k"], 1)
                quarter(2, 0)
                if on(t, B):
                    act.wait_ge(done["vx"], b + 1)
                    v = bank_of["vx"][:, :].rearrange("p (u g r d) -> p u g r d", u=2, r=2, d=DH)
                    for par in range(2):
                        for u in range(2):
                            m = act.activation(vx[(i - B) % 2][:, u, :, par, par * DH:(par + 1) * DH], v[:, u, :, par, :], COPY)
                    m.then_inc(drained["vx"], 1)
                quarter(3, 1)
                if on(t, B):
                    drain("x1T", x1T[:].rearrange(flat), b + 1)
                if on(t, A):
                    act.wait_ge(s_max_done, a + 1)
                    for u in range(2):
                        m = act.activation(p_sb[:, u, :], bank_of["s"][:, u * P:(u + 1) * P], ACT.Exp,
                                           bias=s_nmax[:, u:u + 1], accum_out=s_sum[:, u:u + 1])
                    m.then_inc(drained["s"], 1)
                quarter(4, 2)
                if on(t, C):
                    drain("x2T", x2T[:].rearrange(flat), c + 1)
                if on(t, A):
                    drain("v", v_sb[:].rearrange(flat), a + 1)
                quarter(5, 3)
                if on(t, C):
                    act.wait_ge(drained["logits"], c + 1)
                    act.activation(ex[:], lg[:], ACT.Exp).then_inc(ex_done, 1)
                    tanh_gate(0)
                if on(t, B):
                    act.wait_ge(done["qx"], b + 1)
                    for par in range(2):
                        for mb in range(2):
                            m = act.activation(qx[(i - B) % 2][:, mb, par, :], bank_of["qx"][:, mb * 256:(mb + 1) * 256],
                                               IDENT, bias=b_qm[:, par, mb:mb + 1], scale=par_mask[:, par:par + 1])
                    m.then_inc(drained["qx"], 1)
                quarter(6, 4)
                if on(t, Q):
                    drain_heads(0)
                if on(t, C):
                    tanh_gate(1)
                quarter(7, 5)
                if on(t, A):
                    drain("pT", pT_sb[:].rearrange(flat), a + 1, 256)
                if on(t, C):
                    tanh_gate(2)
                quarter(None, 6)
                if on(t, C):
                    tanh_gate(3)
                quarter(None, 7)
                if on(t, Q):
                    drain_heads(1)

            ticks(act, tick, C, PEEL, 2, PAIRS)

            def expert_tick(t, i):
                if on(t, 0, E):
                    act.wait_ge(xgT_done, t + 1)
                    wait(act, egu_done, t - 1)
                    act.activation(xgT[i % 2][:].rearrange("p k n -> p (k n)"), score_ps[i % 2][:, 0:256], COPY)\
                        .then_inc(xgT_out, 1)
                if on(t, 1, E):
                    n, k = t - 1, i - 1
                    act.wait_ge(egu_done, n + 1)
                    wait(act, eh_done, n - 1)
                    act.activation(eth[k % 2][:], probT_ps[k % 2][:, 0:P], ACT.Tanh, scale=0.5).then_inc(eth_done, 1)

            ticks(act, expert_tick, 2, 2 * RING, 2 * RING, E)

            out_tiles = out.rearrange("s r f -> (s r) f").rearrange("(n p u) f -> n p u f", u=FT, p=P)

            def finish(n, i):
                act.wait_ge(f_nb_done, n + 1)
                for u in range(FT):
                    m = act.activation(f_in[i][:, u, :], f_in[i][:, u, :], ACT.Identity, bias=f_nb[i % 2][:, u:u + 1],
                                       scale=f_rstd[i % 2][:, u:u + 1])
                m.then_inc(f_norm, 1)
                act.wait_ge(f_norm, n + 1)
                act.dma_start(out_tiles[n], f_in[i]).then_inc(f_stored[i], 16)
            with act.Fori(0, F_STEPS // F_RING) as r:
                for u in range(F_RING):
                    finish(r * F_RING + u, u)
            for i in range(F_RING):
                act.wait_ge(f_stored[i], 16 * (F_STEPS // F_RING))

        @block.vector
        def _(dve):
            dve.wait_ge(loaded_w[0], 16 * W_LOADS[0])
            dve.wait_ge(first_consts, 1)
            for n, b in ((0, b_v), (1, b_vx)):
                for kb in range(KB):
                    m = dve.tensor_scalar(bv_rows[:, n, kb, :], bv_rows[:, n, kb, :], b[:, kb:kb + 1], None, ALU.add)
            m.then_inc(bv_rows_done, 1)
            dve.wait_ge(loaded_w[1], 16 * W_LOADS[1])
            dve.wait_ge(first_consts, 2)
            for par in range(2):
                dve.tensor_scalar(b_qm[:, par, :], b_q[:], par_mask[:, par:par + 1], None, ALU.mult)
            dve.tensor_scalar(b_q1[:], b_qk[:, 0:KB], SCALE, None, ALU.mult).then_inc(pre, 1)
            dve.wait_ge(pre_pe, 2)
            dve.tensor_copy(w_vo[:].rearrange("p k n -> p (k n)"), shared_ps[1][:, :]).then_inc(pre, 1)
            dve.tensor_tensor(bias_a[:], shared_ps[2][:, 0:D], bout_rows[:, 0, :], ALU.add).then_inc(pre, 1)
            dve.tensor_tensor(bias_x[:], shared_ps[2][:, D:2 * D], bout_rows[:, 1, :], ALU.add).then_inc(pre, 1)

            def tick(t, i):
                a, b, q2, c = t - A, t - B, t - Q, t - C

                def head_max(q):
                    dve.wait_ge(score_done, nth(q2, q))
                    wait(dve, exp_done, nth(q2, q - 4))
                    dve.tensor_reduce(h_nmax[q % 4][:], score_ps[q % 2][:, :].rearrange("p (n k) -> p n k", k=P), AX.X,
                                      ALU.max, negate=True).then_inc(max_done, 1)

                def head_recip(q):
                    dve.wait_ge(exp_done, nth(q2, q))
                    wait(dve, norm_done, nth(q2, q - 4))
                    dve.reciprocal(h_rsum[q % 4][:], h_sum[q % 4][:]).then_inc(recip_done, 1)

                def gated(j):
                    bank = bank_of[f"gu{j}"]
                    dve.wait_ge(th_done[j], c + 1)
                    dve.scalar_tensor_tensor(silu[j % 2][:], th[j % 2][:], 1.0, bank[:, 0:256], ALU.add, ALU.mult)\
                        .then_inc(silu_step, 1)
                    dve.wait_ge(silu_step, c * FB + (j + 1))
                    if j == 0:
                        wait(dve, done["dn"], c)
                    dve.scalar_tensor_tensor(h_sb[:, j, :], silu[j % 2][:], 0.5, bank[:, 256:512], ALU.mult, ALU.mult)\
                        .then_inc(drained[f"gu{j}"], 1)

                def statistics(r, st, mv, st_done, mv_done, n):
                    for u in range(2):
                        m = dve.bn_stats(st[:, u, :], r[:, u, :])
                    m.then_inc(st_done, 1)
                    dve.wait_ge(st_done, n + 1)
                    carry_wait(dve)
                    for u in range(2):
                        m = dve.bn_aggr(mv[:, u, :], st[:, u, :])
                    m.then_inc(mv_done, 1)

                def normalise(r, mv, rstd, dst, rstd_done, dst_done, n):
                    dve.wait_ge(rstd_done, n + 1)
                    for u in range(2):
                        m = dve.tensor_scalar(dst[:, u, 0:D], r[:, u, :], mv[:, u, 0:1], rstd[:, u:u + 1],
                                              ALU.subtract, ALU.mult)
                    m.then_inc(dst_done, 1)

                GATE = 10

                def router():
                    n = c * GATE
                    bank = bank_of["logits"][:, 0:2 * (E + 1)].rearrange("p (u e) -> p u e", u=2)

                    def per_seq(col):
                        return col[:].unsqueeze(2).to_broadcast([P, 2, E])
                    dve.wait_ge(done["logits"], c + 1)
                    dve.tensor_reduce(lg_max[:], bank[:, :, 0:E], AX.X, ALU.max).then_inc(gate_step, 1)
                    dve.wait_ge(gate_step, n + 1)
                    dve.tensor_scalar(lg[:, :, E:E + 1], bank[:, :, E:E + 1], -1.0, None, ALU.mult)
                    dve.tensor_tensor(lg[:, :, 0:E], bank[:, :, 0:E], per_seq(lg_max), ALU.subtract).then_inc(drained["logits"], 1)

                def router_top():
                    n = c * GATE + 1

                    def per_seq(col):
                        return col[:].unsqueeze(2).to_broadcast([P, 2, E])
                    dve.wait_ge(ex_done, c + 1)
                    dve.tensor_reduce(z_sum[:], ex[:, :, 0:E], AX.X, ALU.add).then_inc(gate_step, 1)
                    dve.tensor_scalar(sg1[:], ex[:, :, E], 1.0, None, ALU.add).then_inc(gate_step, 1)
                    dve.wait_ge(gate_step, n + 2)
                    dve.reciprocal(z_rsum[:], z_sum[:]).then_inc(gate_step, 1)
                    dve.wait_ge(gate_step, n + 3)
                    dve.tensor_tensor(prob[:], ex[:, :, 0:E], per_seq(z_rsum), ALU.mult).then_inc(gate_step, 1)
                    dve.wait_ge(gate_step, n + 4)
                    dve.reciprocal(sg[:], sg1[:]).then_inc(sg_done, 1)
                    for u in range(2):
                        m = dve.max(top[:, u, :], prob[:, u, :])
                    m.then_inc(gate_step, 1)
                    dve.wait_ge(gate_step, n + 5)
                    dve.tensor_reduce(top_sum[:], top[:], AX.X, ALU.add).then_inc(gate_step, 1)
                    for u in range(2):
                        m = dve.match_replace(out=marked[:, u, :], in_to_replace=top[:, u, :], in_values=prob[:, u, :], imm_value=-1.0)
                    m.then_inc(gate_step, 1)

                def router_weights():
                    n = c * GATE + 1
                    dve.wait_ge(gate_step, n + 7)
                    wait(dve, scattered[(i - C) % 2], half_count(c, i - C, 2 * TOP_K * 16) - 2 * TOP_K * 16)
                    row = send[(i - C) % 2]
                    dve.tensor_copy(row[:, :, 0:D], x2[(i - C) % 2][:])
                    dve.tensor_scalar(row[:, :, ROW - 1:ROW], row[:, :, ROW - 1:ROW], float(4 * P), None, ALU.add)
                    dve.tensor_scalar(chosen[:], marked[:], 0.0, None, ALU.is_lt).then_inc(gate_step, 1)
                    wait(dve, done["pos"], c)
                    dve.tensor_scalar(chosen_bf[:], marked[:], 0.0, None, ALU.is_lt).then_inc(chosen_done, 1)
                    dve.wait_ge(gate_step, n + 8)
                    dve.reciprocal(top_rsum[:], top_sum[:]).then_inc(gate_step, 1)
                    dve.wait_ge(gate_step, n + 9)
                    for u in range(2):
                        m = dve.scalar_tensor_tensor(row[:, u, D:D + E], prob[:, u, :], top_rsum[:, u:u + 1],
                                                     chosen[:, u, :], ALU.mult, ALU.mult)

                PLACE = 5

                def places():
                    n = c * PLACE
                    bank = bank_of["pos"]
                    cnt = count[:].unsqueeze(1).to_broadcast([P, 2, E])
                    dve.wait_ge(done["pos"], c + 1)
                    wait(dve, drained["pos"], c)
                    dve.tensor_tensor(place[:], bank[:, 0:2 * E].rearrange("p (u e) -> p u e", u=2), cnt, ALU.add)\
                        .then_inc(place_step, 1)
                    dve.wait_ge(place_step, n + 1)
                    dve.scalar_tensor_tensor(kept[:], place[:], float(CAPACITY), chosen[:], ALU.is_lt, ALU.mult)\
                        .then_inc(place_step, 1)
                    dve.tensor_tensor(slot_key[:], slot_base[:].unsqueeze(1).to_broadcast([P, 2, E]), place[:],
                                      ALU.subtract).then_inc(place_step, 1)
                    dve.wait_ge(place_step, n + 3)
                    dve.tensor_tensor(key[:], slot_key[:], kept[:], ALU.mult).then_inc(place_step, 1)
                    dve.wait_ge(place_step, n + 4)
                    dve.tensor_tensor(count[:], bank[:, 2 * E:3 * E], count[:], ALU.add).then_inc(drained["pos"], 1)
                    for u in range(2):
                        m = dve.max(key8[:, u, :], key[:, u, :])
                    m.then_inc(place_step, 1)
                    dve.wait_ge(place_step, n + 5)
                    dve.tensor_scalar(slot_no[(i - C) % 2][:], key8[:], -1.0, float(T), ALU.mult, ALU.add).then_inc(slot_done, 1)

                def quarter(recip, top):
                    if on(t, Q):
                        if recip is not None:
                            head_recip(recip)
                        if top is not None:
                            head_max(top)

                quarter(None, 0)
                if on(t, B):
                    wait(dve, done["x1T"], b)
                    wait(dve, x1b_done, b)
                    normalise(r1, mv1, rstd1, x1, rstd1_done, x1_done, b)
                quarter(None, 1)
                if on(t, C):
                    wait(dve, done["x2T"], c - 1)
                    normalise(r2, mv2, rstd2, x2[(i - C) % 2], rstd2_done, x2_done, c)
                quarter(0, 2)
                quarter(1, 3)
                quarter(2, 4)
                if on(t, A):
                    dve.wait_ge(done["s"], a + 1)
                    dve.tensor_reduce(s_nmax[:], bank_of["s"][:, 0:256].rearrange("p (u k) -> p u k", u=2), AX.X,
                                      ALU.max, negate=True).then_inc(s_max_done, 1)
                quarter(3, 5)
                quarter(4, 6)
                if on(t, C):
                    router()
                    gated(0)
                quarter(5, 7)
                if on(t, C):
                    router_top()
                quarter(6, None)
                if on(t, C):
                    router_weights()
                    gated(1)
                quarter(7, None)
                if on(t, C):
                    gated(2)
                    gated(3)
                    places()
                if on(t, A):
                    dve.wait_ge(drained["s"], a + 1)
                    dve.reciprocal(s_rsum[:], s_sum[:]).then_inc(s_rsum_done, 1)
                    dve.wait_ge(done["y"], a + 1)
                    dve.wait_ge(s_rsum_done, a + 1)
                    dve.wait_ge(xb_done, a + 1)
                    for u in range(2):
                        m = dve.scalar_tensor_tensor(r1[:, u, :], bank_of["y"][:, u * D:(u + 1) * D], s_rsum[:, u:u + 1],
                                                     xb[:, u, :], ALU.mult, ALU.add)
                    m.then_inc(drained["y"], 1)
                    dve.wait_ge(drained["y"], a + 1)
                    statistics(r1, st1, mv1, st1_done, mv1_done, a)
                if on(t, C):
                    dve.wait_ge(done["dn"], c + 1)
                    wait(dve, resid_stored[(i - C) % 2], half_count(c, i - C, RESID_STORES * 16) - RESID_STORES * 16)
                    dve.wait_ge(sg_done, c + 1)
                    for u in range(2):
                        m = dve.scalar_tensor_tensor(z_sb[(i - C) % 2][:, u, :], bank_of["dn"][:, u * D:(u + 1) * D],
                                                     sg[:, u:u + 1], x2[(i - C) % 2][:, u, 0:D], ALU.mult, ALU.add)
                    m.then_inc(drained["dn"], 1)
                if on(t, Q):
                    dve.wait_ge(done["yx"], q2 + 1)
                    dve.tensor_tensor(r2[:].rearrange("p u d -> p (u d)"), bank_of["yx"][:, :],
                                      x1b[(i - Q) % 2][:].rearrange("p u d -> p (u d)"), ALU.add).then_inc(drained["yx"], 1)
                    dve.wait_ge(drained["yx"], q2 + 1)
                    statistics(r2, st2, mv2, st2_done, mv2_done, q2)

            ticks(dve, tick, C, PEEL, 2, PAIRS)

            def expert_tick(t, i):
                if on(t, 1, E):
                    n, k = t - 1, i - 1
                    bank = probT_ps[k % 2]
                    dve.wait_ge(eth_done, n + 1)
                    dve.scalar_tensor_tensor(esilu[k % 2][:], eth[k % 2][:], 1.0, bank[:, 0:P], ALU.add, ALU.mult).then_inc(estep, 1)
                    dve.wait_ge(estep, n + 1)
                    wait(dve, edn_done, n - 1)
                    dve.scalar_tensor_tensor(eh[k % 2][:], esilu[k % 2][:], 0.5, bank[:, P:2 * P], ALU.mult, ALU.mult)\
                        .then_inc(eh_done, 1)
                if on(t, 2, E):
                    n, k = t - 2, (i - 2) % (2 * RING)
                    wait(dve, added[k % 2], half_count(n, k) - RING * 16)
                    dve.wait_ge(edn_done, n + 1)
                    dve.tensor_copy(ids[k][:], xg[k][:, ROW - 1:ROW])
                    dve.tensor_scalar(ey[k], shared_ps[1 + k % 2][:, 0:D], xg[k][:, column(n + D)], None,
                                      ALU.mult).then_inc(ey_done, 1)

            ticks(dve, expert_tick, 2, 2 * RING, 2 * RING, E)

            def final(t, i):
                if on(t, 0, F_STEPS):
                    dve.wait_ge(f_sum, t + 1)
                    for u in range(FT):
                        m = dve.bn_stats(f_st[i % 2][:, u, :], f_in[i % F_RING][:, u, :])
                    m.then_inc(f_st_done, 1)
                    dve.wait_ge(f_st_done, t + 1)
                    carry_wait(dve)
                    for u in range(FT):
                        m = dve.bn_aggr(f_mv[i % 2][:, u, :], f_st[i % 2][:, u, :])
                    m.then_inc(f_mv_done, 1)
                    k = i % 2
                    dve.wait_ge(f_rstd_done, t + 1)
                    wait(dve, f_norm, t - 1)
                    dve.scalar_tensor_tensor(f_nb[k][:], f_mv[k][:, :, 0], -1.0, f_rstd[k][:], ALU.mult, ALU.mult)\
                        .then_inc(f_nb_done, 1)
            ticks(dve, final, 0, F_RING, F_RING, F_STEPS)

        @block.gpsimd
        def _(pool):
            steps = 0

            def step(instruction):
                nonlocal steps
                steps += 1
                instruction.then_inc(pool_step, 1)
                pool.wait_ge(pool_step, steps)

            step(pool.memset(ident[:], 0.0))
            step(pool.affine_select(out=ident[:], in_=ident[:], compare_op=ALU.not_equal, fill=1.0, base=0,
                                    pattern=[[-1, P]], channel_multiplier=1))
            pool.memset(bv_rows[:], 0.0).then_inc(first_consts, 1)
            step(pool.memset(before[:], 1.0))
            step(pool.affine_select(out=before[:], in_=before[:], compare_op=ALU.is_gt, fill=0.0, base=0,
                                    pattern=[[1, P]], channel_multiplier=-1))
            step(pool.iota(row_no[:], pattern=[[0, 1]], base=0, channel_multiplier=1))
            step(pool.tensor_copy(row_f[:], row_no[:]))
            step(pool.memset(par_mask[:], 0.0))
            for g in range(1, P // DH):
                step(pool.tensor_scalar(row_ge[:], row_f[:], float(DH * g), 1.0 if g % 2 else -1.0, ALU.is_ge, ALU.mult))
                step(pool.tensor_tensor(par_mask[:, 1:2], par_mask[:, 1:2], row_ge[:], ALU.add))
            step(pool.tensor_scalar(par_mask[:, 0:1], par_mask[:, 1:2], -SCALE, SCALE, ALU.mult, ALU.add))
            step(pool.tensor_scalar(par_mask[:, 1:2], par_mask[:, 1:2], SCALE, None, ALU.mult))
            pool.memset(neg_half[:], -0.5).then_inc(first_consts, 1)
            step(pool.memset(spare_rows[:], 0.0))
            step(pool.tensor_scalar(spare_rows[:, ROW - 1:ROW], row_f[:], float(T), None, ALU.add))
            for i in range(2):
                for u in range(2):
                    step(pool.tensor_scalar(send[i][:, u, ROW - 1:ROW], row_f[:], float((2 * i + u) * P - 4 * P), None, ALU.add))
            step(pool.memset(zero_pair[:], 0.0))
            step(pool.memset(ones_bf[:], 1.0))
            step(pool.memset(f_nh[:], -0.5))
            step(pool.memset(eps_col[:], EPS))
            step(pool.memset(count[:], 0.0))
            for v in vx:
                step(pool.memset(v[:], 0.0))
            step(pool.iota(base_i[:], pattern=[[-CAPACITY, E]], base=T, channel_multiplier=0))
            pool.tensor_copy(slot_base[:], base_i[:]).then_inc(consts, 1)
            slot_bound = pool.to_reg(E * CAPACITY - 1)
            row_bound = pool.to_reg(T + CAPACITY - 1)
            pool.wait_ge(pre, 4)

            def tick(t, i):
                a, b, q2, c = t - A, t - B, t - Q, t - C
                if on(t, A):
                    pool.wait_ge(x_loaded[i % 2], half_count(t, i))
                    wait(pool, drained["y"], a)
                    pool.tensor_tensor(xb[:], x_in[i % 2][:], bias_a[:].unsqueeze(1).to_broadcast([P, 2, D]), ALU.add)\
                        .then_inc(xb_done, 1)
                if on(t, B):
                    pool.wait_ge(x1_done, b + 1)
                    wait(pool, drained["yx"], b - 1)
                    pool.tensor_tensor(x1b[(i - B) % 2][:], x1[:], bias_x[:].unsqueeze(1).to_broadcast([P, 2, D]), ALU.add)\
                        .then_inc(x1b_done, 1)

                def scatter(ci, k):
                    for u in range(2):
                        pool.indirect_dma_start(slot_table[:, :], bass.IndirectOffsetOnAxis(ap=slot_no[ci % 2][:, u, k:k + 1], axis=0),
                                                send[ci % 2][:, u, :], None, bounds_check=slot_bound,
                                                oob_is_err=False).then_inc(scattered[ci % 2], 16)

                def normalise_quarter(q):
                    pool.wait_ge(recip_done, nth(q2, q))
                    pool.tensor_tensor(probs[q % 4][:], probs[q % 4][:],
                                       h_rsum[q % 4][:].unsqueeze(2).to_broadcast([P, 4, P]), ALU.mult).then_inc(norm_done, 1)

                if on(t, C + 1):
                    if isinstance(t, int) and t == C + 1:
                        pool.wait_ge(tables_set, 16 * (2 + FILLS))
                    pool.wait_ge(slot_done, c)
                    carry_wait(pool)
                for k in range(TOP_K):
                    if on(t, Q):
                        normalise_quarter(k)
                    if on(t, C + 1):
                        scatter(i - C - 1, k)

                def rstd(mv, ve, r, mv_done, ve_done, rstd_done, n):
                    pool.wait_ge(mv_done, n + 1)
                    pool.tensor_tensor(ve[:], mv[:, :, 1], eps_col[:, 0:2], ALU.add).then_inc(ve_done, 1)
                    pool.wait_ge(ve_done, n + 1)
                    pool.tensor_tensor(r[:], ve[:], neg_half[:], ALU.pow).then_inc(rstd_done, 1)
                if on(t, A):
                    rstd(mv1, ve1, rstd1, mv1_done, ve1_done, rstd1_done, a)
                if on(t, Q):
                    rstd(mv2, ve2, rstd2, mv2_done, ve2_done, rstd2_done, q2)

            ticks(pool, tick, C + 1, PEEL, 2, PAIRS)

            for i in range(2):
                pool.wait_ge(resid_stored[i], PAIRS // 2 * RESID_STORES * 16)

            def expert_tick(t, i):
                if on(t, 2, E):
                    n, k = t - 2, (i - 2) % (2 * RING)
                    pool.wait_ge(ey_done, n + 1)
                    wait(pool, added[k % 2], half_count(n, k) - 16)
                    carry_wait(pool)
                    pool.indirect_dma_start((resid_table, resid_table2)[k % 2][:, :],
                                            bass.IndirectOffsetOnAxis(ap=ids[k][:], axis=0),
                                            ey[k], None, bounds_check=row_bound,
                                            compute_op=ALU.add).then_inc(added[k % 2], 16)

            ticks(pool, expert_tick, 2, 2 * RING, 2 * RING, E)

            def final(t, i):
                if on(t, 0, F_STEPS):
                    k = i % F_RING
                    pool.wait_ge(f_loaded[k], lap(t, i, 32, F_RING))
                    pool.tensor_tensor(f_in[k], f_in[k], f_in2[k % 4], ALU.add).then_inc(f_sum, 1)
                if on(t, 1, F_STEPS):
                    k = (i - 1) % 2
                    pool.wait_ge(f_mv_done, t)
                    pool.tensor_tensor(f_ve[k][:], f_mv[k][:, :, 1], eps_col[:], ALU.add).then_inc(f_ve_done, 1)
                    pool.wait_ge(f_ve_done, t)
                    wait(pool, f_norm, t - 2)
                    pool.tensor_tensor(f_rstd[k][:], f_ve[k][:], f_nh[:], ALU.pow).then_inc(f_rstd_done, 1)
            ticks(pool, final, 1, F_RING, F_RING, F_STEPS)


_INS = ['x', 'ctx_512', 'L0_attn_W_qkv', 'L0_attn_b_qkv', 'L0_attn_W_out', 'L0_attn_b_out', 'L0_xattn_Wq', 'L0_xattn_bq',
        'L0_xattn_Wk', 'L0_xattn_bk', 'L0_xattn_Wv', 'L0_xattn_bv', 'L0_xattn_Wo', 'L0_xattn_bo', 'L0_ffn_gate_w',
        'L0_ffn_shared_gate_w', 'L0_ffn_shared_gate_up_w', 'L0_ffn_shared_down_w', 'L0_ffn_expert_gate_up_w',
        'L0_ffn_expert_down_w']
_OUTS = [((64, 128, 256), 'float32')]


def kernel(**inputs):
    import numpy as _np
    import concourse.bacc as _bacc
    from concourse import mybir as _mybir
    from concourse.bass_utils import run_bass_kernel_spmd as _run

    nc = _bacc.Bacc("TRN2", target_bir_lowering=False, num_devices=1)
    arrays, args = {}, []
    for name in _INS:
        a = _np.ascontiguousarray(inputs[name])
        arrays[f"in_{name}_dram"] = a
        args.append(nc.dram_tensor(f"in_{name}_dram", a.shape, _mybir.dt.from_np(a.dtype), kind="ExternalInput").ap())
    for i, (shape, dtype) in enumerate(_OUTS):
        dt = _mybir.dt.from_np(_np.dtype(dtype))
        args.append(nc.dram_tensor(f"out_{i}_dram", shape, dt, kind="ExternalOutput").ap())
    decoder_layer(nc, *args)
    r = _run(nc, [arrays], core_ids=[0])
    return r.results[0]["out_0_dram"]
```
